# Optimizing a Trainium2 kernel written in Bass

```python
import numpy as np
import jax
import jax.numpy as jnp

def _softmax(x, axis=-1):
    return jax.nn.softmax(x, axis=axis)

def _gelu(x):
    return jax.nn.gelu(x, approximate=True)

def _silu(x):
    return jax.nn.silu(x)

def _sigmoid(x):
    return jax.nn.sigmoid(x)

def _layernorm(x, axis=-1, eps=1e-05):
    m = jnp.mean(x, axis=axis, keepdims=True)
    v = jnp.var(x, axis=axis, keepdims=True)
    return (x - m) / jnp.sqrt(v + eps)

def _scatter_add(tgt, idx, src, axis=0):
    return tgt.at[idx].add(src)

def _segment_sum(src, seg, n):
    return jax.ops.segment_sum(src, seg, n)
kernel_name = 'mk_cond_seq_d2_seqx_r4_5f8fd4'

def setup_inputs(seed: int=0):
    np.random.seed(seed)
    _w = jnp.asarray

    def _rec_inputs():
        import jax
        import jax.numpy as jnp
        _rk = jax.random.key(seed)
        x = 7.22e-05 + 1 * jax.random.normal(jax.random.fold_in(_rk, 1), (128, 64, 256), jnp.float32)
        _lenS = 64 - jax.random.randint(jax.random.fold_in(_rk, 7), (128,), 0, max(1, 64 // 4) + 1, jnp.int32)
        _lenS2 = 64 - jax.random.randint(jax.random.fold_in(_rk, 8), (128,), 0, max(1, 64 // 4) + 1, jnp.int32)
        cond_1024 = 0.00782532 + 1.00527 * jax.random.normal(jax.random.fold_in(_rk, 11), (128, 256), jnp.float32)
        _validS = jnp.arange(64)[None, :] < _lenS[:, None]
        _validS2 = jnp.arange(64)[None, :] < _lenS2[:, None]
        _causal = jnp.tril(jnp.ones((64, 64), dtype=bool))
        mask_BxS_bk1 = jnp.broadcast_to(_validS[:, :], (128, 64))
        return (x, cond_1024, mask_BxS_bk1)
    x, cond_1024, mask_BxS_bk1 = _rec_inputs()

    def _L0_cond_setup():
        import jax, jax.numpy as jnp
        import numpy as np
        B, N, C = (8, 256, 256)
        H = 16
        HD = C // H
        MLP = 4 * C
        EPS = 1e-06

        def _layernorm(x):
            mu = jnp.mean(x, axis=-1, keepdims=True)
            var = jnp.mean((x - mu) ** 2, axis=-1, keepdims=True)
            return (x - mu) * jax.lax.rsqrt(var + EPS)

        def _modulate(x, shift, scale):
            return x * (1.0 + scale[:, None, :]) + shift[:, None, :]

        def _attention(x, padding_mask, qkv_w, qkv_b, proj_w, proj_b):
            b, n, cdim = x.shape
            qkv = x @ qkv_w.T + qkv_b
            qkv = qkv.reshape(b, n, 3, H, HD).transpose(2, 0, 3, 1, 4)
            q, k, v = (qkv[0], qkv[1], qkv[2])
            scale = HD ** (-0.5)
            attn = jnp.einsum('bhnd,bhmd->bhnm', q, k) * scale
            mask = padding_mask[:, None, :] & padding_mask[:, :, None]
            attn = jnp.where(mask[:, None, :, :], attn, -1000000000.0)
            attn = jax.nn.softmax(attn, axis=-1)
            out = jnp.einsum('bhnm,bhmd->bhnd', attn, v)
            out = out.transpose(0, 2, 1, 3).reshape(b, n, cdim)
            return out @ proj_w.T + proj_b
        key = jax.random.key(seed)
        ks = jax.random.split(key, 12)
        x = jax.random.normal(ks[0], (B, N, C), dtype=jnp.float32)
        c = jax.random.normal(ks[1], (B, C), dtype=jnp.float32)
        lengths = jax.random.randint(ks[2], (B,), N // 2, N + 1)
        padding_mask = jnp.arange(N)[None, :] < lengths[:, None]
        s = 0.02
        qkv_w = jax.random.normal(ks[3], (3 * C, C), dtype=jnp.float32) * s
        qkv_b = jnp.zeros((3 * C,), dtype=jnp.float32)
        proj_w = jax.random.normal(ks[4], (C, C), dtype=jnp.float32) * s
        proj_b = jnp.zeros((C,), dtype=jnp.float32)
        fc1_w = jax.random.normal(ks[5], (MLP, C), dtype=jnp.float32) * s
        fc1_b = jnp.zeros((MLP,), dtype=jnp.float32)
        fc2_w = jax.random.normal(ks[6], (C, MLP), dtype=jnp.float32) * s
        fc2_b = jnp.zeros((C,), dtype=jnp.float32)
        ada_w = jax.random.normal(ks[7], (6 * C, C), dtype=jnp.float32) * s
        ada_b = jnp.zeros((6 * C,), dtype=jnp.float32)
        return {'x': x, 'c': c, 'padding_mask': padding_mask, 'qkv_w': qkv_w, 'qkv_b': qkv_b, 'proj_w': proj_w, 'proj_b': proj_b, 'fc1_w': fc1_w, 'fc1_b': fc1_b, 'fc2_w': fc2_w, 'fc2_b': fc2_b, 'ada_w': ada_w, 'ada_b': ada_b}
    _L0_cond_all = _L0_cond_setup()
    _L0_cond_in = {k: v for k, v in _L0_cond_all.items() if k in ('qkv_w', 'qkv_b', 'proj_w', 'proj_b', 'fc1_w', 'fc1_b', 'fc2_w', 'fc2_b', 'ada_w', 'ada_b')}
    del _L0_cond_all

    def _L1_cond_setup():
        import jax, jax.numpy as jnp
        import numpy as np
        B, N, D = (2, 512, 256)
        H, HD = (16, 64)
        E, DD = (8, 1024)
        EPS = 1e-05

        def _ln(x, g, b):
            m = jnp.mean(x, axis=-1, keepdims=True)
            v = jnp.var(x, axis=-1, keepdims=True)
            return (x - m) * jax.lax.rsqrt(v + EPS) * g + b
        key = jax.random.key(seed)
        ks = jax.random.split(key, 16)
        s = 0.02
        return {'x': jax.random.normal(ks[0], (B, N, D), jnp.float32), 't': jax.random.normal(ks[1], (B, 1, D), jnp.float32), 'W_ada': jax.random.normal(ks[2], (D, D), jnp.float32) * s, 'b_ada': jnp.zeros((D,), jnp.float32), 'ln1_g': jnp.ones((D,), jnp.float32), 'ln1_b': jnp.zeros((D,), jnp.float32), 'Wqkv': jax.random.normal(ks[3], (3 * H * HD, D), jnp.float32) * s, 'qn_g': jnp.ones((HD,), jnp.float32), 'qn_b': jnp.zeros((HD,), jnp.float32), 'kn_g': jnp.ones((HD,), jnp.float32), 'kn_b': jnp.zeros((HD,), jnp.float32), 'Wout': jax.random.normal(ks[4], (D, H * HD), jnp.float32) * s, 'mlp_g': jnp.ones((D,), jnp.float32), 'mlp_b': jnp.zeros((D,), jnp.float32), 'Wgate': jax.random.normal(ks[5], (E, D), jnp.float32) * s, 'fc1s': jax.random.normal(ks[6], (E, DD, D), jnp.float32) * s, 'b1s': jnp.zeros((E, DD), jnp.float32), 'fc2s': jax.random.normal(ks[7], (E, D, DD), jnp.float32) * s, 'b2s': jnp.zeros((E, D), jnp.float32)}
    _L1_cond_all = _L1_cond_setup()
    _L1_cond_in = {k: v for k, v in _L1_cond_all.items() if k in ('W_ada', 'b_ada', 'ln1_g', 'ln1_b', 'Wqkv', 'qn_g', 'qn_b', 'kn_g', 'kn_b', 'Wout', 'mlp_g', 'mlp_b', 'Wgate', 'fc1s', 'b1s', 'fc2s', 'b2s')}
    del _L1_cond_all
    return {'x': x, 'cond_1024': cond_1024, 'mask_BxS_bk1': mask_BxS_bk1, 'L0_cond_qkv_w': _L0_cond_in['qkv_w'], 'L0_cond_qkv_b': _L0_cond_in['qkv_b'], 'L0_cond_proj_w': _L0_cond_in['proj_w'], 'L0_cond_proj_b': _L0_cond_in['proj_b'], 'L0_cond_fc1_w': _L0_cond_in['fc1_w'], 'L0_cond_fc1_b': _L0_cond_in['fc1_b'], 'L0_cond_fc2_w': _L0_cond_in['fc2_w'], 'L0_cond_fc2_b': _L0_cond_in['fc2_b'], 'L0_cond_ada_w': _L0_cond_in['ada_w'], 'L0_cond_ada_b': _L0_cond_in['ada_b'], 'L1_cond_W_ada': _L1_cond_in['W_ada'], 'L1_cond_b_ada': _L1_cond_in['b_ada'], 'L1_cond_ln1_g': _L1_cond_in['ln1_g'], 'L1_cond_ln1_b': _L1_cond_in['ln1_b'], 'L1_cond_Wqkv': _L1_cond_in['Wqkv'], 'L1_cond_qn_g': _L1_cond_in['qn_g'], 'L1_cond_qn_b': _L1_cond_in['qn_b'], 'L1_cond_kn_g': _L1_cond_in['kn_g'], 'L1_cond_kn_b': _L1_cond_in['kn_b'], 'L1_cond_Wout': _L1_cond_in['Wout'], 'L1_cond_mlp_g': _L1_cond_in['mlp_g'], 'L1_cond_mlp_b': _L1_cond_in['mlp_b'], 'L1_cond_Wgate': _L1_cond_in['Wgate'], 'L1_cond_fc1s': _L1_cond_in['fc1s'], 'L1_cond_b1s': _L1_cond_in['b1s'], 'L1_cond_fc2s': _L1_cond_in['fc2s'], 'L1_cond_b2s': _L1_cond_in['b2s']}

def reference(x, cond_1024, mask_BxS_bk1, L0_cond_qkv_w, L0_cond_qkv_b, L0_cond_proj_w, L0_cond_proj_b, L0_cond_fc1_w, L0_cond_fc1_b, L0_cond_fc2_w, L0_cond_fc2_b, L0_cond_ada_w, L0_cond_ada_b, L1_cond_W_ada, L1_cond_b_ada, L1_cond_ln1_g, L1_cond_ln1_b, L1_cond_Wqkv, L1_cond_qn_g, L1_cond_qn_b, L1_cond_kn_g, L1_cond_kn_b, L1_cond_Wout, L1_cond_mlp_g, L1_cond_mlp_b, L1_cond_Wgate, L1_cond_fc1s, L1_cond_b1s, L1_cond_fc2s, L1_cond_b2s):
    import jax
    import jax.numpy as jnp

    def _L0_cond_ref(x, c, padding_mask, qkv_w, qkv_b, proj_w, proj_b, fc1_w, fc1_b, fc2_w, fc2_b, ada_w, ada_b):
        import jax, jax.numpy as jnp
        import numpy as np
        B, N, C = (8, 256, 256)
        H = 16
        HD = C // H
        MLP = 4 * C
        EPS = 1e-06

        def _layernorm(x):
            mu = jnp.mean(x, axis=-1, keepdims=True)
            var = jnp.mean((x - mu) ** 2, axis=-1, keepdims=True)
            return (x - mu) * jax.lax.rsqrt(var + EPS)

        def _modulate(x, shift, scale):
            return x * (1.0 + scale[:, None, :]) + shift[:, None, :]

        def _attention(x, padding_mask, qkv_w, qkv_b, proj_w, proj_b):
            b, n, cdim = x.shape
            qkv = x @ qkv_w.T + qkv_b
            qkv = qkv.reshape(b, n, 3, H, HD).transpose(2, 0, 3, 1, 4)
            q, k, v = (qkv[0], qkv[1], qkv[2])
            scale = HD ** (-0.5)
            attn = jnp.einsum('bhnd,bhmd->bhnm', q, k) * scale
            mask = padding_mask[:, None, :] & padding_mask[:, :, None]
            attn = jnp.where(mask[:, None, :, :], attn, -1000000000.0)
            attn = jax.nn.softmax(attn, axis=-1)
            out = jnp.einsum('bhnm,bhmd->bhnd', attn, v)
            out = out.transpose(0, 2, 1, 3).reshape(b, n, cdim)
            return out @ proj_w.T + proj_b
        mod = jax.nn.silu(c) @ ada_w.T + ada_b
        shift_msa, scale_msa, gate_msa, shift_mlp, scale_mlp, gate_mlp = jnp.split(mod, 6, axis=1)
        h = _modulate(_layernorm(x), shift_msa, scale_msa)
        x = x + gate_msa[:, None, :] * _attention(h, padding_mask, qkv_w, qkv_b, proj_w, proj_b)
        h = _modulate(_layernorm(x), shift_mlp, scale_mlp)
        h = jax.nn.gelu(h @ fc1_w.T + fc1_b, approximate=True) @ fc2_w.T + fc2_b
        x = x + gate_mlp[:, None, :] * h
        return x

    def _L1_cond_ref(x, t, W_ada, b_ada, ln1_g, ln1_b, Wqkv, qn_g, qn_b, kn_g, kn_b, Wout, mlp_g, mlp_b, Wgate, fc1s, b1s, fc2s, b2s):
        import jax, jax.numpy as jnp
        import numpy as np
        B, N, D = (2, 512, 256)
        H, HD = (16, 64)
        E, DD = (8, 1024)
        EPS = 1e-05

        def _ln(x, g, b):
            m = jnp.mean(x, axis=-1, keepdims=True)
            v = jnp.var(x, axis=-1, keepdims=True)
            return (x - m) * jax.lax.rsqrt(v + EPS) * g + b
        b, n, d = x.shape
        shift = jax.nn.silu(t) @ W_ada.T + b_ada
        h = _ln(x, ln1_g, ln1_b) + shift
        qkv = (h @ Wqkv.T).reshape(b, n, 3, H, HD)
        q = _ln(qkv[:, :, 0].transpose(0, 2, 1, 3), qn_g, qn_b)
        k = _ln(qkv[:, :, 1].transpose(0, 2, 1, 3), kn_g, kn_b)
        v = qkv[:, :, 2].transpose(0, 2, 1, 3)
        scores = jnp.einsum('bhnd,bhmd->bhnm', q, k) / jnp.sqrt(jnp.float32(HD))
        attn = jax.nn.softmax(scores, axis=-1)
        o = jnp.einsum('bhnm,bhmd->bhnd', attn, v)
        o = o.transpose(0, 2, 1, 3).reshape(b, n, H * HD)
        x = x + o @ Wout.T
        tok = x.reshape(-1, d)
        bs = tok.shape[0]
        gate = jax.nn.softmax(tok @ Wgate.T, axis=-1)
        k_cap = bs // E
        vals, idx = jax.lax.top_k(gate.T, k_cap)
        idx_flat = idx.T.reshape(-1)
        w = vals.T
        g = _ln(tok[idx_flat], mlp_g, mlp_b).reshape(k_cap, E, d)
        y = jnp.einsum('ked,ehd->keh', g, fc1s) + b1s
        y = jax.nn.gelu(y, approximate=True)
        y = jnp.einsum('keh,edh->ked', y, fc2s) + b2s
        y = y * w[..., None]
        tok = tok.at[idx_flat].add(y.reshape(-1, d))
        return tok.reshape(x.shape)
    x = _L0_cond_ref(x, cond_1024, mask_BxS_bk1, L0_cond_qkv_w, L0_cond_qkv_b, L0_cond_proj_w, L0_cond_proj_b, L0_cond_fc1_w, L0_cond_fc1_b, L0_cond_fc2_w, L0_cond_fc2_b, L0_cond_ada_w, L0_cond_ada_b)
    x = _L1_cond_ref(x, cond_1024[:, None, :], L1_cond_W_ada, L1_cond_b_ada, L1_cond_ln1_g, L1_cond_ln1_b, L1_cond_Wqkv, L1_cond_qn_g, L1_cond_qn_b, L1_cond_kn_g, L1_cond_kn_b, L1_cond_Wout, L1_cond_mlp_g, L1_cond_mlp_b, L1_cond_Wgate, L1_cond_fc1s, L1_cond_b1s, L1_cond_fc2s, L1_cond_b2s)
    return x

_drawn_inputs = setup_inputs


def setup_inputs(seed=0):
    import zlib

    import numpy as np

    out = dict(_drawn_inputs(seed))
    spreads = {'L0_cond_qkv_b': (0.0, 0.8),
     'L0_cond_proj_b': (0.0, 0.323),
     'L0_cond_fc1_b': (0.0, 0.8),
     'L0_cond_fc2_b': (0.0, 0.354),
     'L0_cond_ada_b': (0.0, 0.378),
     'L1_cond_b_ada': (0.0, 0.333),
     'L1_cond_ln1_g': (1.0, 0.6),
     'L1_cond_ln1_b': (0.0, 0.415),
     'L1_cond_qn_g': (1.0, 0.6),
     'L1_cond_qn_b': (0.0, 2.0),
     'L1_cond_kn_g': (1.0, 0.6),
     'L1_cond_kn_b': (0.0, 2.0),
     'L1_cond_mlp_g': (1.0, 0.6),
     'L1_cond_mlp_b': (0.0, 2.0),
     'L1_cond_b1s': (0.0, 0.8),
     'L1_cond_b2s': (0.0, 0.424)}
    factors = {'L0_cond_qkv_w': 8.0, 'L0_cond_proj_w': 6.184, 'L1_cond_W_ada': 3.023}
    for name, (base, spread) in spreads.items():
        noise = np.random.default_rng([zlib.crc32(name.encode()), seed]).standard_normal(out[name].shape)
        drawn = base * np.exp(spread * noise) if base else spread * noise
        out[name] = jnp.asarray(drawn.astype(out[name].dtype))
    for name, factor in factors.items():
        out[name] = (out[name] * factor).astype(out[name].dtype)
    return out
```

```python
import numpy as np
import concourse.bass as bass
from concourse import mybir
from contextlib import ExitStack

F32 = mybir.dt.float32
BF16 = mybir.dt.bfloat16
I32 = mybir.dt.int32
U32 = mybir.dt.uint32
U8 = mybir.dt.uint8
ALU = mybir.AluOpType
ACT = mybir.ActivationFunctionType
AX = mybir.AxisListType.X

P = 128
B, S, D = 128, 64, 256
TOK = B * S
NT = TOK // P
DC = D // P
H = 16
HD0 = D // H
HD1 = 64
QK1 = 2 * H * HD1
V1 = H * HD1
MLP = 4 * D
MC = MLP // P
GT = 4
GTOK = GT * P
NG = NT // GT
E = 8
CAP = TOK // E
SH = CAP // P
EPS0, EPS1 = 1e-6, 1e-5
SCALE0, SCALE1 = HD0 ** -0.5, HD1 ** -0.5
HIDE = -1e30
NOSLOT = 4096.0

C_ID, C_UP, C_SAME, C_IOTA = 0, P, 2 * P, 3 * P
C_HEAD = 4 * P
C_PICK = C_HEAD + 8
C_P = C_PICK + 8
C_ROW = C_P + 1
C_GROW = C_ROW + 8
C_BITS = C_GROW + 8
BITS = 30
C_ALL = C_BITS + BITS + 1


def constants():
    c = np.zeros((P, C_ALL), np.float32)
    p = np.arange(P)
    c[:, C_ID:C_ID + P] = np.eye(P)
    c[:, C_UP:C_UP + P] = p[:, None] < p[None, :]
    c[:, C_SAME:C_SAME + P] = p[:, None] // 16 == p[None, :] // 16
    c[:, C_IOTA:C_IOTA + P] = p[None, :]
    c[:, C_HEAD:C_HEAD + 8] = p[:, None] // 16 == np.arange(8)[None, :]
    c[:, C_PICK:C_PICK + 8] = p[:, None] == 16 * np.arange(8)[None, :]
    c[:, C_P] = p
    for j in range(8):
        c[j, C_ROW + j], c[8 + j, C_ROW + j] = P, 1
        c[j, C_GROW + j], c[8 + j, C_GROW + j] = 1, NT
    c[:, C_BITS:C_BITS + BITS] = 2.0 ** np.arange(BITS - 1, -1, -1)
    return c


def pipeline(eng, step, n, before, after):
    def edge(i):
        step(i, lambda k: 0 <= i + k < n)
    for i in range(-before, after):
        edge(i)
    with eng.Fori(after, n - before) as i:
        step(i, lambda k: True)
    for i in range(n - before, n + after):
        edge(i)


def later(t):
    return not isinstance(t, int) or t > 0


def block_of(PT, b_pt, half, b, e):
    to = PT[b * S:(b + 1) * S, half * 8:half * 8 + 8, b * S:(b + 1) * S]
    src = b_pt[e * S:(e + 1) * S, half * 4 * P:(half + 1) * 4 * P].rearrange("p (j q) -> p j q", q=P)
    return to.rearrange("p (j e) q -> p e j q", e=2)[:, e], src[:, :, b * S:(b + 1) * S]


class Mem:

    def __init__(self, nc, ctx):
        self.nc, self.ctx, self.sems = nc, ctx, []

    def sb(self, name, shape, dt=F32):
        return self.ctx.enter_context(self.nc.sbuf_tensor(name, shape, dt))

    def ps(self, name, cols):
        return self.ctx.enter_context(self.nc.psum_tensor(name, [P, cols], F32))

    def sem(self, name):
        self.sems.append(self.nc.alloc_semaphore(name))
        return self.sems[-1]

    def clear(self):
        self.nc.all_engine_barrier()
        self.nc.clear_and_free_semaphores(self.sems)
        self.nc.all_engine_barrier()


def setup_phase(nc, a, g):
    with ExitStack() as ctx:
        m = Mem(nc, ctx)
        wada = m.sb("wada", [P, DC, 6 * D])
        wada1 = m.sb("wada1", [P, DC, D])
        cT = m.sb("cT", [P, DC, B])
        sT = m.sb("sT", [P, DC, B])
        adab = m.sb("adab", [P, 4 * DC])
        bada1 = m.sb("bada1", [P, DC])
        ln1b = m.sb("ln1b", [P, DC])
        gbias = m.sb("gbias", [P, 2 * D])
        gates = m.sb("gates", [P, 2 * D])
        mask_keys = m.sb("mask_keys", [P, NT, S], U8)
        mask_rows = m.sb("mask_rows", [P, NT], U8)
        keysf = m.sb("keysf", [P, NT, S])
        hide = m.sb("hide", [P, NT])
        shb = m.sb("shb", [P, DC])
        pt = [m.ps(f"pmod{j}", 4 * P) for j in range(2)]
        pg = [m.ps(f"pgate{j}", 4 * P) for j in range(2)]
        loaded_c, loaded_w, loaded_b, loaded_m = (m.sem(n) for n in
                                                  ("loaded_c", "loaded_w", "loaded_b", "loaded_m"))
        silu_done, table_mm, table_out = m.sem("silu_done"), m.sem("table_mm"), m.sem("table_out")
        gate_mm, gate_out, gate_saved = m.sem("gate_mm"), m.sem("gate_out"), m.sem("gate_saved")
        keys_f, hide_done, hidden_done = m.sem("keys_f"), m.sem("hide_done"), m.sem("hidden_done")
        cleared, shift_bias = m.sem("cleared"), m.sem("shift_bias")
        parts = [(g.sh_a, 0, 0), (g.sc_a, 1, 0), (g.sh_m, 3, 1), (g.sc_m, 4, 1)]
        jobs = [(tab, k, c, n) for n, (tab, k, _) in enumerate(parts) for c in range(DC)]
        jobs += [(g.sh_1, None, c, 4) for c in range(DC)]
        with nc.Block() as block:
            @block.sync
            def _(sp):
                sp.dma_start(cT[:, :, :], a["condT"]).then_inc(loaded_c, 16)
                sp.dma_start(wada[:, :, :], a["ada_w"]).then_inc(loaded_w, 16)
                sp.dma_start(wada1[:, :, :], a["ada1_w"]).then_inc(loaded_w, 16)
                sp.dma_start(adab[:, :], a["ada_b"]).then_inc(loaded_b, 16)
                sp.dma_start(bada1[:, :], a["ada1_b"]).then_inc(loaded_b, 16)
                sp.dma_start(ln1b[:, :], a["ln1_b"]).then_inc(loaded_b, 16)
                for j, k in enumerate((2, 5)):
                    sp.dma_start(gbias[:, j * D:(j + 1) * D],
                                 a["ada_row"][:, k * D:(k + 1) * D].to_broadcast([P, D])).then_inc(loaded_b, 16)
                for s in range(2):
                    sp.dma_start(mask_keys[s * S:(s + 1) * S, :, :],
                                 a["mask"].rearrange("(t s) k -> s t k", s=2)[s:s + 1]
                                 .to_broadcast([S, NT, S])).then_inc(loaded_m, 16)
                sp.dma_start(mask_rows[:, :], a["maskT"]).then_inc(loaded_m, 16)
                for w, n in ((g.wqkv0, "qkv0_w"), (g.wproj0, "proj0_w"), (g.qkb0, "qk0_b"), (g.ln1g, "ln1_g")):
                    sp.dma_start(w, a[n]).then_inc(g.loaded, 16)
                sp.dma_start(g.vb0, a["qkv0_row"][:, 2 * D:].to_broadcast([P, D])).then_inc(g.loaded, 16)
                sp.dma_start(g.pb0, a["proj0_row"].to_broadcast([P, D])).then_inc(g.loaded, 16)
                sp.dma_start(g.cst, a["consts"]).then_inc(g.loaded, 16)
                sp.wait_ge(g.loaded, 16 * 7)
                sp.wait_ge(gate_out, 2)
                sp.dma_start(g.gate_dram, gates[:, :]).then_inc(gate_saved, 16)
                sp.wait_ge(gate_saved, 16)

            @block.gpsimd
            def _(pool):
                nc.gpsimd.memset(g.PT[:, :, :], 0.0).then_inc(cleared, 1)
                nc.gpsimd.memset(g.vm[:, :, :, :], 0.0).then_inc(cleared, 1)
                nc.gpsimd.memset(g.mhalf[:, :], -0.5).then_inc(cleared, 1)
                pool.wait_ge(loaded_m, 48)
                nc.gpsimd.tensor_scalar(keysf[:, :, :], mask_keys[:, :, :], -1.0, None, ALU.add).then_inc(keys_f, 1)
                nc.gpsimd.tensor_scalar(g.mrow, mask_rows[:, :], 1.0, None, ALU.mult).then_inc(keys_f, 1)
                nc.gpsimd.tensor_scalar(hide[:, :], mask_rows[:, :], -HIDE, None, ALU.mult).then_inc(keys_f, 1)
                pool.wait_ge(keys_f, 3)
                nc.gpsimd.tensor_tensor(g.hidden, keysf[:, :, :],
                                        hide[:, :].unsqueeze(2).to_broadcast([P, NT, S]), ALU.mult)\
                    .then_inc(hidden_done, 1)

            @block.scalar
            def _(act):
                act.wait_ge(loaded_c, 16)
                nc.scalar.activation(sT[:, :, :], cT[:, :, :], ACT.Silu).then_inc(silu_done, 1)

            @block.tensor
            def _(pe):
                pe.wait_ge(silu_done, 1)
                pe.wait_ge(loaded_w, 32)
                for n, (tab, k, c, _) in enumerate(jobs):
                    if n >= 2:
                        pe.wait_ge(table_out, n - 1)
                    for kc in range(DC):
                        w = wada1[:, kc, c * P:(c + 1) * P] if k is None else \
                            wada[:, kc, k * D + c * P:k * D + (c + 1) * P]
                        last = nc.tensor.matmul(pt[n % 2][:, 0:P], w, sT[:, kc, :],
                                                start=(kc == 0), stop=(kc == DC - 1))
                    last.then_inc(table_mm, 1)
                for j, k in enumerate((2, 5)):
                    for kc in range(DC):
                        last = nc.tensor.matmul(pg[j][:, 0:D], sT[:, kc, :],
                                                wada[:, kc, k * D:(k + 1) * D],
                                                start=(kc == 0), stop=(kc == DC - 1))
                    last.then_inc(gate_mm, 1)

            @block.vector
            def _(dve):
                dve.wait_ge(loaded_b, 16 * 5)
                nc.vector.tensor_tensor(shb[:, :], bada1[:, :], ln1b[:, :], ALU.add).then_inc(shift_bias, 1)
                dve.wait_ge(shift_bias, 1)
                for n, (tab, k, c, q) in enumerate(jobs):
                    dve.wait_ge(table_mm, n + 1)
                    if k is None:
                        ins = nc.vector.tensor_scalar(tab[:, c, :], pt[n % 2][:, 0:P], shb[:, c:c + 1], None, ALU.add)
                    else:
                        ins = nc.vector.tensor_scalar(tab[:, c, :], pt[n % 2][:, 0:P],
                                                      adab[:, 2 * q + c:2 * q + c + 1],
                                                      float(q % 2), ALU.add, ALU.add)
                    ins.then_inc(table_out, 1)
                for j in range(2):
                    dve.wait_ge(gate_mm, j + 1)
                    nc.vector.tensor_tensor(gates[:, j * D:(j + 1) * D], pg[j][:, 0:D],
                                            gbias[:, j * D:(j + 1) * D], ALU.add).then_inc(gate_out, 1)
        m.clear()


def attention0_phase(nc, a, g):
    with ExitStack() as ctx:
        m = Mem(nc, ctx)
        xhat = m.sb("a0_xhat", [P, D])
        st = m.sb("a0_st", [P, 6])
        mv = m.sb("a0_mv", [P, 2])
        veps = m.sb("a0_veps", [P, 1])
        rstd = m.sb("a0_rstd", [P, 1])
        hT = m.sb("a0_hT", [P, DC, P])
        hm = m.sb("a0_hm", [P, DC, P])
        qT = m.sb("a0_qT", [P, DC, P])
        kT = m.sb("a0_kT", [P, DC, P])
        kbd = m.sb("a0_kbd", [P, DC, 2, 8, S])
        vall = m.sb("a0_v", [P, NT, D])
        pr = m.sb("a0_p", [P, H, S])
        mx = m.sb("a0_mx", [P, H])
        sm = m.sb("a0_sm", [P, H])
        rs = m.sb("a0_rs", [P, H])
        oT = m.sb("a0_oT", [P, DC, P])
        gt = m.sb("a0_gate", [P, D])
        tmp = m.sb("a0_tmp", [P, D])
        tmp2 = m.sb("a0_tmp2", [P, D])
        b_qk, b_vt = m.ps("a0_bqk", 4 * P), m.ps("a0_bvt", 4 * P)
        b_s, b_pt = m.ps("a0_bs", H * S), m.ps("a0_bpt", H * S)
        b_o, b_pj = m.ps("a0_bo", 4 * P), m.ps("a0_bpj", 4 * P)
        names = ("x_in stats aggr eps rstd xhat xT h_mul hT qk v q_out k_out kbd v_out vm s scored maxed "
                 "shifted exped summed recip probs pT pT_act pT_dve o oT proj p1 p2 res gate").split()
        s = {n: m.sem("a0_" + n) for n in names}
        ident = g.cst[:, C_ID:C_ID + P]
        PT = g.PT

        with nc.Block() as block:
            @block.sync
            def _(sp):
                AHEAD = 8

                def load_x(t):
                    if later(t):
                        sp.wait_ge(s["x_in"], 16 * t)
                    sp.dma_start(g.X[:, t, :], a["x"][t]).then_inc(s["x_in"], 16)

                def load_gates(t):
                    if later(t):
                        sp.wait_ge(s["p2"], t)
                    for b in range(2):
                        sp.dma_start(gt[b * S:(b + 1) * S, :],
                                     g.gate_dram[bass.ds(2 * t + b, 1), 0:D].to_broadcast([S, D]))\
                            .then_inc(s["gate"], 16)
                for t in range(AHEAD):
                    load_x(t)
                load_gates(0)
                with sp.Fori(1, NT - AHEAD + 1) as t:
                    load_x(t + AHEAD - 1)
                    load_gates(t)
                with sp.Fori(NT - AHEAD + 1, NT) as t:
                    load_gates(t)

            @block.scalar
            def _(act):
                def step(i, has):
                    if has(-2):
                        act.wait_ge(s["pT"], i - 1)
                        for b in range(2):
                            for e in range(2):
                                last = nc.scalar.copy(*block_of(PT, b_pt, 0, b, e))
                        last.then_inc(s["pT_act"], 1)
                    if has(0):
                        act.wait_ge(s["qk"], i + 1)
                        if later(i):
                            act.wait_ge(s["s"], i)
                        for c in range(DC):
                            last = nc.scalar.activation(qT[:, c, :], b_qk[:, c * P:(c + 1) * P], ACT.Identity,
                                                        bias=g.qkb0[:, c:c + 1])
                        last.then_inc(s["q_out"], 1)
                        if later(i):
                            act.wait_ge(s["kbd"], i)
                        for c in range(DC):
                            last = nc.scalar.activation(kT[:, c, :], b_qk[:, (DC + c) * P:(DC + c + 1) * P],
                                                        ACT.Identity, bias=g.qkb0[:, DC + c:DC + c + 1])
                        last.then_inc(s["k_out"], 1)
                    if has(-2):
                        act.wait_ge(s["o"], i - 1)
                        nc.scalar.copy(oT[:, :, :], b_o[:, 0:DC * P].rearrange("p (c t) -> p c t", c=DC))\
                            .then_inc(s["oT"], 1)
                    if has(-1):
                        act.wait_ge(s["shifted"], i)
                        nc.scalar.activation(pr[:, :, :], pr[:, :, :], ACT.Exp, scale=SCALE0).then_inc(s["exped"], 1)
                pipeline(act, step, NT, 0, 3)

            @block.gpsimd
            def _(pool):
                def ln_power(t):
                    pool.wait_ge(s["eps"], t + 1)
                    nc.gpsimd.tensor_tensor(rstd[:, :], veps[:, :], g.mhalf[:, 0:1], ALU.pow).then_inc(s["rstd"], 1)

                def step(i, has):
                    if has(2):
                        ln_power(i + 2)
                    if has(-2):
                        pool.wait_ge(s["v_out"], i - 1)
                        if later(i - 2):
                            pool.wait_ge(s["o"], i - 2)
                        for e in range(2):
                            last = nc.gpsimd.tensor_copy(
                                g.vm[:, e, :, e * HD0:(e + 1) * HD0],
                                vall[:, i - 2, :].rearrange("p (j e d) -> p e j d", e=2, d=HD0)[:, e])
                        last.then_inc(s["vm"], 1)
                    if has(0):
                        pool.wait_ge(s["k_out"], i + 1)
                        for c in range(DC):
                            last = nc.gpsimd.tensor_tensor(
                                kbd[:, c, :, :, :],
                                kT[:, c, :].rearrange("p (b k) -> p b k", b=2).unsqueeze(2).to_broadcast([P, 2, 8, S]),
                                g.cst[:, C_HEAD:C_HEAD + 8].unsqueeze(1).unsqueeze(3).to_broadcast([P, 2, 8, S]),
                                ALU.mult)
                        last.then_inc(s["kbd"], 1)
                pipeline(pool, step, NT, 2, 3)

            @block.vector
            def _(dve):
                def stats(t):
                    dve.wait_ge(s["x_in"], 16 * (t + 1))
                    nc.vector.bn_stats(st[:, :], g.X[:, t, :]).then_inc(s["stats"], 1)

                def variance(t):
                    nc.vector.bn_aggr(mv[:, :], st[:, :]).then_inc(s["aggr"], 1)
                    dve.wait_ge(s["aggr"], t + 1)
                    nc.vector.tensor_scalar(veps[:, :], mv[:, 1:2], EPS0, None, ALU.add).then_inc(s["eps"], 1)

                def normal(t):
                    dve.wait_ge(s["rstd"], t + 1)
                    if later(t):
                        dve.wait_ge(s["xT"], t)
                    nc.vector.tensor_scalar(xhat[:, :], g.X[:, t, :], mv[:, 0:1], rstd[:, 0:1],
                                            ALU.subtract, ALU.mult).then_inc(s["xhat"], 1)

                def step(i, has):
                    if has(2):
                        stats(i + 2)
                        dve.wait_ge(s["stats"], i + 3)
                    if has(0):
                        dve.wait_ge(s["v"], i + 1)
                        nc.vector.tensor_tensor(vall[:, i, :], b_vt[:, 0:D], g.vb0, ALU.add).then_inc(s["v_out"], 1)
                    if has(2):
                        variance(i + 2)
                    if has(-2):
                        dve.wait_ge(s["pT"], i - 1)
                        for b in range(2):
                            for e in range(2):
                                last = nc.vector.tensor_copy(*block_of(PT, b_pt, 1, b, e))
                        last.then_inc(s["pT_dve"], 1)
                    if has(1):
                        dve.wait_ge(s["xT"], i + 2)
                        nc.vector.tensor_tensor(
                            hm[:, :, :].rearrange("p c (b t) -> p c b t", b=2),
                            b_vt[:, D:2 * D].rearrange("p (c b t) -> p c b t", c=DC, b=2),
                            g.sc_a[:, :, bass.ds(2 * (i + 1), 2)].unsqueeze(3).to_broadcast([P, DC, 2, S]),
                            ALU.mult).then_inc(s["h_mul"], 1)
                        dve.wait_ge(s["h_mul"], i + 2)
                        nc.vector.tensor_tensor(
                            hT[:, :, :].rearrange("p c (b t) -> p c b t", b=2),
                            hm[:, :, :].rearrange("p c (b t) -> p c b t", b=2),
                            g.sh_a[:, :, bass.ds(2 * (i + 1), 2)].unsqueeze(3).to_broadcast([P, DC, 2, S]),
                            ALU.add).then_inc(s["hT"], 1)
                    if has(-3):
                        dve.wait_ge(s["proj"], i - 2)
                        nc.vector.tensor_tensor(tmp[:, :], b_pj[:, 0:D], g.pb0, ALU.add).then_inc(s["p1"], 1)
                        dve.wait_ge(s["p1"], i - 2)
                        dve.wait_ge(s["gate"], 32 * (i - 2))
                        nc.vector.tensor_tensor(tmp2[:, :], tmp[:, :], gt[:, :], ALU.mult).then_inc(s["p2"], 1)
                        dve.wait_ge(s["p2"], i - 2)
                        nc.vector.tensor_tensor(g.X[:, i - 3, :], g.X[:, i - 3, :], tmp2[:, :], ALU.add)\
                            .then_inc(s["res"], 1)
                    if has(-1):
                        dve.wait_ge(s["s"], i)
                        nc.vector.scalar_tensor_tensor(
                            pr[:, :, :], b_s[:, :].rearrange("p (h k) -> p h k", h=H), g.mrow[:, bass.ds(i - 1, 1)],
                            g.hidden[:, i - 1, :].unsqueeze(1).to_broadcast([P, H, S]),
                            ALU.mult, ALU.add).then_inc(s["scored"], 1)
                        dve.wait_ge(s["scored"], i)
                        nc.vector.reduce_max(mx[:, :], pr[:, :, :], AX).then_inc(s["maxed"], 1)
                        dve.wait_ge(s["maxed"], i)
                        nc.vector.tensor_tensor(pr[:, :, :], pr[:, :, :],
                                                mx[:, :].unsqueeze(2).to_broadcast([P, H, S]), ALU.subtract)\
                            .then_inc(s["shifted"], 1)
                    if has(2):
                        normal(i + 2)
                    if has(-1):
                        dve.wait_ge(s["exped"], i)
                        nc.vector.reduce_sum(sm[:, :], pr[:, :, :], AX).then_inc(s["summed"], 1)
                        dve.wait_ge(s["summed"], i)
                        nc.vector.reciprocal(rs[:, :], sm[:, :]).then_inc(s["recip"], 1)
                        dve.wait_ge(s["recip"], i)
                        nc.vector.tensor_tensor(pr[:, :, :], pr[:, :, :],
                                                rs[:, :].unsqueeze(2).to_broadcast([P, H, S]), ALU.mult)\
                            .then_inc(s["probs"], 1)
                pipeline(dve, step, NT, 2, 3)

            @block.tensor
            def _(pe):
                def transpose_x(t):
                    pe.wait_ge(s["xhat"], t + 1)
                    if later(t):
                        pe.wait_ge(s["hT"], t)
                        pe.wait_ge(s["v_out"], t)
                    for c in range(DC):
                        last = nc.tensor.transpose(b_vt[:, D + c * P:D + (c + 1) * P],
                                                   xhat[:, c * P:(c + 1) * P], ident)
                    last.then_inc(s["xT"], 1)

                def step(i, has):
                    if has(0):
                        pe.wait_ge(s["hT"], i + 1)
                        if later(i):
                            pe.wait_ge(s["k_out"], i)
                        for n in range(2 * DC):
                            for kc in range(DC):
                                last = nc.tensor.matmul(b_qk[:, n * P:(n + 1) * P],
                                                        g.wqkv0[:, kc, n * P:(n + 1) * P], hT[:, kc, :],
                                                        start=(kc == 0), stop=(kc == DC - 1))
                        last.then_inc(s["qk"], 1)
                        if later(i):
                            pe.wait_ge(s["v_out"], i)
                        for kc in range(DC):
                            last = nc.tensor.matmul(b_vt[:, 0:D], hT[:, kc, :], g.wqkv0[:, kc, 2 * D:3 * D],
                                                    start=(kc == 0), stop=(kc == DC - 1))
                        last.then_inc(s["v"], 1)
                    if has(-3):
                        pe.wait_ge(s["oT"], i - 2)
                        if later(i - 3):
                            pe.wait_ge(s["res"], i - 3)
                        for kc in range(DC):
                            last = nc.tensor.matmul(b_pj[:, 0:D], oT[:, kc, :], g.wproj0[:, kc, :],
                                                    start=(kc == 0), stop=(kc == DC - 1))
                        last.then_inc(s["proj"], 1)
                    if has(-2):
                        pe.wait_ge(s["probs"], i - 1)
                        for j in range(H // 2):
                            last = nc.tensor.transpose(b_pt[:, j * P:(j + 1) * P],
                                                       pr[:, 2 * j:2 * j + 2, :].rearrange("p h k -> p (h k)"), ident)
                        last.then_inc(s["pT"], 1)
                    if has(1):
                        transpose_x(i + 1)
                    if has(-1):
                        pe.wait_ge(s["kbd"], i)
                        pe.wait_ge(s["q_out"], i)
                        for c in range(DC):
                            for b in range(2):
                                last = nc.tensor.matmul(b_s[b * S:(b + 1) * S, c * 512:(c + 1) * 512],
                                                        qT[:, c, b * S:(b + 1) * S],
                                                        kbd[:, c, b, :, :].rearrange("p h k -> p (h k)"),
                                                        start=True, stop=True)
                        last.then_inc(s["s"], 1)
                    if has(-2):
                        pe.wait_ge(s["pT_act"], i - 1)
                        pe.wait_ge(s["pT_dve"], i - 1)
                        pe.wait_ge(s["vm"], i - 1)
                        for j in range(H // 2):
                            r, c = j % 4, j // 4
                            for e in range(2):
                                last = nc.tensor.matmul(b_o[32 * r:32 * r + 32, c * P:(c + 1) * P],
                                                        g.vm[:, e, j, :], PT[:, 2 * j + e, :],
                                                        start=(e == 0), stop=(e == 1))
                        last.then_inc(s["o"], 1)
                pipeline(pe, step, NT, 1, 3)
        m.clear()


def mlp0_phase(nc, a, g):
    with ExitStack() as ctx:
        m = Mem(nc, ctx)
        w1 = m.sb("m0_w1", [P, DC, MLP])
        w2 = m.sb("m0_w2", [P, MC, D])
        b1 = m.sb("m0_b1", [P, MC])
        b2 = m.sb("m0_b2", [P, D])
        xhat = m.sb("m0_xhat", [P, GT, D])
        st = m.sb("m0_st", [P, GT, 6])
        mv = m.sb("m0_mv", [P, GT, 2])
        veps = m.sb("m0_veps", [P, GT])
        rstd = m.sb("m0_rstd", [P, GT])
        hm = m.sb("m0_hm", [P, DC, GTOK])
        hT = m.sb("m0_hT", [P, DC, GTOK])
        uT = m.sb("m0_uT", [P, MC, GTOK])
        gt = m.sb("m0_gate", [P, GT, D])
        tmp = m.sb("m0_tmp", [P, D])
        tmp2 = m.sb("m0_tmp2", [P, D])
        wsum = m.sb("wsum", [P, DC, 2 * H, HD1 // 2])
        wmean = m.sb("wmean", [P, DC, 2 * H])
        b_u = [m.ps(f"m0_bu{j}", GTOK) for j in range(4)]
        b_x = [m.ps(f"m0_bx{j}", GTOK) for j in range(DC)]
        b_y = [m.ps(f"m0_by{j}", GTOK) for j in range(2)]
        names = "w1 w2 gate stats aggr eps rstd xhat xT h_mul hT u gelu y p1 p2 res halved wmean".split()
        s = {n: m.sem("m0_" + n) for n in names}
        ident = g.cst[:, C_ID:C_ID + P]

        with nc.Block() as block:
            @block.sync
            def _(sp):
                sp.dma_start(w1[:, :, :], a["fc1_0_w"]).then_inc(s["w1"], 16)
                sp.dma_start(b1[:, :], a["fc1_0_b"]).then_inc(s["w1"], 16)
                sp.dma_start(w2[:, :, :], a["fc2_0_w"]).then_inc(s["w2"], 16)
                sp.dma_start(b2[:, :], a["fc2_0_row"].to_broadcast([P, D])).then_inc(s["w2"], 16)

                def load_gates(i):
                    if later(i):
                        sp.wait_ge(s["p2"], GT * i)
                    for b in range(2):
                        rows = g.gate_dram[bass.ds(2 * GT * i, 2 * GT), D:2 * D]\
                            .rearrange("(t b) d -> b t d", b=2)
                        sp.dma_start(gt[b * S:(b + 1) * S, :, :], rows[b:b + 1].to_broadcast([S, GT, D]))\
                            .then_inc(s["gate"], 16)
                load_gates(0)
                for w, n in ((g.wqkv1, "qkv1_w"), (g.wout1, "out1_w"), (g.wgate, "gate_w"), (g.qn, "qn"), (g.kn, "kn")):
                    sp.dma_start(w, a[n]).then_inc(g.loaded1, 16)
                with sp.Fori(1, NG) as i:
                    load_gates(i)

            @block.scalar
            def _(act):
                def step(i, has):
                    if has(0):
                        for n in range(MC):
                            act.wait_ge(s["u"], MC * i + n + 1)
                            if n == 0 and later(i):
                                act.wait_ge(s["y"], GT * i)
                            nc.scalar.activation(uT[:, n, :], b_u[n % 4][:, :], ACT.Gelu_apprx_tanh,
                                                 bias=b1[:, n:n + 1]).then_inc(s["gelu"], 1)
                act.wait_ge(s["w1"], 32)
                pipeline(act, step, NG, 2, 1)

            @block.gpsimd
            def _(pool):
                def step(i, has):
                    if has(2):
                        pool.wait_ge(s["eps"], i + 3)
                        nc.gpsimd.tensor_tensor(rstd[:, :], veps[:, :], g.mhalf[:, 0:GT], ALU.pow)\
                            .then_inc(s["rstd"], 1)
                pipeline(pool, step, NG, 2, 1)
                pool.wait_ge(g.loaded1, 16 * 5)
                heads = g.wqkv1[:, :, 0:QK1].rearrange("p c (h d) -> p c h d", d=HD1)
                n = HD1 // 2
                nc.gpsimd.tensor_tensor(wsum[:, :, :, 0:n], heads[:, :, :, 0:n], heads[:, :, :, n:2 * n], ALU.add)\
                    .then_inc(s["halved"], 1)
                halvings = 1
                while n > 1:
                    n //= 2
                    pool.wait_ge(s["halved"], halvings)
                    nc.gpsimd.tensor_tensor(wsum[:, :, :, 0:n], wsum[:, :, :, 0:n], wsum[:, :, :, n:2 * n], ALU.add)\
                        .then_inc(s["halved"], 1)
                    halvings += 1
                pool.wait_ge(s["halved"], halvings)
                nc.gpsimd.tensor_scalar(wmean[:, :, :], wsum[:, :, :, 0], 1.0 / HD1, None, ALU.mult)\
                    .then_inc(s["wmean"], 1)
                pool.wait_ge(s["wmean"], 1)
                for c in range(DC):
                    last = nc.gpsimd.tensor_tensor(heads[:, c], heads[:, c],
                                                   wmean[:, c, :].unsqueeze(2).to_broadcast([P, 2 * H, HD1]),
                                                   ALU.subtract)
                last.then_inc(g.centred, 1)

            @block.vector
            def _(dve):
                def stats(i):
                    for k in range(GT):
                        nc.vector.bn_stats(st[:, k, :], g.X[:, GT * i + k, :]).then_inc(s["stats"], 1)

                def variance(i):
                    for k in range(GT):
                        nc.vector.bn_aggr(mv[:, k, :], st[:, k, :]).then_inc(s["aggr"], 1)
                    dve.wait_ge(s["aggr"], GT * (i + 1))
                    nc.vector.tensor_scalar(veps[:, :], mv[:, :, 1], EPS0, None, ALU.add).then_inc(s["eps"], 1)

                def normal(i):
                    dve.wait_ge(s["rstd"], i + 1)
                    if later(i):
                        dve.wait_ge(s["xT"], i)
                    for k in range(GT):
                        nc.vector.tensor_scalar(xhat[:, k, :], g.X[:, GT * i + k, :], mv[:, k, 0:1], rstd[:, k:k + 1],
                                                ALU.subtract, ALU.mult).then_inc(s["xhat"], 1)

                def step(i, has):
                    if has(2):
                        stats(i + 2)
                        dve.wait_ge(s["stats"], GT * (i + 3))
                    if has(1):
                        dve.wait_ge(s["xT"], i + 2)
                        for c in range(DC):
                            nc.vector.tensor_tensor(
                                hm[:, c, :].rearrange("p (b t) -> p b t", t=S),
                                b_x[c][:, :].rearrange("p (b t) -> p b t", t=S),
                                g.sc_m[:, c, bass.ds(2 * GT * (i + 1), 2 * GT)].unsqueeze(2)
                                .to_broadcast([P, 2 * GT, S]), ALU.mult).then_inc(s["h_mul"], 1)
                        for c in range(DC):
                            dve.wait_ge(s["h_mul"], DC * (i + 1) + c + 1)
                            nc.vector.tensor_tensor(
                                hT[:, c, :].rearrange("p (b t) -> p b t", t=S),
                                hm[:, c, :].rearrange("p (b t) -> p b t", t=S),
                                g.sh_m[:, c, bass.ds(2 * GT * (i + 1), 2 * GT)].unsqueeze(2)
                                .to_broadcast([P, 2 * GT, S]), ALU.add).then_inc(s["hT"], 1)
                    if has(2):
                        variance(i + 2)
                        normal(i + 2)
                    if has(0):
                        dve.wait_ge(s["gate"], 32 * (i + 1))
                        for k in range(GT):
                            n = GT * i + k
                            dve.wait_ge(s["y"], n + 1)
                            nc.vector.tensor_tensor(tmp[:, :], b_y[k % 2][:, 0:D], b2[:, :], ALU.add)\
                                .then_inc(s["p1"], 1)
                            dve.wait_ge(s["p1"], n + 1)
                            nc.vector.tensor_tensor(tmp2[:, :], tmp[:, :], gt[:, k, :], ALU.mult)\
                                .then_inc(s["p2"], 1)
                            dve.wait_ge(s["p2"], n + 1)
                            nc.vector.tensor_tensor(g.X[:, n, :], g.X[:, n, :], tmp2[:, :], ALU.add)\
                                .then_inc(s["res"], 1)
                dve.wait_ge(s["w2"], 32)
                pipeline(dve, step, NG, 2, 1)
                dve.wait_ge(s["res"], NT)

            @block.tensor
            def _(pe):
                def transpose_x(i):
                    pe.wait_ge(s["xhat"], GT * (i + 1))
                    if later(i):
                        pe.wait_ge(s["hT"], DC * i)
                    for c in range(DC):
                        for k in range(GT):
                            last = nc.tensor.transpose(b_x[c][:, k * P:(k + 1) * P],
                                                       xhat[:, k, c * P:(c + 1) * P], ident)
                    last.then_inc(s["xT"], 1)

                def step(i, has):
                    if has(0):
                        pe.wait_ge(s["hT"], DC * (i + 1))
                        for n in range(MC):
                            if n >= 4:
                                pe.wait_ge(s["gelu"], MC * i + n - 3)
                            elif later(i):
                                pe.wait_ge(s["gelu"], MC * i + n - 3)
                            for kc in range(DC):
                                last = nc.tensor.matmul(b_u[n % 4][:, :], w1[:, kc, n * P:(n + 1) * P],
                                                        hT[:, kc, :], start=(kc == 0), stop=(kc == DC - 1))
                            last.then_inc(s["u"], 1)
                    if has(1):
                        transpose_x(i + 1)
                    if has(0):
                        pe.wait_ge(s["gelu"], MC * (i + 1))
                        for k in range(GT):
                            n = GT * i + k
                            if k >= 2:
                                pe.wait_ge(s["p1"], n - 1)
                            elif later(i):
                                pe.wait_ge(s["p1"], n - 1)
                            for kc in range(MC):
                                last = nc.tensor.matmul(b_y[k % 2][:, 0:D], uT[:, kc, k * P:(k + 1) * P],
                                                        w2[:, kc, :], start=(kc == 0), stop=(kc == MC - 1))
                            last.then_inc(s["y"], 1)
                pe.wait_ge(s["w1"], 32)
                pe.wait_ge(s["w2"], 32)
                pipeline(pe, step, NG, 2, 1)
        m.clear()


def attention1_phase(nc, a, out, g):
    with ExitStack() as ctx:
        m = Mem(nc, ctx)
        xhat = m.sb("a1_xhat", [P, D])
        st = m.sb("a1_st", [P, 6])
        mv = m.sb("a1_mv", [P, 2])
        veps = m.sb("a1_veps", [P, 1])
        rstd = m.sb("a1_rstd", [P, 1])
        hT = m.sb("a1_hT", [P, DC, P])
        sq = m.sb("a1_sq", [P, QK1])
        ss = m.sb("a1_ss", [P, 2 * H])
        vq = m.sb("a1_vq", [P, 2 * H])
        rq = m.sb("a1_rq", [P, 2 * H])
        qk = m.sb("a1_qk", [P, QK1])
        qT = m.sb("a1_qT", [P, H // 2, P])
        kbd = m.sb("a1_kbd", [P, H // 2, 2, 2, S])
        v = m.sb("a1_v", [P, V1])
        pr = m.sb("a1_p", [P, H, S])
        mx = m.sb("a1_mx", [P, H])
        sm = m.sb("a1_sm", [P, H])
        rs = m.sb("a1_rs", [P, H])
        oT = m.sb("a1_oT", [P, H // 2, P])
        xs = m.sb("a1_xs", [P, D])
        xsT = m.sb("a1_xsT", [P, DC, P])
        b_qk = m.ps("a1_bqk", QK1)
        b_a = m.ps("a1_ba", H * S)
        b_b = m.ps("a1_bb", H * S)
        BK = 512
        names = ("stats aggr eps rstd xhat xT hT qk sq red vq rq qn kn qkT q_out kbd_lo kbd_hi v v_out s maxed "
                 "shifted exped summed recip probs pT pT_act pT_dve o oT proj res xsT xsT_out lg lg_out "
                 "stored cleared").split()
        s = {n: m.sem("a1_" + n) for n in names}
        ident = g.cst[:, C_ID:C_ID + P]
        PT = g.PT
        QG = 4

        with nc.Block() as block:
            @block.sync
            def _(sp):
                def store(t):
                    sp.wait_ge(s["res"], t + 1)
                    sp.dma_start(g.tok_dram[t], xs[:, :]).then_inc(s["stored"], 16)
                    sp.dma_start(out[t], xs[:, :]).then_inc(s["stored"], 16)
                with sp.Fori(0, NT) as t:
                    store(t)
                sp.wait_ge(s["stored"], 32 * NT)

            @block.scalar
            def _(act):
                def step(i, has):
                    if has(0):
                        for n in range(QG):
                            act.wait_ge(s["qk"], QG * i + n + 1)
                            if later(i):
                                act.wait_ge(s["red"], QG * i + n - QG + 1)
                            nc.scalar.activation(sq[:, n * BK:(n + 1) * BK], b_qk[:, n * BK:(n + 1) * BK],
                                                 ACT.Square).then_inc(s["sq"], 1)
                            if n == 0 and has(-1):
                                act.wait_ge(s["shifted"], i)
                                nc.scalar.activation(pr[:, :, :], pr[:, :, :], ACT.Exp, scale=SCALE1)\
                                    .then_inc(s["exped"], 1)
                    elif has(-1):
                        act.wait_ge(s["shifted"], i)
                        nc.scalar.activation(pr[:, :, :], pr[:, :, :], ACT.Exp, scale=SCALE1)\
                            .then_inc(s["exped"], 1)
                    if has(-1):
                        act.wait_ge(s["pT"], i)
                        for b in range(2):
                            for e in range(2):
                                last = nc.scalar.copy(*block_of(PT, b_b, 0, b, e))
                        last.then_inc(s["pT_act"], 1)
                        act.wait_ge(s["o"], i)
                        nc.scalar.copy(oT[:, :, :].rearrange("p j t -> p (j t)"), b_b[:, :]).then_inc(s["oT"], 1)
                    if has(0):
                        act.wait_ge(s["v"], i + 1)
                        nc.scalar.copy(v[:, :], b_a[:, :]).then_inc(s["v_out"], 1)
                        act.wait_ge(s["qkT"], i + 1)
                        nc.scalar.activation(qT[:, :, :].rearrange("p j t -> p (j t)"), b_qk[:, 0:V1], ACT.Identity,
                                             bias=g.qn[:, 1:2], scale=g.qn[:, 0:1]).then_inc(s["q_out"], 1)
                        if not later(i):
                            act.wait_ge(s["cleared"], 1)
                        nc.scalar.activation(kbd[0:S, :, :, 0, :].rearrange("p j b k -> p (j b) k"),
                                             b_qk[0:S, V1:QK1].rearrange("p (n k) -> p n k", k=S), ACT.Identity,
                                             bias=g.kn[0:S, 1:2], scale=g.kn[0:S, 0:1]).then_inc(s["kbd_lo"], 1)
                act.wait_ge(g.loaded1, 16 * 5)
                pipeline(act, step, NT, 0, 2)

            @block.gpsimd
            def _(pool):
                def step(i, has):
                    if has(1):
                        pool.wait_ge(s["eps"], i + 2)
                        nc.gpsimd.tensor_tensor(rstd[:, :], veps[:, :], g.mhalf[:, 0:1], ALU.pow)\
                            .then_inc(s["rstd"], 1)
                    if has(0):
                        pool.wait_ge(s["vq"], i + 1)
                        nc.gpsimd.tensor_tensor(rq[:, :], vq[:, :], g.mhalf[:, 0:2 * H], ALU.pow)\
                            .then_inc(s["rq"], 1)
                nc.gpsimd.memset(kbd[:, :, :, :, :], 0.0).then_inc(s["cleared"], 1)
                pipeline(pool, step, NT, 1, 2)

            @block.vector
            def _(dve):
                def step(i, has):
                    if has(1):
                        nc.vector.bn_stats(st[:, :], g.X[:, i + 1, :]).then_inc(s["stats"], 1)
                        dve.wait_ge(s["stats"], i + 2)
                    if has(0):
                        dve.wait_ge(s["xT"], i + 1)
                        for c in range(DC):
                            last = nc.vector.scalar_tensor_tensor(
                                hT[:, c, :].rearrange("p (b t) -> p b t", b=2),
                                b_b[:, BK + c * P:BK + (c + 1) * P].rearrange("p (b t) -> p b t", b=2),
                                g.ln1g[:, c:c + 1],
                                g.sh_1[:, c, bass.ds(2 * i, 2)].unsqueeze(2).to_broadcast([P, 2, S]),
                                ALU.mult, ALU.add)
                        last.then_inc(s["hT"], 1)
                    if has(1):
                        nc.vector.bn_aggr(mv[:, :], st[:, :]).then_inc(s["aggr"], 1)
                    if has(-2):
                        dve.wait_ge(s["proj"], i - 1)
                        if later(i - 2):
                            dve.wait_ge(s["stored"], 32 * (i - 2))
                            dve.wait_ge(s["xsT"], i - 2)
                        nc.vector.tensor_tensor(xs[:, :], g.X[:, i - 2, :], b_b[:, 0:D], ALU.add)\
                            .then_inc(s["res"], 1)
                    if has(-1):
                        dve.wait_ge(s["s"], i)
                        nc.vector.reduce_max(mx[:, :], b_a[:, :].rearrange("p (h k) -> p h k", h=H), AX)\
                            .then_inc(s["maxed"], 1)
                        dve.wait_ge(s["maxed"], i)
                        nc.vector.tensor_tensor(pr[:, :, :], b_a[:, :].rearrange("p (h k) -> p h k", h=H),
                                                mx[:, :].unsqueeze(2).to_broadcast([P, H, S]), ALU.subtract)\
                            .then_inc(s["shifted"], 1)
                    if has(1):
                        dve.wait_ge(s["aggr"], i + 2)
                        nc.vector.tensor_scalar(veps[:, :], mv[:, 1:2], EPS1, None, ALU.add).then_inc(s["eps"], 1)
                    if has(-2):
                        dve.wait_ge(s["xsT"], i - 1)
                        nc.vector.tensor_copy(xsT[:, :, :].rearrange("p c t -> p (c t)"), b_b[:, 0:D])\
                            .then_inc(s["xsT_out"], 1)

                    def sums(n):
                        dve.wait_ge(s["sq"], QG * i + n + 1)
                        nc.vector.reduce_sum(ss[:, n * 8:(n + 1) * 8],
                                             sq[:, n * BK:(n + 1) * BK].rearrange("p (h d) -> p h d", d=HD1), AX)\
                            .then_inc(s["red"], 1)
                    if has(0):
                        sums(0)
                    if has(-1):
                        dve.wait_ge(s["exped"], i)
                        nc.vector.reduce_sum(sm[:, :], pr[:, :, :], AX).then_inc(s["summed"], 1)
                        dve.wait_ge(s["summed"], i)
                        nc.vector.reciprocal(rs[:, :], sm[:, :]).then_inc(s["recip"], 1)
                        dve.wait_ge(s["recip"], i)
                        nc.vector.tensor_tensor(pr[:, :, :], pr[:, :, :],
                                                rs[:, :].unsqueeze(2).to_broadcast([P, H, S]), ALU.mult)\
                            .then_inc(s["probs"], 1)
                    if has(0):
                        for n in range(1, QG):
                            sums(n)
                        dve.wait_ge(s["red"], QG * (i + 1))
                        nc.vector.tensor_scalar(vq[:, :], ss[:, :], 1.0 / HD1, EPS1, ALU.mult, ALU.add)\
                            .then_inc(s["vq"], 1)
                    if has(-2):
                        dve.wait_ge(s["lg"], i - 1)
                        nc.vector.tensor_copy(g.lg[:, :, bass.ds(i - 2, 1)], b_b[:, BK:BK + E].unsqueeze(2))\
                            .then_inc(s["lg_out"], 1)
                    if has(-1):
                        dve.wait_ge(s["pT"], i)
                        for b in range(2):
                            for e in range(2):
                                last = nc.vector.tensor_copy(*block_of(PT, b_b, 1, b, e))
                        last.then_inc(s["pT_dve"], 1)
                    if has(1):
                        dve.wait_ge(s["rstd"], i + 2)
                        if later(i + 1):
                            dve.wait_ge(s["xT"], i + 1)
                        nc.vector.tensor_scalar(xhat[:, :], g.X[:, i + 1, :], mv[:, 0:1], rstd[:, 0:1],
                                                ALU.subtract, ALU.mult).then_inc(s["xhat"], 1)
                    if has(0):
                        dve.wait_ge(s["rq"], i + 1)
                        if later(i):
                            dve.wait_ge(s["qkT"], i)
                        for n, done in enumerate(("qn", "kn")):
                            nc.vector.tensor_tensor(
                                qk[:, n * V1:(n + 1) * V1].rearrange("p (h d) -> p h d", h=H),
                                b_qk[:, n * V1:(n + 1) * V1].rearrange("p (h d) -> p h d", h=H),
                                rq[:, n * H:(n + 1) * H].unsqueeze(2).to_broadcast([P, H, HD1]), ALU.mult)\
                                .then_inc(s[done], 1)
                        dve.wait_ge(s["qkT"], i + 1)
                        if not later(i):
                            dve.wait_ge(s["cleared"], 1)
                        nc.vector.tensor_scalar(kbd[S:P, :, :, 1, :].rearrange("p j b k -> p (j b) k"),
                                                b_qk[S:P, V1:QK1].rearrange("p (n k) -> p n k", k=S),
                                                g.kn[S:P, 0:1], g.kn[S:P, 1:2], ALU.mult, ALU.add)\
                            .then_inc(s["kbd_hi"], 1)
                dve.wait_ge(g.loaded1, 16 * 5)
                pipeline(dve, step, NT, 1, 2)

            @block.tensor
            def _(pe):
                def step(i, has):
                    if has(-1):
                        pe.wait_ge(s["q_out"], i)
                        pe.wait_ge(s["kbd_lo"], i)
                        pe.wait_ge(s["kbd_hi"], i)
                        pe.wait_ge(s["v_out"], i)
                        for j in range(H // 2):
                            for b in range(2):
                                last = nc.tensor.matmul(b_a[b * S:(b + 1) * S, j * P:(j + 1) * P],
                                                        qT[:, j, b * S:(b + 1) * S],
                                                        kbd[:, j, b, :, :].rearrange("p e k -> p (e k)"),
                                                        start=True, stop=True)
                        last.then_inc(s["s"], 1)

                    def products(n):
                        for kc in range(DC):
                            last = nc.tensor.matmul(b_qk[:, n * BK:(n + 1) * BK], hT[:, kc, :],
                                                    g.wqkv1[:, kc, n * BK:(n + 1) * BK],
                                                    start=(kc == 0), stop=(kc == DC - 1))
                        last.then_inc(s["qk"], 1)
                    if has(0):
                        pe.wait_ge(s["hT"], i + 1)
                        products(0)
                        products(1)
                    if has(-2):
                        pe.wait_ge(s["res"], i - 1)
                        for c in range(DC):
                            last = nc.tensor.transpose(b_b[:, c * P:(c + 1) * P], xs[:, c * P:(c + 1) * P], ident)
                        last.then_inc(s["xsT"], 1)
                    if has(0):
                        products(2)
                        products(3)
                    if has(-2):
                        pe.wait_ge(s["xsT_out"], i - 1)
                        for kc in range(DC):
                            last = nc.tensor.matmul(b_b[:, BK:BK + E], xsT[:, kc, :], g.wgate[:, kc, :],
                                                    start=(kc == 0), stop=(kc == DC - 1))
                        last.then_inc(s["lg"], 1)
                    if has(-1):
                        pe.wait_ge(s["probs"], i)
                        if later(i - 1):
                            pe.wait_ge(s["lg_out"], i - 1)
                        for j in range(H // 2):
                            last = nc.tensor.transpose(b_b[:, j * P:(j + 1) * P],
                                                       pr[:, 2 * j:2 * j + 2, :].rearrange("p h k -> p (h k)"), ident)
                        last.then_inc(s["pT"], 1)
                    if has(0):
                        for n in range(2):
                            for kc in range(DC):
                                last = nc.tensor.matmul(b_a[:, n * BK:(n + 1) * BK], hT[:, kc, :],
                                                        g.wqkv1[:, kc, QK1 + n * BK:QK1 + (n + 1) * BK],
                                                        start=(kc == 0), stop=(kc == DC - 1))
                        last.then_inc(s["v"], 1)
                    if has(-1):
                        pe.wait_ge(s["pT_act"], i)
                        pe.wait_ge(s["pT_dve"], i)
                        for h in range(H):
                            r, j = h % 2, h // 2
                            last = nc.tensor.matmul(b_b[r * S:(r + 1) * S, j * P:(j + 1) * P],
                                                    v[:, h * HD1:(h + 1) * HD1], PT[:, h, :],
                                                    start=True, stop=True)
                        last.then_inc(s["o"], 1)
                    if has(0):
                        pe.wait_ge(s["qn"], i + 1)
                        pe.wait_ge(s["kn"], i + 1)
                        for j in range(H):
                            last = nc.tensor.transpose(b_qk[:, j * P:(j + 1) * P], qk[:, j * P:(j + 1) * P], ident)
                        last.then_inc(s["qkT"], 1)
                    if has(-1):
                        pe.wait_ge(s["oT"], i)
                        for kc in range(H // 2):
                            last = nc.tensor.matmul(b_b[:, 0:D], oT[:, kc, :], g.wout1[:, kc, :],
                                                    start=(kc == 0), stop=(kc == H // 2 - 1))
                        last.then_inc(s["proj"], 1)
                    if has(1):
                        pe.wait_ge(s["xhat"], i + 2)
                        for c in range(DC):
                            last = nc.tensor.transpose(b_b[:, BK + c * P:BK + (c + 1) * P],
                                                       xhat[:, c * P:(c + 1) * P], ident)
                        last.then_inc(s["xT"], 1)
                pe.wait_ge(g.loaded1, 16 * 5)
                pe.wait_ge(g.centred, 1)
                pipeline(pe, step, NT, 1, 2)
        m.clear()


def route_phase(nc, a, g):
    NE = E * NT
    with ExitStack() as ctx:
        m = Mem(nc, ctx)
        mx = m.sb("r_mx", [P, NT])
        sm = m.sb("r_sm", [P, NT])
        rs = m.sb("r_rs", [P, NT])
        pb = m.sb("r_prob", [P, E, NT])
        pbt = m.sb("r_prob_t", [P, NT, E])
        pbq = m.sb("r_prob_q", [P, 4, E, 16])
        byp = m.sb("r_by_expert", [P, 4 * P])
        junk = m.sb("r_junk", [P, 4 * P])
        cnt = m.sb("r_cnt", [P, 1])
        bitsi = m.sb("r_bitsi", [P, BITS + 1], I32)
        cand = m.sb("r_cand", [P, 1], I32)
        drop = m.sb("r_drop", [P, 1], I32)
        thr = m.sb("r_thr", [P, P])
        gt, eq = m.sb("r_gt", [P, E, NT], BF16), m.sb("r_eq", [P, E, NT], BF16)
        up, ones = m.sb("r_up", [P, P], BF16), m.sb("r_ones", [P, P], BF16)
        keep = m.sb("r_keep", [P, E, NT])
        inc_g, inc_e = m.sb("r_inc_g", [P, E, NT]), m.sb("r_inc_e", [P, E, NT])
        ag, ae = m.sb("r_ag", [P, E, NT]), m.sb("r_ae", [P, E, NT])
        bg, be = m.sb("r_bg", [P, E, NT]), m.sb("r_be", [P, E, NT])
        ce = m.sb("r_ce", [P, E, NT])
        sg, se = m.sb("r_sg", [P, E, NT]), m.sb("r_se", [P, E, NT])
        slot = m.sb("r_slot", [P, E, NT], I32)
        loi, hii = m.sb("r_loi", [P, E, NT], I32), m.sb("r_hii", [P, E, NT], I32)
        lo, hi = m.sb("r_lo", [P, E, NT], BF16), m.sb("r_hi", [P, E, NT], BF16)
        iota = m.sb("r_iota", [P, P], BF16)
        hot_lo = m.sb("r_hot_lo", [P, NT, P], BF16)
        hot_hi = m.sb("r_hot_hi", [P, NT, SH], BF16)
        pair = m.sb("r_pair", [P, NT, 2 * SH], BF16)
        lists = m.sb("r_lists", [2 * SH, P])
        b_t, b_n, b_l, b_i = (m.ps(f"r_b{n}", 512) for n in "tnli")
        b_pg, b_tg, b_pe, b_te = (m.ps(f"r_b{n}", 512) for n in ("pg", "tg", "pe", "te"))
        names = ("max sub exp sum recip prob prob_t prob_q saved tr by_p count counted drop cand thr_out thr_in "
                 "masks pre scan slots ints hot_lo hot_hi pair lists lists_out rows rows_out consts1").split()
        s = {n: m.sem("r_" + n) for n in names}
        cst = g.cst

        def over_tiles(x, n=NT):
            return x.unsqueeze(1).to_broadcast([P, E, n])

        with nc.Block() as block:
            @block.sync
            def _(sp):
                sp.wait_ge(s["prob_t"], 1)
                sp.dma_start(g.prob_dram, pbt[:, :, :]).then_inc(s["saved"], 16)
                sp.wait_ge(s["cand"], BITS + 1)
                sp.dma_start(g.thr_dram.rearrange("a p -> p a"), cand[:, :].bitcast(F32)).then_inc(s["thr_out"], 16)
                sp.wait_ge(s["thr_out"], 16)
                sp.dma_start(thr[:, :], g.thr_dram.to_broadcast([P, P])).then_inc(s["thr_in"], 16)
                sp.wait_ge(s["saved"], 16)

            @block.scalar
            def _(act):
                act.wait_ge(s["sub"], 1)
                nc.scalar.activation(pb[:, :, :], pb[:, :, :], ACT.Exp).then_inc(s["exp"], 1)
                act.wait_ge(s["tr"], 1)
                nc.scalar.copy(byp[:, :], b_t[:, :]).then_inc(s["by_p"], 1)

            @block.gpsimd
            def _(pool):
                nc.gpsimd.tensor_copy(up[:, :], cst[:, C_UP:C_UP + P]).then_inc(s["consts1"], 1)
                nc.gpsimd.tensor_copy(iota[:, :], cst[:, C_IOTA:C_IOTA + P]).then_inc(s["consts1"], 1)
                nc.gpsimd.memset(ones[:, :], 1.0).then_inc(s["consts1"], 1)
                nc.gpsimd.memset(keep[:, :, 1:NT], 1.0).then_inc(s["consts1"], 1)
                nc.gpsimd.memset(keep[:, :, 0:1], 0.0).then_inc(s["consts1"], 1)
                nc.gpsimd.tensor_copy(bitsi[:, :], cst[:, C_BITS:C_BITS + BITS + 1]).then_inc(s["consts1"], 1)

            @block.vector
            def _(dve):
                nc.vector.reduce_max(mx[:, :], g.lg[:, :, :].rearrange("p e t -> p t e"), AX).then_inc(s["max"], 1)
                dve.wait_ge(s["max"], 1)
                nc.vector.tensor_tensor(pb[:, :, :], g.lg[:, :, :], over_tiles(mx[:, :]), ALU.subtract)\
                    .then_inc(s["sub"], 1)
                dve.wait_ge(s["exp"], 1)
                nc.vector.reduce_sum(sm[:, :], pb[:, :, :].rearrange("p e t -> p t e"), AX).then_inc(s["sum"], 1)
                dve.wait_ge(s["sum"], 1)
                nc.vector.reciprocal(rs[:, :], sm[:, :]).then_inc(s["recip"], 1)
                dve.wait_ge(s["recip"], 1)
                nc.vector.tensor_tensor(pb[:, :, :], pb[:, :, :], over_tiles(rs[:, :]), ALU.mult)\
                    .then_inc(s["prob"], 1)
                dve.wait_ge(s["prob"], 1)
                nc.vector.tensor_copy(pbq[:, :, :, :], pb[:, :, :].rearrange("p e (b t) -> p b e t", b=4))\
                    .then_inc(s["prob_q"], 1)
                nc.vector.tensor_copy(pbt[:, :, :], pb[:, :, :].rearrange("p e t -> p t e")).then_inc(s["prob_t"], 1)
                dve.wait_ge(s["consts1"], 6)
                nc.vector.tensor_copy(cand[:, :], bitsi[:, 0:1]).then_inc(s["cand"], 1)
                dve.wait_ge(s["by_p"], 1)
                with dve.Fori(0, BITS) as i:
                    dve.wait_ge(s["cand"], i + 1)
                    nc.vector.tensor_scalar(junk[:, :], byp[:, :], cand[:, :].bitcast(F32), None, ALU.is_ge, ALU.add,
                                            accum_out=cnt[:, :]).then_inc(s["count"], 1)
                    dve.wait_ge(s["counted"], i + 1)
                    nc.vector.tensor_scalar(drop[:, :], b_n[:, 0:1], float(CAP), cst[:, bass.ds(C_BITS + i, 1)],
                                            ALU.is_lt, ALU.mult).then_inc(s["drop"], 1)
                    dve.wait_ge(s["drop"], i + 1)
                    nc.vector.scalar_tensor_tensor(cand[:, :], cand[:, :], bitsi[:, bass.ds(i + 1, 1)], drop[:, :],
                                                   ALU.bitwise_or, ALU.bitwise_xor).then_inc(s["cand"], 1)
                dve.wait_ge(s["thr_in"], 16)
                t8 = thr[:, :].rearrange("p (e t) -> p e t", t=16)[:, :, 0:1].to_broadcast([P, E, NT])
                nc.vector.tensor_tensor(gt[:, :, :], pb[:, :, :], t8, ALU.is_gt).then_inc(s["masks"], 1)
                nc.vector.tensor_tensor(eq[:, :, :], pb[:, :, :], t8, ALU.is_equal).then_inc(s["masks"], 1)
                dve.wait_ge(s["pre"], 4)
                for n, (inc, tot) in enumerate(((inc_g, b_tg), (inc_e, b_te))):
                    nc.vector.tensor_tensor_scan(inc[:, :, :].rearrange("p e t -> p (e t)"),
                                                 keep[:, :, :].rearrange("p e t -> p (e t)"), tot[:, :], 0.0,
                                                 ALU.mult, ALU.add).then_inc(s["scan"], 1)
                dve.wait_ge(s["scan"], 2)
                grid = "p (e t) -> p e t"
                nc.vector.tensor_tensor(ag[:, :, :], inc_g[:, :, :], b_tg[:, :].rearrange(grid, e=E), ALU.subtract)\
                    .then_inc(s["slots"], 1)
                nc.vector.tensor_tensor(ae[:, :, :], inc_e[:, :, :], b_te[:, :].rearrange(grid, e=E), ALU.subtract)\
                    .then_inc(s["slots"], 1)
                dve.wait_ge(s["slots"], 2)
                nc.vector.tensor_tensor(bg[:, :, :], ag[:, :, :], b_pg[:, :].rearrange(grid, e=E), ALU.add)\
                    .then_inc(s["slots"], 1)
                nc.vector.tensor_tensor(be[:, :, :], ae[:, :, :], b_pe[:, :].rearrange(grid, e=E), ALU.add)\
                    .then_inc(s["slots"], 1)
                dve.wait_ge(s["slots"], 4)
                nc.vector.scalar_tensor_tensor(sg[:, :, :], bg[:, :, :], -NOSLOT, gt[:, :, :], ALU.add, ALU.mult)\
                    .then_inc(s["slots"], 1)
                nc.vector.tensor_tensor(ce[:, :, :], be[:, :, :], inc_g[:, :, NT - 1:NT].to_broadcast([P, E, NT]),
                                        ALU.add).then_inc(s["slots"], 1)
                dve.wait_ge(s["slots"], 6)
                nc.vector.scalar_tensor_tensor(se[:, :, :], ce[:, :, :], -NOSLOT, eq[:, :, :], ALU.add, ALU.mult)\
                    .then_inc(s["slots"], 1)
                dve.wait_ge(s["slots"], 7)
                nc.vector.scalar_tensor_tensor(slot[:, :, :], sg[:, :, :], NOSLOT, se[:, :, :], ALU.add, ALU.add)\
                    .then_inc(s["slots"], 1)
                dve.wait_ge(s["slots"], 8)
                nc.vector.tensor_single_scalar(loi[:, :, :], slot[:, :, :], P - 1, ALU.bitwise_and)\
                    .then_inc(s["ints"], 1)
                nc.vector.tensor_single_scalar(hii[:, :, :], slot[:, :, :], 7, ALU.logical_shift_right)\
                    .then_inc(s["ints"], 1)
                dve.wait_ge(s["ints"], 2)
                nc.vector.tensor_copy(lo[:, :, :], loi[:, :, :]).then_inc(s["ints"], 1)
                nc.vector.tensor_copy(hi[:, :, :], hii[:, :, :]).then_inc(s["ints"], 1)
                dve.wait_ge(s["ints"], 4)

                def compact(e):
                    if later(e):
                        dve.wait_ge(s["lists"], e)
                    nc.vector.tensor_tensor(hot_lo[:, :, :], iota[:, :].unsqueeze(1).to_broadcast([P, NT, P]),
                                            lo[:, bass.ds(e, 1), :].rearrange("p e t -> p (e t)").unsqueeze(2)
                                            .to_broadcast([P, NT, P]), ALU.is_equal).then_inc(s["hot_lo"], 1)
                    nc.vector.tensor_tensor(hot_hi[:, :, :], cst[:, C_IOTA:C_IOTA + SH].unsqueeze(1)
                                            .to_broadcast([P, NT, SH]),
                                            hi[:, bass.ds(e, 1), :].rearrange("p e t -> p (e t)").unsqueeze(2)
                                            .to_broadcast([P, NT, SH]), ALU.is_equal).then_inc(s["hot_hi"], 1)
                    dve.wait_ge(s["hot_hi"], e + 1)
                    nc.vector.tensor_tensor(pair[:, :, 0:SH], hot_hi[:, :, :],
                                            cst[:, C_IOTA:C_IOTA + NT].unsqueeze(2).to_broadcast([P, NT, SH]),
                                            ALU.mult).then_inc(s["pair"], 1)
                    nc.vector.tensor_scalar(pair[:, :, SH:2 * SH], hot_hi[:, :, :], cst[:, C_P:C_P + 1], None,
                                            ALU.mult).then_inc(s["pair"], 1)
                    dve.wait_ge(s["lists"], e + 1)
                    nc.vector.tensor_copy(lists[:, :], b_l[0:2 * SH, 0:P]).then_inc(s["lists_out"], 1)
                    dve.wait_ge(s["rows"], e + 1)
                    nc.vector.tensor_copy(g.rows[:, bass.ds(e, 1), :], b_i[:, 0:2 * SH].unsqueeze(1))\
                        .then_inc(s["rows_out"], 1)
                compact(0)
                with dve.Fori(1, E) as e:
                    compact(e)
                dve.wait_ge(s["rows_out"], E)

            @block.tensor
            def _(pe):
                pe.wait_ge(s["prob_q"], 1)
                for b in range(4):
                    last = nc.tensor.transpose(b_t[:, b * P:(b + 1) * P],
                                               pbq[:, b, :, :].rearrange("p e t -> p (e t)"),
                                               cst[:, C_ID:C_ID + P])
                last.then_inc(s["tr"], 1)
                with pe.Fori(0, BITS) as i:
                    pe.wait_ge(s["count"], i + 1)
                    nc.tensor.matmul(b_n[:, 0:1], cst[:, C_SAME:C_SAME + P], cnt[:, :], start=True, stop=True)\
                        .then_inc(s["counted"], 1)
                pe.wait_ge(s["consts1"], 6)
                pe.wait_ge(s["masks"], 2)
                for w, mask, to in ((up, gt, b_pg), (ones, gt, b_tg), (up, eq, b_pe), (ones, eq, b_te)):
                    nc.tensor.matmul(to[:, :], w[:, :], mask[:, :, :].rearrange("p e t -> p (e t)"),
                                     start=True, stop=True).then_inc(s["pre"], 1)

                def compact(e):
                    pe.wait_ge(s["hot_lo"], e + 1)
                    pe.wait_ge(s["pair"], 2 * (e + 1))
                    for t in range(NT):
                        last = nc.tensor.matmul(b_l[0:2 * SH, 0:P], pair[:, t, :], hot_lo[:, t, :],
                                                start=(t == 0), stop=(t == NT - 1))
                    last.then_inc(s["lists"], 1)
                    pe.wait_ge(s["lists_out"], e + 1)
                    if later(e):
                        pe.wait_ge(s["rows_out"], e)
                    nc.tensor.matmul(b_i[:, 0:2 * SH], lists[:, :], cst[0:2 * SH, C_ROW:C_ROW + 2 * SH],
                                     start=True, stop=True).then_inc(s["rows"], 1)
                compact(0)
                with pe.Fori(1, E) as e:
                    compact(e)
        m.clear()


def experts_phase(nc, a, out, g):
    with ExitStack() as ctx:
        m = Mem(nc, ctx)
        w1 = m.sb("e_w1", [P, DC, MLP])
        w2 = m.sb("e_w2", [P, MC, D])
        b1 = m.sb("e_b1", [P, E, MC])
        b2 = m.sb("e_b2", [P, E, D])
        lnw = m.sb("e_lnw", [P, DC, 2])
        b1e = m.sb("e_b1e", [P, MC])
        rows_g = m.sb("e_rows_g", [P, 2 * SH], U32)
        rows_s = m.sb("e_rows_s", [P, SH], U32)
        xg = [m.sb(f"e_xg{h}", [P, GT, D]) for h in range(2)]
        pg = [m.sb(f"e_pg{h}", [P, GT, E]) for h in range(2)]
        wt = [m.sb(f"e_wt{h}", [P, GT]) for h in range(2)]
        xhat = m.sb("e_xhat", [P, GT, D])
        st = m.sb("e_st", [P, GT, 6])
        mv = m.sb("e_mv", [P, GT, 2])
        veps = m.sb("e_veps", [P, GT])
        rstd = m.sb("e_rstd", [P, GT])
        hT = m.sb("e_hT", [P, DC, GTOK])
        uT = m.sb("e_uT", [P, MC, GTOK])
        tmp = m.sb("e_tmp", [P, D])
        ys = [m.sb(f"e_ys{h}", [P, GT, D]) for h in range(2)]
        b_u = [m.ps(f"e_bu{j}", GTOK) for j in range(4)]
        b_x = [m.ps(f"e_bx{j}", GTOK) for j in range(DC)]
        b_y = [m.ps(f"e_by{j}", GTOK) for j in range(2)]
        names = ("w1 w2 small rows_g rows_s held gather0 gather1 b1e wt dve_held stats aggr eps rstd xhat xT hT u gelu "
                 "y y1 ys added").split()
        s = {n: m.sem("e_" + n) for n in names}
        ident = g.cst[:, C_ID:C_ID + P]
        HALF = 2

        with nc.Block() as block:
            @block.sync
            def _(sp):
                sp.dma_start(b1[:, :, :], a["b1s"]).then_inc(s["small"], 16)
                sp.dma_start(lnw[:, :, :], a["mlp_ln"]).then_inc(s["small"], 16)
                sp.dma_start(b2[:, :, :], a["b2s"].to_broadcast([P, E, D])).then_inc(s["small"], 16)

                def load(e):
                    if later(e):
                        sp.wait_ge(s["u"], HALF * MC * e)
                    sp.dma_start(w1[:, :, :], a["fc1s"][e]).then_inc(s["w1"], 16)
                    if later(e):
                        sp.wait_ge(s["y"], HALF * GT * e)
                    sp.dma_start(w2[:, :, :], a["fc2s"][e]).then_inc(s["w2"], 16)
                load(0)
                with sp.Fori(1, E) as e:
                    load(e)

            @block.scalar
            def _(act):
                def step(e, has):
                    for h in range(HALF):
                        i = HALF * e + h
                        if has(0):
                            for n in range(MC):
                                act.wait_ge(s["u"], MC * i + n + 1)
                                if h == 0 and n == 0:
                                    act.wait_ge(s["b1e"], e + 1)
                                if n == 0 and (h or later(e)):
                                    act.wait_ge(s["y"], GT * i)
                                nc.scalar.activation(uT[:, n, :], b_u[n % 4][:, :], ACT.Gelu_apprx_tanh,
                                                     bias=b1e[:, n:n + 1]).then_inc(s["gelu"], 1)
                pipeline(act, step, E, 1, 1)

            @block.gpsimd
            def _(pool):
                def step(e, has):
                    for h in range(HALF):
                        i = HALF * e + h
                        if has(1):
                            if h == 0:
                                pool.wait_ge(s["rows_g"], e + 2)
                            if later(e + 1):
                                pool.wait_ge(s["xhat"], GT * (i + 1))
                            pool.sem_inc(s["held"], 1)
                            for k in range(GT):
                                c = h * GT + k
                                nc.gpsimd.indirect_dma_start(
                                    xg[h][:, k, :], None, g.tok_dram.rearrange("t p d -> (t p) d"),
                                    bass.IndirectOffsetOnAxis(rows_g[:, c:c + 1], 0)).then_inc(s[f"gather{h}"], 16)
                                nc.gpsimd.indirect_dma_start(
                                    pg[h][:, k, :], None, g.prob_dram.rearrange("p t e -> (p t) e"),
                                    bass.IndirectOffsetOnAxis(rows_g[:, SH + c:SH + c + 1], 0))\
                                    .then_inc(s[f"gather{h}"], 16)
                            pool.wait_ge(s["eps"], i + 3)
                            nc.gpsimd.tensor_tensor(rstd[:, :], veps[:, :], g.mhalf[:, 0:GT], ALU.pow)\
                                .then_inc(s["rstd"], 1)
                        if has(0):
                            for k in range(GT):
                                c = h * GT + k
                                pool.wait_ge(s["ys"], GT * i + k + 1)
                                if h or k or later(e):
                                    pool.wait_ge(s["added"], 16 * (GT * i + k))
                                pool.sem_inc(s["held"], 1)
                                nc.gpsimd.indirect_dma_start(
                                    out.rearrange("t p d -> (t p) d"),
                                    bass.IndirectOffsetOnAxis(rows_s[:, c:c + 1], 0), ys[h][:, k, :], None,
                                    compute_op=ALU.add).then_inc(s["added"], 16)
                pipeline(pool, step, E, 1, 1)
                pool.wait_ge(s["added"], 16 * E * SH)

            @block.vector
            def _(dve):
                def step(e, has):
                    if has(1):
                        if later(e + 1):
                            dve.wait_ge(s["gather0"], 32 * GT * (e + 1))
                            dve.wait_ge(s["gather1"], 32 * GT * (e + 1))
                        nc.vector.tensor_scalar(rows_g[:, :], g.rows[:, bass.ds(e + 1, 1), :]
                                                .rearrange("p e r -> p (e r)"), 0.0, None, ALU.add)\
                            .then_inc(s["rows_g"], 1)
                    if has(0):
                        if later(e):
                            dve.wait_ge(s["added"], 16 * SH * e)
                            dve.wait_ge(s["gelu"], HALF * MC * e)
                        nc.vector.tensor_scalar(rows_s[:, :], g.rows[:, bass.ds(e, 1), 0:SH]
                                                .rearrange("p e r -> p (e r)"), 0.0, None, ALU.add)\
                            .then_inc(s["rows_s"], 1)
                        nc.vector.tensor_scalar(b1e[:, :], b1[:, bass.ds(e, 1), :].rearrange("p e r -> p (e r)"),
                                                0.0, None, ALU.add).then_inc(s["b1e"], 1)
                    for h in range(HALF):
                        i = HALF * e + h
                        if h == 0 and has(0) or h == 1 and has(1):
                            dve.wait_ge(s["xT"], i + 2)
                            for c in range(DC):
                                nc.vector.tensor_scalar(hT[:, c, :], b_x[c][:, :], lnw[:, c, 0:1], lnw[:, c, 1:2],
                                                        ALU.mult, ALU.add).then_inc(s["hT"], 1)
                        if has(0):
                            for k in range(GT):
                                n = GT * i + k
                                dve.wait_ge(s["y"], n + 1)
                                if k or h or later(e):
                                    dve.wait_ge(s["ys"], n)
                                if k == 0 and later(e):
                                    dve.wait_ge(s["added"], 16 * (GT * (i - 1)))
                                nc.vector.tensor_tensor(tmp[:, :], b_y[k % 2][:, 0:D],
                                                        b2[:, bass.ds(e, 1), :].rearrange("p e r -> p (e r)"),
                                                        ALU.add).then_inc(s["y1"], 1)
                                dve.wait_ge(s["y1"], n + 1)
                                if k == 0:
                                    dve.wait_ge(s["wt"], i + 1)
                                nc.vector.tensor_scalar(ys[h][:, k, :], tmp[:, :],
                                                        wt[h][:, k:k + 1], None,
                                                        ALU.mult).then_inc(s["ys"], 1)
                        if has(1):
                            dve.wait_ge(s[f"gather{h}"], 32 * GT * (e + 2))
                            for k in range(GT):
                                nc.vector.bn_stats(st[:, k, :], xg[h][:, k, :]).then_inc(s["stats"], 1)
                            if has(0):
                                dve.wait_ge(s["ys"], GT * (i + 1))
                            nc.vector.tensor_copy(wt[h][:, :].unsqueeze(2), pg[h][:, :, bass.ds(e + 1, 1)])\
                                .then_inc(s["wt"], 1)
                            dve.wait_ge(s["stats"], GT * (i + 3))
                            dve.sem_inc(s["dve_held"], 1)
                            for k in range(GT):
                                nc.vector.bn_aggr(mv[:, k, :], st[:, k, :]).then_inc(s["aggr"], 1)
                            dve.wait_ge(s["aggr"], GT * (i + 3))
                            nc.vector.tensor_scalar(veps[:, :], mv[:, :, 1], EPS1, None, ALU.add)\
                                .then_inc(s["eps"], 1)
                            dve.wait_ge(s["rstd"], i + 3)
                            if h or later(e + 1):
                                dve.wait_ge(s["xT"], i + 2)
                            for k in range(GT):
                                nc.vector.tensor_scalar(xhat[:, k, :], xg[h][:, k, :], mv[:, k, 0:1],
                                                        rstd[:, k:k + 1], ALU.subtract, ALU.mult)\
                                    .then_inc(s["xhat"], 1)
                dve.wait_ge(s["small"], 48)
                pipeline(dve, step, E, 1, 1)

            @block.tensor
            def _(pe):
                def step(e, has):
                    for h in range(HALF):
                        i = HALF * e + h
                        if has(0):
                            pe.wait_ge(s["hT"], DC * (i + 1))
                            if h == 0:
                                pe.wait_ge(s["w1"], 16 * (e + 1))
                            for n in range(MC):
                                if n >= 4 or h or later(e):
                                    pe.wait_ge(s["gelu"], MC * i + n - 3)
                                for kc in range(DC):
                                    last = nc.tensor.matmul(b_u[n % 4][:, :], w1[:, kc, n * P:(n + 1) * P],
                                                            hT[:, kc, :], start=(kc == 0), stop=(kc == DC - 1))
                                last.then_inc(s["u"], 1)
                        if h == 0 and has(0) or h == 1 and has(1):
                            pe.wait_ge(s["xhat"], GT * (i + 2))
                            if h == 0 or later(e + 1):
                                pe.wait_ge(s["hT"], DC * (i + 1))
                            for c in range(DC):
                                for k in range(GT):
                                    last = nc.tensor.transpose(b_x[c][:, k * P:(k + 1) * P],
                                                               xhat[:, k, c * P:(c + 1) * P], ident)
                            last.then_inc(s["xT"], 1)
                        if has(0):
                            if h == 0:
                                pe.wait_ge(s["w2"], 16 * (e + 1))
                            pe.wait_ge(s["gelu"], MC * (i + 1))
                            for k in range(GT):
                                n = GT * i + k
                                if k >= 2 or h or later(e):
                                    pe.wait_ge(s["y1"], n - 1)
                                for kc in range(MC):
                                    last = nc.tensor.matmul(b_y[k % 2][:, 0:D], uT[:, kc, k * P:(k + 1) * P],
                                                            w2[:, kc, :], start=(kc == 0), stop=(kc == MC - 1))
                                last.then_inc(s["y"], 1)
                pipeline(pe, step, E, 1, 1)
        m.clear()


class Kept:
    pass


def program(nc, a, out, phases=9):
    with ExitStack() as ctx:
        m = Mem(nc, ctx)
        g = Kept()
        g.cst = m.sb("consts_sb", [P, C_ALL])[:, :]
        g.mhalf = m.sb("minus_half", [P, 32])
        g.X = m.sb("X", [P, NT, D])
        g.PT = m.sb("PT", [P, H, P])
        g.sh_1 = m.sb("shift_1", [P, DC, B])
        g.ln1g = m.sb("ln1g", [P, DC])[:, :]
        g.lg = m.sb("expert_scores", [P, E, NT])
        g.loaded, g.loaded1, g.centred = m.sem("loaded"), m.sem("loaded1"), m.sem("centred")
        g.rows = m.sb("rows", [P, E, 2 * SH], U32)
        g.prob_dram = nc.dram_tensor("probs", [P, NT, E], F32, kind="Internal").ap()
        g.thr_dram = nc.dram_tensor("thresholds", [1, P], F32, kind="Internal").ap()
        g.tok_dram = nc.dram_tensor("tokens", [NT, P, D], F32, kind="Internal").ap()
        g.gate_dram = nc.dram_tensor("gates_of_rows", [B, 2 * D], F32, kind="Internal").ap()
        with ExitStack() as ctx0:
            m0 = Mem(nc, ctx0)
            g.sh_m, g.sc_m = (m0.sb(n, [P, DC, B]) for n in ("shift_mlp", "scale_mlp"))
            with ExitStack() as ctx1:
                m1 = Mem(nc, ctx1)
                g.sh_a, g.sc_a = (m1.sb(n, [P, DC, B]) for n in ("shift_msa", "scale_msa"))
                g.wqkv0 = m1.sb("wqkv0", [P, DC, 3 * D])[:, :, :]
                g.wproj0 = m1.sb("wproj0", [P, DC, D])[:, :, :]
                g.qkb0 = m1.sb("qkb0", [P, 2 * DC])[:, :]
                g.vb0 = m1.sb("vb0", [P, D])[:, :]
                g.pb0 = m1.sb("pb0", [P, D])[:, :]
                g.mrow = m1.sb("mrow", [P, NT])[:, :]
                g.hidden = m1.sb("hidden", [P, NT, S])[:, :, :]
                g.vm = m1.sb("vm", [P, 2, H // 2, 2 * HD0])
                setup_phase(nc, a, g)
                if phases >= 1:
                    attention0_phase(nc, a, g)
            g.wqkv1 = m0.sb("wqkv1", [P, DC, 3 * V1])[:, :, :]
            g.wout1 = m0.sb("wout1", [P, H // 2, D])[:, :, :]
            g.wgate = m0.sb("wgate", [P, DC, E])[:, :, :]
            g.qn, g.kn = (m0.sb(n, [P, 2])[:, :] for n in ("qn", "kn"))
            if phases >= 2:
                mlp0_phase(nc, a, g)
            if phases >= 3:
                attention1_phase(nc, a, out, g)
        if phases >= 4:
            route_phase(nc, a, g)
        if phases >= 5:
            experts_phase(nc, a, out, g)


def feature_major(v):
    return np.ascontiguousarray(v.reshape(-1, P).T)


def weight(w):
    return np.ascontiguousarray(w.T.reshape(-1, P, w.shape[0]).transpose(1, 0, 2))


def layouts(x, cond_1024, mask_BxS_bk1, **w):
    n = {k: np.asarray(v) for k, v in w.items()}
    L0, L1 = "L0_cond_", "L1_cond_"
    mask = np.asarray(mask_BxS_bk1)
    ada_b = n[L0 + "ada_b"].reshape(6, DC, P)
    return {
        "x": np.asarray(x).reshape(NT, P, D),
        "condT": weight(np.asarray(cond_1024)),
        "mask": mask,
        "maskT": np.ascontiguousarray(mask.reshape(NT, P).T),
        "consts": constants(),
        "ada_w": weight(n[L0 + "ada_w"]),
        "ada_b": np.ascontiguousarray(ada_b[[0, 1, 3, 4]].reshape(4 * DC, P).T),
        "ada_row": n[L0 + "ada_b"].reshape(1, -1),
        "ada1_w": weight(n[L1 + "W_ada"]),
        "ada1_b": feature_major(n[L1 + "b_ada"]),
        "ln1_b": feature_major(n[L1 + "ln1_b"]),
        "ln1_g": feature_major(n[L1 + "ln1_g"]),
        "qkv0_w": weight(n[L0 + "qkv_w"]),
        "qkv0_row": n[L0 + "qkv_b"].reshape(1, -1),
        "qk0_b": feature_major(n[L0 + "qkv_b"][:2 * D]),
        "proj0_w": weight(n[L0 + "proj_w"]),
        "fc1_0_w": weight(n[L0 + "fc1_w"]),
        "fc1_0_b": feature_major(n[L0 + "fc1_b"]),
        "fc2_0_w": weight(n[L0 + "fc2_w"]),
        "fc2_0_row": n[L0 + "fc2_b"].reshape(1, -1),
        "qkv1_w": weight(n[L1 + "Wqkv"]),
        "out1_w": weight(n[L1 + "Wout"]),
        "gate_w": weight(n[L1 + "Wgate"]),
        "qn": np.stack([np.tile(n[L1 + "qn_g"], 2), np.tile(n[L1 + "qn_b"], 2)], 1),
        "kn": np.stack([np.tile(n[L1 + "kn_g"], 2), np.tile(n[L1 + "kn_b"], 2)], 1),
        "fc1s": np.stack([weight(w1) for w1 in n[L1 + "fc1s"]]),
        "fc2s": np.stack([weight(w2) for w2 in n[L1 + "fc2s"]]),
        "b1s": np.ascontiguousarray(n[L1 + "b1s"].reshape(E, MC, P).transpose(2, 0, 1)),
        "b2s": n[L1 + "b2s"].reshape(1, E, D),
        "mlp_ln": np.stack([feature_major(n[L1 + "mlp_g"]), feature_major(n[L1 + "mlp_b"])], 2),
        "proj0_row": n[L0 + "proj_b"].reshape(1, -1),
    }


def kernel(**inputs):
    import concourse.bacc as bacc
    from concourse.bass_utils import run_bass_kernel_spmd

    nc = bacc.Bacc("TRN2", target_bir_lowering=False, num_devices=1)
    arrays = {"in_" + n: v for n, v in layouts(**inputs).items()}
    a = {n[3:]: nc.dram_tensor(n, v.shape, mybir.dt.from_np(v.dtype), kind="ExternalInput").ap()
         for n, v in arrays.items()}
    out = nc.dram_tensor("out", [NT, P, D], F32, kind="ExternalOutput").ap()
    program(nc, a, out)
    r = run_bass_kernel_spmd(nc, [arrays], core_ids=[0])
    return r.results[0]["out"].reshape(B, S, D)
```

```python
import numpy as np
import concourse.bass as bass
from concourse import mybir
from contextlib import ExitStack

F32 = mybir.dt.float32
BF16 = mybir.dt.bfloat16
I32 = mybir.dt.int32
U32 = mybir.dt.uint32
U8 = mybir.dt.uint8
ALU = mybir.AluOpType
ACT = mybir.ActivationFunctionType
AX = mybir.AxisListType.X

P = 128
B, S, D = 128, 64, 256
TOK = B * S
NT = TOK // P
DC = D // P
H = 16
HD0 = D // H
HD1 = 64
QK1 = 2 * H * HD1
V1 = H * HD1
MLP = 4 * D
MC = MLP // P
GT = 4
GTOK = GT * P
NG = NT // GT
E = 8
CAP = TOK // E
SH = CAP // P
EPS0, EPS1 = 1e-6, 1e-5
SCALE0, SCALE1 = HD0 ** -0.5, HD1 ** -0.5
HIDE = -1e30
NOSLOT = 4096.0

C_ID, C_UP, C_SAME, C_IOTA = 0, P, 2 * P, 3 * P
C_HEAD = 4 * P
C_PICK = C_HEAD + 8
C_P = C_PICK + 8
C_ROW = C_P + 1
C_GROW = C_ROW + 8
C_BITS = C_GROW + 8
BITS = 30
C_ALL = C_BITS + BITS + 1


def constants():
    c = np.zeros((P, C_ALL), np.float32)
    p = np.arange(P)
    c[:, C_ID:C_ID + P] = np.eye(P)
    c[:, C_UP:C_UP + P] = p[:, None] < p[None, :]
    c[:, C_SAME:C_SAME + P] = p[:, None] // 16 == p[None, :] // 16
    c[:, C_IOTA:C_IOTA + P] = p[None, :]
    c[:, C_HEAD:C_HEAD + 8] = p[:, None] // 16 == np.arange(8)[None, :]
    c[:, C_PICK:C_PICK + 8] = p[:, None] == 16 * np.arange(8)[None, :]
    c[:, C_P] = p
    for j in range(8):
        c[j, C_ROW + j], c[8 + j, C_ROW + j] = P, 1
        c[j, C_GROW + j], c[8 + j, C_GROW + j] = 1, NT
    c[:, C_BITS:C_BITS + BITS] = 2.0 ** np.arange(BITS - 1, -1, -1)
    return c


def pipeline(eng, step, n, before, after):
    def edge(i):
        step(i, lambda k: 0 <= i + k < n)
    for i in range(-before, after):
        edge(i)
    with eng.Fori(after, n - before) as i:
        step(i, lambda k: True)
    for i in range(n - before, n + after):
        edge(i)


def pipeline_by_2(eng, step, n, before, after):
    def edge(i):
        step(i, lambda k: 0 <= i + k < n, i % 2)
    first = after + after % 2
    last = n - before - (n - before - first) % 2
    for i in range(-before, first):
        edge(i)
    with eng.Fori(0, (last - first) // 2) as pair:
        for par in range(2):
            step(2 * pair + first + par, lambda k: True, par)
    for i in range(last, n + after):
        edge(i)


def later(t):
    return not isinstance(t, int) or t > 0


def block_of(PT, b_pt, half, b, e):
    to = PT[b * S:(b + 1) * S, half * 8:half * 8 + 8, b * S:(b + 1) * S]
    src = b_pt[e * S:(e + 1) * S, half * 4 * P:(half + 1) * 4 * P].rearrange("p (j q) -> p j q", q=P)
    return to.rearrange("p (j e) q -> p e j q", e=2)[:, e], src[:, :, b * S:(b + 1) * S]


def blocks_of(PT, b_pt, b, e):
    to = PT[b * S:(b + 1) * S, :, b * S:(b + 1) * S]
    src = b_pt[e * S:(e + 1) * S, :].rearrange("p (j q) -> p j q", q=P)
    return to.rearrange("p (j e) q -> p e j q", e=2)[:, e], src[:, :, b * S:(b + 1) * S]


class Mem:

    def __init__(self, nc, ctx):
        self.nc, self.ctx, self.sems = nc, ctx, []

    def sb(self, name, shape, dt=F32):
        return self.ctx.enter_context(self.nc.sbuf_tensor(name, shape, dt))

    def ps(self, name, cols):
        return self.ctx.enter_context(self.nc.psum_tensor(name, [P, cols], F32))

    def sem(self, name):
        self.sems.append(self.nc.alloc_semaphore(name))
        return self.sems[-1]

    def clear(self):
        self.nc.all_engine_barrier()
        self.nc.clear_and_free_semaphores(self.sems)
        self.nc.all_engine_barrier()


def setup_phase(nc, a, g):
    with ExitStack() as ctx:
        m = Mem(nc, ctx)
        wada = m.sb("wada", [P, DC, 6 * D])
        wada1 = m.sb("wada1", [P, DC, D])
        cT = m.sb("cT", [P, DC, B])
        sT = m.sb("sT", [P, DC, B])
        adab = m.sb("adab", [P, 4 * DC])
        bada1 = m.sb("bada1", [P, DC])
        ln1b = m.sb("ln1b", [P, DC])
        gbias = m.sb("gbias", [P, 2 * D])
        gates = m.sb("gates", [P, 2 * D])
        mask_keys = m.sb("mask_keys", [P, NT, S], U8)
        mask_rows = m.sb("mask_rows", [P, NT], U8)
        keysf = m.sb("keysf", [P, NT, S])
        hide = m.sb("hide", [P, NT])
        shb = m.sb("shb", [P, DC])
        pt = [m.ps(f"pmod{j}", 4 * P) for j in range(2)]
        pg = [m.ps(f"pgate{j}", 4 * P) for j in range(2)]
        loaded_c, loaded_w, loaded_b, loaded_m = (m.sem(n) for n in
                                                  ("loaded_c", "loaded_w", "loaded_b", "loaded_m"))
        silu_done, table_mm, table_out = m.sem("silu_done"), m.sem("table_mm"), m.sem("table_out")
        gate_mm, gate_out, gate_saved = m.sem("gate_mm"), m.sem("gate_out"), m.sem("gate_saved")
        keys_f, hide_done, hidden_done = m.sem("keys_f"), m.sem("hide_done"), m.sem("hidden_done")
        cleared, shift_bias = m.sem("cleared"), m.sem("shift_bias")
        parts = [(g.sh_a, 0, 0), (g.sc_a, 1, 0), (g.sh_m, 3, 1), (g.sc_m, 4, 1)]
        jobs = [(tab, k, c, n) for n, (tab, k, _) in enumerate(parts) for c in range(DC)]
        jobs += [(g.sh_1, None, c, 4) for c in range(DC)]
        with nc.Block() as block:
            @block.sync
            def _(sp):
                sp.dma_start(cT[:, :, :], a["condT"]).then_inc(loaded_c, 16)
                for s in range(2):
                    sp.dma_start(mask_keys[s * S:(s + 1) * S, :, :],
                                 a["mask"].rearrange("(t s) k -> s t k", s=2)[s:s + 1]
                                 .to_broadcast([S, NT, S])).then_inc(loaded_m, 16)
                sp.dma_start(mask_rows[:, :], a["maskT"]).then_inc(loaded_m, 16)
                sp.dma_start(wada[:, :, :], a["ada_w"]).then_inc(loaded_w, 16)
                sp.dma_start(wada1[:, :, :], a["ada1_w"]).then_inc(loaded_w, 16)
                sp.dma_start(adab[:, :], a["ada_b"]).then_inc(loaded_b, 16)
                sp.dma_start(bada1[:, :], a["ada1_b"]).then_inc(loaded_b, 16)
                sp.dma_start(ln1b[:, :], a["ln1_b"]).then_inc(loaded_b, 16)
                for j, k in enumerate((2, 5)):
                    sp.dma_start(gbias[:, j * D:(j + 1) * D],
                                 a["ada_row"][:, k * D:(k + 1) * D].to_broadcast([P, D])).then_inc(loaded_b, 16)
                for w, n in ((g.wqkv0, "qkv0_w"), (g.wproj0, "proj0_w"), (g.qkb0, "qk0_b"), (g.ln1g, "ln1_g")):
                    sp.dma_start(w, a[n]).then_inc(g.loaded, 16)
                sp.dma_start(g.vb0, a["qkv0_row"][:, 2 * D:].to_broadcast([P, D])).then_inc(g.loaded, 16)
                sp.dma_start(g.pb0, a["proj0_row"].to_broadcast([P, D])).then_inc(g.loaded, 16)
                sp.dma_start(g.cst, a["consts"]).then_inc(g.loaded, 16)
                sp.wait_ge(g.loaded, 16 * 7)
                sp.wait_ge(gate_out, 2)
                sp.dma_start(g.gate_dram, gates[:, :]).then_inc(gate_saved, 16)
                sp.wait_ge(gate_saved, 16)

            @block.gpsimd
            def _(pool):
                nc.gpsimd.memset(g.PT[:, :, :], 0.0).then_inc(cleared, 1)
                nc.gpsimd.memset(g.vm[:, :, :, :], 0.0).then_inc(cleared, 1)
                nc.gpsimd.memset(g.mhalf[:, :], -0.5).then_inc(cleared, 1)

            @block.scalar
            def _(act):
                act.wait_ge(loaded_c, 16)
                nc.scalar.activation(sT[:, :, :], cT[:, :, :], ACT.Silu).then_inc(silu_done, 1)

            @block.tensor
            def _(pe):
                pe.wait_ge(silu_done, 1)
                pe.wait_ge(loaded_w, 32)
                for n, (tab, k, c, _) in enumerate(jobs):
                    if n >= 2:
                        pe.wait_ge(table_out, n - 1)
                    for kc in range(DC):
                        w = wada1[:, kc, c * P:(c + 1) * P] if k is None else \
                            wada[:, kc, k * D + c * P:k * D + (c + 1) * P]
                        last = nc.tensor.matmul(pt[n % 2][:, 0:P], w, sT[:, kc, :],
                                                start=(kc == 0), stop=(kc == DC - 1))
                    last.then_inc(table_mm, 1)
                for j, k in enumerate((2, 5)):
                    for kc in range(DC):
                        last = nc.tensor.matmul(pg[j][:, 0:D], sT[:, kc, :],
                                                wada[:, kc, k * D:(k + 1) * D],
                                                start=(kc == 0), stop=(kc == DC - 1))
                    last.then_inc(gate_mm, 1)

            @block.vector
            def _(dve):
                dve.wait_ge(loaded_m, 48)
                nc.vector.tensor_scalar(keysf[:, :, :], mask_keys[:, :, :], -1.0, None, ALU.add).then_inc(keys_f, 1)
                nc.vector.tensor_scalar(g.mrow, mask_rows[:, :], 1.0, None, ALU.mult).then_inc(keys_f, 1)
                nc.vector.tensor_scalar(hide[:, :], mask_rows[:, :], -HIDE, None, ALU.mult).then_inc(keys_f, 1)
                dve.wait_ge(keys_f, 3)
                nc.vector.tensor_tensor(g.hidden, keysf[:, :, :],
                                        hide[:, :].unsqueeze(2).to_broadcast([P, NT, S]), ALU.mult)\
                    .then_inc(hidden_done, 1)
                dve.wait_ge(loaded_b, 16 * 5)
                nc.vector.tensor_tensor(shb[:, :], bada1[:, :], ln1b[:, :], ALU.add).then_inc(shift_bias, 1)
                dve.wait_ge(shift_bias, 1)
                for n, (tab, k, c, q) in enumerate(jobs):
                    dve.wait_ge(table_mm, n + 1)
                    if k is None:
                        ins = nc.vector.tensor_scalar(tab[:, c, :], pt[n % 2][:, 0:P], shb[:, c:c + 1], None, ALU.add)
                    else:
                        ins = nc.vector.tensor_scalar(tab[:, c, :], pt[n % 2][:, 0:P],
                                                      adab[:, 2 * q + c:2 * q + c + 1],
                                                      float(q % 2), ALU.add, ALU.add)
                    ins.then_inc(table_out, 1)
                for j in range(2):
                    dve.wait_ge(gate_mm, j + 1)
                    nc.vector.tensor_tensor(gates[:, j * D:(j + 1) * D], pg[j][:, 0:D],
                                            gbias[:, j * D:(j + 1) * D], ALU.add).then_inc(gate_out, 1)
        m.clear()


def attention0_phase(nc, a, g):
    with ExitStack() as ctx:
        m = Mem(nc, ctx)
        xhat = m.sb("a0_xhat", [P, D])
        st = m.sb("a0_st", [P, 6])
        mv = m.sb("a0_mv", [P, 2])
        veps = m.sb("a0_veps", [P, 1])
        rstd = m.sb("a0_rstd", [P, 1])
        hT = m.sb("a0_hT", [P, DC, P])
        hm = m.sb("a0_hm", [P, DC, P])
        qT = m.sb("a0_qT", [P, DC, P])
        kT = m.sb("a0_kT", [P, DC, P])
        kbd = m.sb("a0_kbd", [P, DC, 2, 8, S])
        vall = m.sb("a0_v", [P, NT, D])
        pr = m.sb("a0_p", [P, 2, H, S])
        mx = m.sb("a0_mx", [P, H])
        sm = m.sb("a0_sm", [P, H])
        rs = m.sb("a0_rs", [P, H])
        oT = m.sb("a0_oT", [P, DC, P])
        gt = m.sb("a0_gate", [P, D])
        tmp = m.sb("a0_tmp", [P, D])
        tmp2 = m.sb("a0_tmp2", [P, D])
        b_qk, b_vt = m.ps("a0_bqk", 4 * P), m.ps("a0_bvt", 4 * P)
        b_s, b_pt = m.ps("a0_bs", H * S), m.ps("a0_bpt", H * S)
        b_o, b_pj = m.ps("a0_bo", 4 * P), m.ps("a0_bpj", 4 * P)
        names = ("x_in stats aggr eps rstd xhat xT h_mul hT qk v q_out k_out kbd v_out vm s scored maxed "
                 "shifted exped summed recip probs pT pT_out o oT proj p1 p2 res gate").split()
        s = {n: m.sem("a0_" + n) for n in names}
        ident = g.cst[:, C_ID:C_ID + P]
        PT = g.PT

        with nc.Block() as block:
            @block.sync
            def _(sp):
                AHEAD = 8

                def load_x(t):
                    if later(t):
                        sp.wait_ge(s["x_in"], 16 * t)
                    sp.dma_start(g.X[:, t, :], a["x"][t]).then_inc(s["x_in"], 16)

                def load_gates(t):
                    if later(t):
                        sp.wait_ge(s["p2"], t)
                    for b in range(2):
                        sp.dma_start(gt[b * S:(b + 1) * S, :],
                                     g.gate_dram[bass.ds(2 * t + b, 1), 0:D].to_broadcast([S, D]))\
                            .then_inc(s["gate"], 16)
                for t in range(AHEAD):
                    load_x(t)
                load_gates(0)
                sp.dma_start(g.w1_0, a["fc1_0_w"]).then_inc(g.loaded_w1, 16)
                with sp.Fori(1, NT - AHEAD + 1) as t:
                    load_x(t + AHEAD - 1)
                    load_gates(t)
                with sp.Fori(NT - AHEAD + 1, NT) as t:
                    load_gates(t)

            @block.scalar
            def _(act):
                def step(i, has, par):
                    if has(-3):
                        act.wait_ge(s["pT"], i - 2)
                        if later(i - 3):
                            act.wait_ge(s["o"], i - 3)
                        for b in range(2):
                            for e in range(2):
                                last = nc.scalar.copy(*blocks_of(PT, b_pt, b, e))
                        last.then_inc(s["pT_out"], 1)
                    if has(0):
                        act.wait_ge(s["qk"], i + 1)
                        if later(i):
                            act.wait_ge(s["kbd"], i)
                        for c in range(DC):
                            last = nc.scalar.activation(kT[:, c, :], b_qk[:, (DC + c) * P:(DC + c + 1) * P],
                                                        ACT.Identity, bias=g.qkb0[:, DC + c:DC + c + 1])
                        last.then_inc(s["k_out"], 1)
                        if later(i):
                            act.wait_ge(s["s"], i)
                        for c in range(DC):
                            last = nc.scalar.activation(qT[:, c, :], b_qk[:, c * P:(c + 1) * P], ACT.Identity,
                                                        bias=g.qkb0[:, c:c + 1])
                        last.then_inc(s["q_out"], 1)
                        act.wait_ge(s["v"], i + 1)
                        nc.scalar.copy(vall[:, i, :], b_vt[:, 0:D]).then_inc(s["v_out"], 1)
                    if has(-3):
                        act.wait_ge(s["o"], i - 2)
                        if later(i - 3):
                            act.wait_ge(s["proj"], i - 3)
                        nc.scalar.copy(oT[:, :, :], b_o[:, 0:DC * P].rearrange("p (c t) -> p c t", c=DC))\
                            .then_inc(s["oT"], 1)
                    if has(-1):
                        act.wait_ge(s["shifted"], i)
                        nc.scalar.activation(pr[:, 1 - par, :, :], pr[:, 1 - par, :, :], ACT.Exp, scale=SCALE0)\
                            .then_inc(s["exped"], 1)
                pipeline_by_2(act, step, NT, 0, 5)

            @block.gpsimd
            def _(pool):
                def step(i, has, par):
                    if has(2):
                        pool.wait_ge(s["eps"], i + 3)
                        nc.gpsimd.tensor_tensor(rstd[:, :], veps[:, :], g.mhalf[:, 0:1], ALU.pow)\
                            .then_inc(s["rstd"], 1)
                    if has(-4):
                        pool.wait_ge(s["p1"], i - 3)
                        pool.wait_ge(s["gate"], 32 * (i - 3))
                        if later(i - 4):
                            pool.wait_ge(s["res"], i - 4)
                        nc.gpsimd.tensor_tensor(tmp2[:, :], tmp[:, :], gt[:, :], ALU.mult).then_inc(s["p2"], 1)
                        pool.wait_ge(s["p2"], i - 3)
                        nc.gpsimd.tensor_tensor(g.X[:, i - 4, :], g.X[:, i - 4, :], tmp2[:, :], ALU.add)\
                            .then_inc(s["res"], 1)
                    if has(0):
                        pool.wait_ge(s["k_out"], i + 1)
                        if later(i):
                            pool.wait_ge(s["s"], i)
                        for c in range(DC):
                            last = nc.gpsimd.tensor_tensor(
                                kbd[:, c, :, :, :],
                                kT[:, c, :].rearrange("p (b k) -> p b k", b=2).unsqueeze(2).to_broadcast([P, 2, 8, S]),
                                g.cst[:, C_HEAD:C_HEAD + 8].unsqueeze(1).unsqueeze(3).to_broadcast([P, 2, 8, S]),
                                ALU.mult)
                        last.then_inc(s["kbd"], 1)
                    if has(-2):
                        pool.wait_ge(s["v_out"], i - 1)
                        if later(i - 2):
                            pool.wait_ge(s["o"], i - 2)
                        for e in range(2):
                            last = nc.gpsimd.tensor_tensor(
                                g.vm[:, e, :, e * HD0:(e + 1) * HD0],
                                vall[:, i - 2, :].rearrange("p (j e d) -> p e j d", e=2, d=HD0)[:, e],
                                g.vb0.rearrange("p (j e d) -> p e j d", e=2, d=HD0)[:, e], ALU.add)
                        last.then_inc(s["vm"], 1)
                pipeline_by_2(pool, step, NT, 2, 5)

            @block.vector
            def _(dve):
                def step(i, has, par):
                    pa, pb = pr[:, 1 - par, :, :], pr[:, par, :, :]
                    if has(2):
                        dve.wait_ge(s["x_in"], 16 * (i + 3))
                        nc.vector.bn_stats(st[:, :], g.X[:, i + 2, :]).then_inc(s["stats"], 1)
                        if later(i + 2):
                            dve.wait_ge(s["xhat"], i + 2)
                        dve.wait_ge(s["stats"], i + 3)
                    if has(-4):
                        dve.wait_ge(s["proj"], i - 3)
                        if later(i - 4):
                            dve.wait_ge(s["p2"], i - 4)
                        nc.vector.tensor_tensor(tmp[:, :], b_pj[:, 0:D], g.pb0, ALU.add).then_inc(s["p1"], 1)
                    if has(2):
                        nc.vector.bn_aggr(mv[:, :], st[:, :]).then_inc(s["aggr"], 1)
                        dve.wait_ge(s["aggr"], i + 3)
                        nc.vector.tensor_scalar(veps[:, :], mv[:, 1:2], EPS0, None, ALU.add).then_inc(s["eps"], 1)
                    if has(-2):
                        dve.wait_ge(s["exped"], i - 1)
                        nc.vector.reduce_sum(sm[:, :], pb, AX).then_inc(s["summed"], 1)
                        dve.wait_ge(s["summed"], i - 1)
                        nc.vector.reciprocal(rs[:, :], sm[:, :]).then_inc(s["recip"], 1)
                    if has(-1):
                        dve.wait_ge(s["s"], i)
                        if later(i - 1) and has(-3):
                            dve.wait_ge(s["pT"], i - 2)
                        nc.vector.scalar_tensor_tensor(
                            pa, b_s[:, :].rearrange("p (h k) -> p h k", h=H), g.mrow[:, bass.ds(i - 1, 1)],
                            g.hidden[:, i - 1, :].unsqueeze(1).to_broadcast([P, H, S]),
                            ALU.mult, ALU.add).then_inc(s["scored"], 1)
                    if has(-2):
                        dve.wait_ge(s["recip"], i - 1)
                        nc.vector.tensor_tensor(pb, pb, rs[:, :].unsqueeze(2).to_broadcast([P, H, S]), ALU.mult)\
                            .then_inc(s["probs"], 1)
                    if has(-1):
                        dve.wait_ge(s["scored"], i)
                        nc.vector.reduce_max(mx[:, :], pa, AX).then_inc(s["maxed"], 1)
                        dve.wait_ge(s["maxed"], i)
                        nc.vector.tensor_tensor(pa, pa, mx[:, :].unsqueeze(2).to_broadcast([P, H, S]),
                                                ALU.subtract).then_inc(s["shifted"], 1)
                    if has(1):
                        dve.wait_ge(s["xT"], i + 2)
                        nc.vector.tensor_tensor(
                            hm[:, :, :].rearrange("p c (b t) -> p c b t", b=2),
                            b_vt[:, D:2 * D].rearrange("p (c b t) -> p c b t", c=DC, b=2),
                            g.sc_a[:, :, bass.ds(2 * (i + 1), 2)].unsqueeze(3).to_broadcast([P, DC, 2, S]),
                            ALU.mult).then_inc(s["h_mul"], 1)
                        dve.wait_ge(s["h_mul"], i + 2)
                        nc.vector.tensor_tensor(
                            hT[:, :, :].rearrange("p c (b t) -> p c b t", b=2),
                            hm[:, :, :].rearrange("p c (b t) -> p c b t", b=2),
                            g.sh_a[:, :, bass.ds(2 * (i + 1), 2)].unsqueeze(3).to_broadcast([P, DC, 2, S]),
                            ALU.add).then_inc(s["hT"], 1)
                    if has(2):
                        dve.wait_ge(s["rstd"], i + 3)
                        if later(i + 2):
                            dve.wait_ge(s["xT"], i + 2)
                        nc.vector.tensor_scalar(xhat[:, :], g.X[:, i + 2, :], mv[:, 0:1], rstd[:, 0:1],
                                                ALU.subtract, ALU.mult).then_inc(s["xhat"], 1)
                pipeline_by_2(dve, step, NT, 2, 5)

            @block.tensor
            def _(pe):
                def step(i, has, par):
                    if has(-1):
                        pe.wait_ge(s["kbd"], i)
                        pe.wait_ge(s["q_out"], i)
                        if later(i - 1):
                            pe.wait_ge(s["scored"], i - 1)
                        for c in range(DC):
                            for b in range(2):
                                last = nc.tensor.matmul(b_s[b * S:(b + 1) * S, c * 512:(c + 1) * 512],
                                                        qT[:, c, b * S:(b + 1) * S],
                                                        kbd[:, c, b, :, :].rearrange("p h k -> p (h k)"),
                                                        start=True, stop=True)
                        last.then_inc(s["s"], 1)
                    if has(0):
                        pe.wait_ge(s["hT"], i + 1)
                        if later(i):
                            pe.wait_ge(s["q_out"], i)
                        for n in (2, 3, 0, 1):
                            for kc in range(DC):
                                last = nc.tensor.matmul(b_qk[:, n * P:(n + 1) * P],
                                                        g.wqkv0[:, kc, n * P:(n + 1) * P], hT[:, kc, :],
                                                        start=(kc == 0), stop=(kc == DC - 1))
                        last.then_inc(s["qk"], 1)
                        if later(i):
                            pe.wait_ge(s["v_out"], i)
                        for kc in range(DC):
                            last = nc.tensor.matmul(b_vt[:, 0:D], hT[:, kc, :], g.wqkv0[:, kc, 2 * D:3 * D],
                                                    start=(kc == 0), stop=(kc == DC - 1))
                        last.then_inc(s["v"], 1)
                    if has(-3):
                        pe.wait_ge(s["pT_out"], i - 2)
                        pe.wait_ge(s["vm"], i - 2)
                        if later(i - 3):
                            pe.wait_ge(s["oT"], i - 3)
                        for j in range(H // 2):
                            r, c = j % 4, j // 4
                            for e in range(2):
                                last = nc.tensor.matmul(b_o[32 * r:32 * r + 32, c * P:(c + 1) * P],
                                                        g.vm[:, e, j, :], PT[:, 2 * j + e, :],
                                                        start=(e == 0), stop=(e == 1))
                        last.then_inc(s["o"], 1)
                    if has(1):
                        pe.wait_ge(s["xhat"], i + 2)
                        if has(0):
                            pe.wait_ge(s["v_out"], i + 1)
                        for c in range(DC):
                            last = nc.tensor.transpose(b_vt[:, D + c * P:D + (c + 1) * P],
                                                       xhat[:, c * P:(c + 1) * P], ident)
                        last.then_inc(s["xT"], 1)
                    if has(-2):
                        pe.wait_ge(s["probs"], i - 1)
                        if later(i - 2):
                            pe.wait_ge(s["pT_out"], i - 2)
                        for j in range(H // 2):
                            last = nc.tensor.transpose(
                                b_pt[:, j * P:(j + 1) * P],
                                pr[:, par, 2 * j:2 * j + 2, :].rearrange("p h k -> p (h k)"), ident)
                        last.then_inc(s["pT"], 1)
                    if has(-3):
                        pe.wait_ge(s["oT"], i - 2)
                        if later(i - 3):
                            pe.wait_ge(s["p1"], i - 3)
                        for kc in range(DC):
                            last = nc.tensor.matmul(b_pj[:, 0:D], oT[:, kc, :], g.wproj0[:, kc, :],
                                                    start=(kc == 0), stop=(kc == DC - 1))
                        last.then_inc(s["proj"], 1)
                pipeline_by_2(pe, step, NT, 1, 5)
        m.clear()


def mlp0_phase(nc, a, g):
    with ExitStack() as ctx:
        m = Mem(nc, ctx)
        w1 = g.w1_0
        w2 = m.sb("m0_w2", [P, MC, D])
        b1 = m.sb("m0_b1", [P, MC])
        b2 = m.sb("m0_b2", [P, D])
        xhat = m.sb("m0_xhat", [P, GT, D])
        st = m.sb("m0_st", [P, GT, 6])
        mv = m.sb("m0_mv", [P, GT, 2])
        veps = m.sb("m0_veps", [P, GT])
        rstd = m.sb("m0_rstd", [P, GT])
        hm = m.sb("m0_hm", [P, DC, GTOK])
        hT = m.sb("m0_hT", [P, DC, GTOK])
        uT = m.sb("m0_uT", [P, MC, GTOK])
        gt = m.sb("m0_gate", [P, GT, D])
        tmp = m.sb("m0_tmp", [P, D])
        tmp2 = m.sb("m0_tmp2", [P, D])
        wsum = m.sb("wsum", [P, DC, 2 * H, HD1 // 2])
        wmean = m.sb("wmean", [P, DC, 2 * H])
        b_u = [m.ps(f"m0_bu{j}", GTOK) for j in range(4)]
        b_x = [m.ps(f"m0_bx{j}", GTOK) for j in range(DC)]
        b_y = [m.ps(f"m0_by{j}", GTOK) for j in range(2)]
        names = "w1 w2 gate stats aggr eps rstd xhat xT h_mul hT u gelu y p1 p2 res halved wmean".split()
        s = {n: m.sem("m0_" + n) for n in names}
        ident = g.cst[:, C_ID:C_ID + P]

        with nc.Block() as block:
            @block.sync
            def _(sp):
                sp.dma_start(b1[:, :], a["fc1_0_b"]).then_inc(s["w1"], 16)
                sp.dma_start(w2[:, :, :], a["fc2_0_w"]).then_inc(s["w2"], 16)
                sp.dma_start(b2[:, :], a["fc2_0_row"].to_broadcast([P, D])).then_inc(s["w2"], 16)

                def load_gates(i):
                    if later(i):
                        sp.wait_ge(s["p2"], GT * i)
                    for b in range(2):
                        rows = g.gate_dram[bass.ds(2 * GT * i, 2 * GT), D:2 * D]\
                            .rearrange("(t b) d -> b t d", b=2)
                        sp.dma_start(gt[b * S:(b + 1) * S, :, :], rows[b:b + 1].to_broadcast([S, GT, D]))\
                            .then_inc(s["gate"], 16)
                load_gates(0)
                for w, n in ((g.wqkv1, "qkv1_w"), (g.wout1, "out1_w"), (g.wgate, "gate_w"), (g.qn, "qn"), (g.kn, "kn")):
                    sp.dma_start(w, a[n]).then_inc(g.loaded1, 16)
                with sp.Fori(1, NG) as i:
                    load_gates(i)

            @block.scalar
            def _(act):
                def step(i, has):
                    if has(0):
                        for n in range(MC):
                            act.wait_ge(s["u"], MC * i + n + 1)
                            if n == 0 and later(i):
                                act.wait_ge(s["y"], GT * i)
                            nc.scalar.activation(uT[:, n, :], b_u[n % 4][:, :], ACT.Gelu_apprx_tanh,
                                                 bias=b1[:, n:n + 1]).then_inc(s["gelu"], 1)
                act.wait_ge(s["w1"], 16)
                pipeline(act, step, NG, 2, 1)

            @block.gpsimd
            def _(pool):
                def step(i, has):
                    if has(2):
                        pool.wait_ge(s["eps"], i + 3)
                        nc.gpsimd.tensor_tensor(rstd[:, :], veps[:, :], g.mhalf[:, 0:GT], ALU.pow)\
                            .then_inc(s["rstd"], 1)
                pipeline(pool, step, NG, 2, 1)
                pool.wait_ge(g.loaded1, 16 * 5)
                heads = g.wqkv1[:, :, 0:QK1].rearrange("p c (h d) -> p c h d", d=HD1)
                n = HD1 // 2
                nc.gpsimd.tensor_tensor(wsum[:, :, :, 0:n], heads[:, :, :, 0:n], heads[:, :, :, n:2 * n], ALU.add)\
                    .then_inc(s["halved"], 1)
                halvings = 1
                while n > 1:
                    n //= 2
                    pool.wait_ge(s["halved"], halvings)
                    nc.gpsimd.tensor_tensor(wsum[:, :, :, 0:n], wsum[:, :, :, 0:n], wsum[:, :, :, n:2 * n], ALU.add)\
                        .then_inc(s["halved"], 1)
                    halvings += 1
                pool.wait_ge(s["halved"], halvings)
                nc.gpsimd.tensor_scalar(wmean[:, :, :], wsum[:, :, :, 0], 1.0 / HD1, None, ALU.mult)\
                    .then_inc(s["wmean"], 1)
                pool.wait_ge(s["wmean"], 1)
                for c in range(DC):
                    last = nc.gpsimd.tensor_tensor(heads[:, c], heads[:, c],
                                                   wmean[:, c, :].unsqueeze(2).to_broadcast([P, 2 * H, HD1]),
                                                   ALU.subtract)
                last.then_inc(g.centred, 1)

            @block.vector
            def _(dve):
                def stats(i):
                    for k in range(GT):
                        nc.vector.bn_stats(st[:, k, :], g.X[:, GT * i + k, :]).then_inc(s["stats"], 1)

                def variance(i):
                    for k in range(GT):
                        nc.vector.bn_aggr(mv[:, k, :], st[:, k, :]).then_inc(s["aggr"], 1)
                    dve.wait_ge(s["aggr"], GT * (i + 1))
                    nc.vector.tensor_scalar(veps[:, :], mv[:, :, 1], EPS0, None, ALU.add).then_inc(s["eps"], 1)

                def normal(i):
                    dve.wait_ge(s["rstd"], i + 1)
                    if later(i):
                        dve.wait_ge(s["xT"], i)
                    for k in range(GT):
                        nc.vector.tensor_scalar(xhat[:, k, :], g.X[:, GT * i + k, :], mv[:, k, 0:1], rstd[:, k:k + 1],
                                                ALU.subtract, ALU.mult).then_inc(s["xhat"], 1)

                def step(i, has):
                    if has(2):
                        stats(i + 2)
                        dve.wait_ge(s["stats"], GT * (i + 3))
                    if has(1):
                        dve.wait_ge(s["xT"], i + 2)
                        for c in range(DC):
                            nc.vector.tensor_tensor(
                                hm[:, c, :].rearrange("p (b t) -> p b t", t=S),
                                b_x[c][:, :].rearrange("p (b t) -> p b t", t=S),
                                g.sc_m[:, c, bass.ds(2 * GT * (i + 1), 2 * GT)].unsqueeze(2)
                                .to_broadcast([P, 2 * GT, S]), ALU.mult).then_inc(s["h_mul"], 1)
                        for c in range(DC):
                            dve.wait_ge(s["h_mul"], DC * (i + 1) + c + 1)
                            nc.vector.tensor_tensor(
                                hT[:, c, :].rearrange("p (b t) -> p b t", t=S),
                                hm[:, c, :].rearrange("p (b t) -> p b t", t=S),
                                g.sh_m[:, c, bass.ds(2 * GT * (i + 1), 2 * GT)].unsqueeze(2)
                                .to_broadcast([P, 2 * GT, S]), ALU.add).then_inc(s["hT"], 1)
                    if has(2):
                        variance(i + 2)
                        normal(i + 2)
                    if has(0):
                        if not later(i):
                            dve.wait_ge(s["w2"], 32)
                        dve.wait_ge(s["gate"], 32 * (i + 1))
                        for k in range(GT):
                            n = GT * i + k
                            dve.wait_ge(s["y"], n + 1)
                            nc.vector.tensor_tensor(tmp[:, :], b_y[k % 2][:, 0:D], b2[:, :], ALU.add)\
                                .then_inc(s["p1"], 1)
                            dve.wait_ge(s["p1"], n + 1)
                            nc.vector.tensor_tensor(tmp2[:, :], tmp[:, :], gt[:, k, :], ALU.mult)\
                                .then_inc(s["p2"], 1)
                            dve.wait_ge(s["p2"], n + 1)
                            nc.vector.tensor_tensor(g.X[:, n, :], g.X[:, n, :], tmp2[:, :], ALU.add)\
                                .then_inc(s["res"], 1)
                pipeline(dve, step, NG, 2, 1)
                dve.wait_ge(s["res"], NT)

            @block.tensor
            def _(pe):
                def transpose_x(i):
                    pe.wait_ge(s["xhat"], GT * (i + 1))
                    if later(i):
                        pe.wait_ge(s["hT"], DC * i)
                    for c in range(DC):
                        for k in range(GT):
                            last = nc.tensor.transpose(b_x[c][:, k * P:(k + 1) * P],
                                                       xhat[:, k, c * P:(c + 1) * P], ident)
                    last.then_inc(s["xT"], 1)

                def step(i, has):
                    if has(0):
                        pe.wait_ge(s["hT"], DC * (i + 1))
                        for n in range(MC):
                            if n >= 4:
                                pe.wait_ge(s["gelu"], MC * i + n - 3)
                            elif later(i):
                                pe.wait_ge(s["gelu"], MC * i + n - 3)
                            for kc in range(DC):
                                last = nc.tensor.matmul(b_u[n % 4][:, :], w1[:, kc, n * P:(n + 1) * P],
                                                        hT[:, kc, :], start=(kc == 0), stop=(kc == DC - 1))
                            last.then_inc(s["u"], 1)
                    if has(1):
                        transpose_x(i + 1)
                    if has(0):
                        pe.wait_ge(s["gelu"], MC * (i + 1))
                        if not later(i):
                            pe.wait_ge(s["w2"], 32)
                        for k in range(GT):
                            n = GT * i + k
                            if k >= 2:
                                pe.wait_ge(s["p1"], n - 1)
                            elif later(i):
                                pe.wait_ge(s["p1"], n - 1)
                            for kc in range(MC):
                                last = nc.tensor.matmul(b_y[k % 2][:, 0:D], uT[:, kc, k * P:(k + 1) * P],
                                                        w2[:, kc, :], start=(kc == 0), stop=(kc == MC - 1))
                            last.then_inc(s["y"], 1)
                pe.wait_ge(g.loaded_w1, 16)
                pipeline(pe, step, NG, 2, 1)
        m.clear()


def attention1_phase(nc, a, out, g):
    with ExitStack() as ctx:
        m = Mem(nc, ctx)
        xhat = m.sb("a1_xhat", [P, D])
        st = m.sb("a1_st", [P, 6])
        mv = m.sb("a1_mv", [P, 2])
        veps = m.sb("a1_veps", [P, 1])
        rstd = m.sb("a1_rstd", [P, 1])
        hT = m.sb("a1_hT", [P, DC, P])
        sq = m.sb("a1_sq", [P, QK1])
        ss = m.sb("a1_ss", [P, 2 * H])
        vq = m.sb("a1_vq", [P, 2 * H])
        rq = m.sb("a1_rq", [P, 2 * H])
        qk = m.sb("a1_qk", [P, QK1])
        qT = m.sb("a1_qT", [P, H // 2, P])
        kbd = m.sb("a1_kbd", [P, H // 2, 2, 2, S])
        v = m.sb("a1_v", [P, V1])
        pr = m.sb("a1_p", [P, H, S])
        mx = m.sb("a1_mx", [P, H])
        sm = m.sb("a1_sm", [P, H])
        rs = m.sb("a1_rs", [P, H])
        oT = m.sb("a1_oT", [P, H // 2, P])
        xs = m.sb("a1_xs", [P, D])
        xsT = m.sb("a1_xsT", [P, DC, P])
        b_qk = m.ps("a1_bqk", QK1)
        b_a = m.ps("a1_ba", H * S)
        b_b = m.ps("a1_bb", H * S)
        BK = 512
        names = ("stats aggr eps rstd xhat xT hT qk sq red vq rq qkn qkT q_out kbd_lo kbd_hi v v_out s maxed "
                 "shifted exped summed recip probs pT pT_act pT_dve o oT proj res xsT xsT_out lg lg_out "
                 "stored cleared").split()
        s = {n: m.sem("a1_" + n) for n in names}
        ident = g.cst[:, C_ID:C_ID + P]
        PT = g.PT
        QG = 4

        with nc.Block() as block:
            @block.sync
            def _(sp):
                def store(t):
                    sp.wait_ge(s["res"], t + 1)
                    sp.dma_start(g.tok_dram[t], xs[:, :]).then_inc(s["stored"], 16)
                    sp.dma_start(out[t], xs[:, :]).then_inc(s["stored"], 16)
                with sp.Fori(0, NT) as t:
                    store(t)
                sp.wait_ge(s["stored"], 32 * NT)

            @block.scalar
            def _(act):
                def step(i, has):
                    if has(0):
                        for n in range(QG):
                            act.wait_ge(s["qk"], QG * i + n + 1)
                            if later(i):
                                act.wait_ge(s["red"], QG * i + n - QG + 1)
                            nc.scalar.activation(sq[:, n * BK:(n + 1) * BK], b_qk[:, n * BK:(n + 1) * BK],
                                                 ACT.Square).then_inc(s["sq"], 1)
                            if n == 0 and has(-1):
                                act.wait_ge(s["shifted"], i)
                                nc.scalar.activation(pr[:, :, :], pr[:, :, :], ACT.Exp, scale=SCALE1)\
                                    .then_inc(s["exped"], 1)
                            if n == 2 and has(-2):
                                act.wait_ge(s["lg"], i - 1)
                                nc.scalar.copy(g.lg[:, :, bass.ds(i - 2, 1)], b_b[:, BK:BK + E].unsqueeze(2))\
                                    .then_inc(s["lg_out"], 1)
                    elif has(-1):
                        act.wait_ge(s["shifted"], i)
                        nc.scalar.activation(pr[:, :, :], pr[:, :, :], ACT.Exp, scale=SCALE1)\
                            .then_inc(s["exped"], 1)
                    if not has(0) and has(-2):
                        act.wait_ge(s["lg"], i - 1)
                        nc.scalar.copy(g.lg[:, :, bass.ds(i - 2, 1)], b_b[:, BK:BK + E].unsqueeze(2))\
                            .then_inc(s["lg_out"], 1)
                    if has(-1):
                        act.wait_ge(s["pT"], i)
                        for b in range(2):
                            for e in range(2):
                                last = nc.scalar.copy(*block_of(PT, b_b, 0, b, e))
                        last.then_inc(s["pT_act"], 1)
                        act.wait_ge(s["o"], i)
                        nc.scalar.copy(oT[:, :, :].rearrange("p j t -> p (j t)"), b_b[:, :]).then_inc(s["oT"], 1)
                    if has(0):
                        act.wait_ge(s["v"], i + 1)
                        nc.scalar.copy(v[:, :], b_a[:, :]).then_inc(s["v_out"], 1)
                        act.wait_ge(s["qkT"], i + 1)
                        nc.scalar.activation(qT[:, :, :].rearrange("p j t -> p (j t)"), b_qk[:, 0:V1], ACT.Identity,
                                             bias=g.qn[:, 1:2], scale=g.qn[:, 0:1]).then_inc(s["q_out"], 1)
                        if not later(i):
                            act.wait_ge(s["cleared"], 1)
                        nc.scalar.activation(kbd[0:S, :, :, 0, :].rearrange("p j b k -> p (j b) k"),
                                             b_qk[0:S, V1:QK1].rearrange("p (n k) -> p n k", k=S), ACT.Identity,
                                             bias=g.kn[0:S, 1:2], scale=g.kn[0:S, 0:1]).then_inc(s["kbd_lo"], 1)
                act.wait_ge(g.loaded1, 16 * 5)
                pipeline(act, step, NT, 0, 3)

            @block.gpsimd
            def _(pool):
                def step(i, has):
                    if has(1):
                        pool.wait_ge(s["eps"], i + 2)
                        nc.gpsimd.tensor_tensor(rstd[:, :], veps[:, :], g.mhalf[:, 0:1], ALU.pow)\
                            .then_inc(s["rstd"], 1)
                    if has(0):
                        for n in range(QG):
                            pool.wait_ge(s["vq"], QG * i + n + 1)
                            nc.gpsimd.tensor_tensor(rq[:, 8 * n:8 * n + 8], vq[:, 8 * n:8 * n + 8],
                                                    g.mhalf[:, 0:8], ALU.pow).then_inc(s["rq"], 1)
                nc.gpsimd.memset(kbd[:, :, :, :, :], 0.0).then_inc(s["cleared"], 1)
                pipeline(pool, step, NT, 1, 3)

            @block.vector
            def _(dve):
                def step(i, has):
                    if has(1):
                        nc.vector.bn_stats(st[:, :], g.X[:, i + 1, :]).then_inc(s["stats"], 1)
                        dve.wait_ge(s["stats"], i + 2)
                    if has(0):
                        dve.wait_ge(s["xT"], i + 1)
                        for c in range(DC):
                            last = nc.vector.scalar_tensor_tensor(
                                hT[:, c, :].rearrange("p (b t) -> p b t", b=2),
                                b_b[:, BK + c * P:BK + (c + 1) * P].rearrange("p (b t) -> p b t", b=2),
                                g.ln1g[:, c:c + 1],
                                g.sh_1[:, c, bass.ds(2 * i, 2)].unsqueeze(2).to_broadcast([P, 2, S]),
                                ALU.mult, ALU.add)
                        last.then_inc(s["hT"], 1)
                    if has(1):
                        nc.vector.bn_aggr(mv[:, :], st[:, :]).then_inc(s["aggr"], 1)
                    if has(-2):
                        dve.wait_ge(s["proj"], i - 1)
                        if later(i - 2):
                            dve.wait_ge(s["stored"], 32 * (i - 2))
                            dve.wait_ge(s["xsT"], i - 2)
                        nc.vector.tensor_tensor(xs[:, :], g.X[:, i - 2, :], b_b[:, 0:D], ALU.add)\
                            .then_inc(s["res"], 1)
                    if has(-1):
                        dve.wait_ge(s["s"], i)
                        nc.vector.reduce_max(mx[:, :], b_a[:, :].rearrange("p (h k) -> p h k", h=H), AX)\
                            .then_inc(s["maxed"], 1)
                        dve.wait_ge(s["maxed"], i)
                        nc.vector.tensor_tensor(pr[:, :, :], b_a[:, :].rearrange("p (h k) -> p h k", h=H),
                                                mx[:, :].unsqueeze(2).to_broadcast([P, H, S]), ALU.subtract)\
                            .then_inc(s["shifted"], 1)
                    if has(1):
                        dve.wait_ge(s["aggr"], i + 2)
                        nc.vector.tensor_scalar(veps[:, :], mv[:, 1:2], EPS1, None, ALU.add).then_inc(s["eps"], 1)
                    if has(-2):
                        dve.wait_ge(s["xsT"], i - 1)
                        nc.vector.tensor_copy(xsT[:, :, :].rearrange("p c t -> p (c t)"), b_b[:, 0:D])\
                            .then_inc(s["xsT_out"], 1)

                    def sums(n):
                        dve.wait_ge(s["sq"], QG * i + n + 1)
                        nc.vector.reduce_sum(ss[:, n * 8:(n + 1) * 8],
                                             sq[:, n * BK:(n + 1) * BK].rearrange("p (h d) -> p h d", d=HD1), AX)\
                            .then_inc(s["red"], 1)

                    def moments(n):
                        dve.wait_ge(s["red"], QG * i + n + 1)
                        nc.vector.tensor_scalar(vq[:, 8 * n:8 * n + 8], ss[:, 8 * n:8 * n + 8], 1.0 / HD1, EPS1,
                                                ALU.mult, ALU.add).then_inc(s["vq"], 1)
                    if has(0):
                        sums(0)
                    if has(-1):
                        dve.wait_ge(s["exped"], i)
                        nc.vector.reduce_sum(sm[:, :], pr[:, :, :], AX).then_inc(s["summed"], 1)
                        dve.wait_ge(s["summed"], i)
                        nc.vector.reciprocal(rs[:, :], sm[:, :]).then_inc(s["recip"], 1)
                        dve.wait_ge(s["recip"], i)
                        nc.vector.tensor_tensor(pr[:, :, :], pr[:, :, :],
                                                rs[:, :].unsqueeze(2).to_broadcast([P, H, S]), ALU.mult)\
                            .then_inc(s["probs"], 1)
                    if has(0):
                        moments(0)
                        for n in range(1, QG):
                            sums(n)
                            moments(n)
                    if has(-1):
                        dve.wait_ge(s["pT"], i)
                        for b in range(2):
                            for e in range(2):
                                last = nc.vector.tensor_copy(*block_of(PT, b_b, 1, b, e))
                        last.then_inc(s["pT_dve"], 1)
                    if has(1):
                        dve.wait_ge(s["rstd"], i + 2)
                        if later(i + 1):
                            dve.wait_ge(s["xT"], i + 1)
                        nc.vector.tensor_scalar(xhat[:, :], g.X[:, i + 1, :], mv[:, 0:1], rstd[:, 0:1],
                                                ALU.subtract, ALU.mult).then_inc(s["xhat"], 1)
                    if has(0):
                        if later(i):
                            dve.wait_ge(s["qkT"], i)
                        for n in range(QG):
                            dve.wait_ge(s["rq"], QG * i + n + 1)
                            nc.vector.tensor_tensor(
                                qk[:, n * BK:(n + 1) * BK].rearrange("p (h d) -> p h d", d=HD1),
                                b_qk[:, n * BK:(n + 1) * BK].rearrange("p (h d) -> p h d", d=HD1),
                                rq[:, 8 * n:8 * n + 8].unsqueeze(2).to_broadcast([P, 8, HD1]), ALU.mult)\
                                .then_inc(s["qkn"], 1)
                        dve.wait_ge(s["qkT"], i + 1)
                        if not later(i):
                            dve.wait_ge(s["cleared"], 1)
                        nc.vector.tensor_scalar(kbd[S:P, :, :, 1, :].rearrange("p j b k -> p (j b) k"),
                                                b_qk[S:P, V1:QK1].rearrange("p (n k) -> p n k", k=S),
                                                g.kn[S:P, 0:1], g.kn[S:P, 1:2], ALU.mult, ALU.add)\
                            .then_inc(s["kbd_hi"], 1)
                dve.wait_ge(g.loaded1, 16 * 5)
                pipeline(dve, step, NT, 1, 3)

            @block.tensor
            def _(pe):
                def step(i, has):
                    if has(-1):
                        pe.wait_ge(s["q_out"], i)
                        pe.wait_ge(s["kbd_lo"], i)
                        pe.wait_ge(s["kbd_hi"], i)
                        pe.wait_ge(s["v_out"], i)
                        for j in range(H // 2):
                            for b in range(2):
                                last = nc.tensor.matmul(b_a[b * S:(b + 1) * S, j * P:(j + 1) * P],
                                                        qT[:, j, b * S:(b + 1) * S],
                                                        kbd[:, j, b, :, :].rearrange("p e k -> p (e k)"),
                                                        start=True, stop=True)
                        last.then_inc(s["s"], 1)

                    def products(n):
                        for kc in range(DC):
                            last = nc.tensor.matmul(b_qk[:, n * BK:(n + 1) * BK], hT[:, kc, :],
                                                    g.wqkv1[:, kc, n * BK:(n + 1) * BK],
                                                    start=(kc == 0), stop=(kc == DC - 1))
                        last.then_inc(s["qk"], 1)
                    if has(0):
                        pe.wait_ge(s["hT"], i + 1)
                        products(0)
                        products(1)
                    if has(-2):
                        pe.wait_ge(s["res"], i - 1)
                        for c in range(DC):
                            last = nc.tensor.transpose(b_b[:, c * P:(c + 1) * P], xs[:, c * P:(c + 1) * P], ident)
                        last.then_inc(s["xsT"], 1)
                    if has(0):
                        products(2)
                    if has(-2):
                        pe.wait_ge(s["xsT_out"], i - 1)
                        for kc in range(DC):
                            last = nc.tensor.matmul(b_b[:, BK:BK + E], xsT[:, kc, :], g.wgate[:, kc, :],
                                                    start=(kc == 0), stop=(kc == DC - 1))
                        last.then_inc(s["lg"], 1)
                    if has(0):
                        products(3)
                    if has(-1):
                        pe.wait_ge(s["probs"], i)
                        if later(i - 1):
                            pe.wait_ge(s["lg_out"], i - 1)
                        for j in range(H // 2):
                            last = nc.tensor.transpose(b_b[:, j * P:(j + 1) * P],
                                                       pr[:, 2 * j:2 * j + 2, :].rearrange("p h k -> p (h k)"), ident)
                        last.then_inc(s["pT"], 1)
                    if has(0):
                        for n in range(2):
                            for kc in range(DC):
                                last = nc.tensor.matmul(b_a[:, n * BK:(n + 1) * BK], hT[:, kc, :],
                                                        g.wqkv1[:, kc, QK1 + n * BK:QK1 + (n + 1) * BK],
                                                        start=(kc == 0), stop=(kc == DC - 1))
                        last.then_inc(s["v"], 1)
                    if has(-1):
                        pe.wait_ge(s["pT_act"], i)
                        pe.wait_ge(s["pT_dve"], i)
                        for h in range(H):
                            r, j = h % 2, h // 2
                            last = nc.tensor.matmul(b_b[r * S:(r + 1) * S, j * P:(j + 1) * P],
                                                    v[:, h * HD1:(h + 1) * HD1], PT[:, h, :],
                                                    start=True, stop=True)
                        last.then_inc(s["o"], 1)
                    if has(0):
                        for j in range(H):
                            if j % QG == 0:
                                pe.wait_ge(s["qkn"], QG * i + j // QG + 1)
                            last = nc.tensor.transpose(b_qk[:, j * P:(j + 1) * P], qk[:, j * P:(j + 1) * P], ident)
                        last.then_inc(s["qkT"], 1)
                    if has(-1):
                        pe.wait_ge(s["oT"], i)
                        for kc in range(H // 2):
                            last = nc.tensor.matmul(b_b[:, 0:D], oT[:, kc, :], g.wout1[:, kc, :],
                                                    start=(kc == 0), stop=(kc == H // 2 - 1))
                        last.then_inc(s["proj"], 1)
                    if has(1):
                        pe.wait_ge(s["xhat"], i + 2)
                        for c in range(DC):
                            last = nc.tensor.transpose(b_b[:, BK + c * P:BK + (c + 1) * P],
                                                       xhat[:, c * P:(c + 1) * P], ident)
                        last.then_inc(s["xT"], 1)
                pe.wait_ge(g.loaded1, 16 * 5)
                pe.wait_ge(g.centred, 1)
                pipeline(pe, step, NT, 1, 3)
        m.clear()


def route_phase(nc, a, g):
    NE = E * NT
    with ExitStack() as ctx:
        m = Mem(nc, ctx)
        mx = m.sb("r_mx", [P, NT])
        sm = m.sb("r_sm", [P, NT])
        rs = m.sb("r_rs", [P, NT])
        pb = m.sb("r_prob", [P, E, NT])
        pbt = m.sb("r_prob_t", [P, NT, E])
        pbq = m.sb("r_prob_q", [P, 4, E, 16])
        byp = m.sb("r_by_expert", [P, 4 * P])
        junk = m.sb("r_junk", [P, 4 * P])
        cnt = m.sb("r_cnt", [P, 1])
        bitsi = m.sb("r_bitsi", [P, BITS + 1], I32)
        cand = m.sb("r_cand", [P, 1], I32)
        drop = m.sb("r_drop", [P, 1], I32)
        thr = m.sb("r_thr", [P, P])
        gt, eq = m.sb("r_gt", [P, E, NT], BF16), m.sb("r_eq", [P, E, NT], BF16)
        up, ones = m.sb("r_up", [P, P], BF16), m.sb("r_ones", [P, P], BF16)
        keep = m.sb("r_keep", [P, E, NT])
        inc_g, inc_e = m.sb("r_inc_g", [P, E, NT]), m.sb("r_inc_e", [P, E, NT])
        ag, ae = m.sb("r_ag", [P, E, NT]), m.sb("r_ae", [P, E, NT])
        bg, be = m.sb("r_bg", [P, E, NT]), m.sb("r_be", [P, E, NT])
        ce = m.sb("r_ce", [P, E, NT])
        sg, se = m.sb("r_sg", [P, E, NT]), m.sb("r_se", [P, E, NT])
        slot = m.sb("r_slot", [P, E, NT], I32)
        loi, hii = m.sb("r_loi", [P, E, NT], I32), m.sb("r_hii", [P, E, NT], I32)
        lo, hi = m.sb("r_lo", [P, E, NT], BF16), m.sb("r_hi", [P, E, NT], BF16)
        iota = m.sb("r_iota", [P, P, NT], BF16)
        hot_lo = m.sb("r_hot_lo", [P, 2, P, NT], BF16)
        hot_hi = m.sb("r_hot_hi", [P, NT, SH], BF16)
        pair = m.sb("r_pair", [P, 2, NT, 2 * SH], BF16)
        lists = m.sb("r_lists", [2 * SH, P])
        b_t, b_n, b_l, b_i = (m.ps(f"r_b{n}", 512) for n in "tnli")
        b_pg, b_tg, b_pe, b_te = (m.ps(f"r_b{n}", 512) for n in ("pg", "tg", "pe", "te"))
        names = ("max sub exp sum recip prob prob_t prob_q saved tr by_p count counted drop cand thr_out thr_in "
                 "masks pre scan slots ints hot_lo iota hot_hi pair pair_p lists lists_out rows rows_out consts1").split()
        s = {n: m.sem("r_" + n) for n in names}
        cst = g.cst
        b_l = (b_l, b_t)

        def over_tiles(x, n=NT):
            return x.unsqueeze(1).to_broadcast([P, E, n])

        with nc.Block() as block:
            @block.sync
            def _(sp):
                for to, n in ((g.e_w1, "fc1s"), (g.e_w2, "fc2s")):
                    sp.dma_start(to, a[n][0]).then_inc(g.loaded_e, 16)
                sp.dma_start(g.e_b1, a["b1s"]).then_inc(g.loaded_e, 16)
                sp.dma_start(g.e_lnw, a["mlp_ln"]).then_inc(g.loaded_e, 16)
                sp.dma_start(g.e_b2, a["b2s"].to_broadcast([P, E, D])).then_inc(g.loaded_e, 16)
                sp.wait_ge(s["prob_t"], 1)
                sp.dma_start(g.prob_dram, pbt[:, :, :]).then_inc(s["saved"], 16)
                sp.wait_ge(s["cand"], BITS + 1)
                sp.dma_start(g.thr_dram.rearrange("a p -> p a"), cand[:, :].bitcast(F32)).then_inc(s["thr_out"], 16)
                sp.wait_ge(s["thr_out"], 16)
                sp.dma_start(thr[:, :], g.thr_dram.to_broadcast([P, P])).then_inc(s["thr_in"], 16)
                sp.wait_ge(s["saved"], 16)

            @block.scalar
            def _(act):
                act.wait_ge(s["sub"], 1)
                nc.scalar.activation(pb[:, :, :], pb[:, :, :], ACT.Exp).then_inc(s["exp"], 1)
                act.wait_ge(s["tr"], 1)
                nc.scalar.copy(byp[:, :], b_t[:, :]).then_inc(s["by_p"], 1)

                def step(e, has, par):
                    if has(0):
                        act.wait_ge(s["hot_hi"], e + 1)
                        if later(e) and later(e - 1):
                            act.wait_ge(s["lists"], e - 1)
                        nc.scalar.activation(pair[:, par, :, SH:2 * SH], hot_hi[:, :, :], ACT.Identity,
                                             scale=cst[:, C_P:C_P + 1]).then_inc(s["pair_p"], 1)
                    if has(-1):
                        act.wait_ge(s["lists"], e)
                        if later(e - 1):
                            act.wait_ge(s["rows"], e - 1)
                        nc.scalar.copy(lists[:, :], b_l[1 - par][0:2 * SH, 0:P]).then_inc(s["lists_out"], 1)
                pipeline_by_2(act, step, E, 0, 2)

            @block.gpsimd
            def _(pool):
                nc.gpsimd.tensor_copy(up[:, :], cst[:, C_UP:C_UP + P]).then_inc(s["consts1"], 1)
                nc.gpsimd.memset(ones[:, :], 1.0).then_inc(s["consts1"], 1)
                nc.gpsimd.memset(keep[:, :, 1:NT], 1.0).then_inc(s["consts1"], 1)
                nc.gpsimd.memset(keep[:, :, 0:1], 0.0).then_inc(s["consts1"], 1)
                nc.gpsimd.tensor_copy(bitsi[:, :], cst[:, C_BITS:C_BITS + BITS + 1]).then_inc(s["consts1"], 1)
                nc.gpsimd.tensor_copy(iota[:, :, :], cst[:, C_IOTA:C_IOTA + P].unsqueeze(2).to_broadcast([P, P, NT]))\
                    .then_inc(s["iota"], 1)

            @block.vector
            def _(dve):
                nc.vector.reduce_max(mx[:, :], g.lg[:, :, :].rearrange("p e t -> p t e"), AX).then_inc(s["max"], 1)
                dve.wait_ge(s["max"], 1)
                nc.vector.tensor_tensor(pb[:, :, :], g.lg[:, :, :], over_tiles(mx[:, :]), ALU.subtract)\
                    .then_inc(s["sub"], 1)
                dve.wait_ge(s["exp"], 1)
                nc.vector.reduce_sum(sm[:, :], pb[:, :, :].rearrange("p e t -> p t e"), AX).then_inc(s["sum"], 1)
                dve.wait_ge(s["sum"], 1)
                nc.vector.reciprocal(rs[:, :], sm[:, :]).then_inc(s["recip"], 1)
                dve.wait_ge(s["recip"], 1)
                nc.vector.tensor_tensor(pb[:, :, :], pb[:, :, :], over_tiles(rs[:, :]), ALU.mult)\
                    .then_inc(s["prob"], 1)
                dve.wait_ge(s["prob"], 1)
                nc.vector.tensor_copy(pbq[:, :, :, :], pb[:, :, :].rearrange("p e (b t) -> p b e t", b=4))\
                    .then_inc(s["prob_q"], 1)
                nc.vector.tensor_copy(pbt[:, :, :], pb[:, :, :].rearrange("p e t -> p t e")).then_inc(s["prob_t"], 1)
                dve.wait_ge(s["consts1"], 5)
                nc.vector.tensor_copy(cand[:, :], bitsi[:, 0:1]).then_inc(s["cand"], 1)
                dve.wait_ge(s["by_p"], 1)
                with dve.Fori(0, BITS) as i:
                    dve.wait_ge(s["cand"], i + 1)
                    nc.vector.tensor_scalar(junk[:, :], byp[:, :], cand[:, :].bitcast(F32), None, ALU.is_ge, ALU.add,
                                            accum_out=cnt[:, :]).then_inc(s["count"], 1)
                    dve.wait_ge(s["counted"], i + 1)
                    nc.vector.tensor_scalar(drop[:, :], b_n[:, 0:1], float(CAP), cst[:, bass.ds(C_BITS + i, 1)],
                                            ALU.is_lt, ALU.mult).then_inc(s["drop"], 1)
                    dve.wait_ge(s["drop"], i + 1)
                    nc.vector.scalar_tensor_tensor(cand[:, :], cand[:, :], bitsi[:, bass.ds(i + 1, 1)], drop[:, :],
                                                   ALU.bitwise_or, ALU.bitwise_xor).then_inc(s["cand"], 1)
                dve.wait_ge(s["thr_in"], 16)
                t8 = thr[:, :].rearrange("p (e t) -> p e t", t=16)[:, :, 0:1].to_broadcast([P, E, NT])
                nc.vector.tensor_tensor(gt[:, :, :], pb[:, :, :], t8, ALU.is_gt).then_inc(s["masks"], 1)
                nc.vector.tensor_tensor(eq[:, :, :], pb[:, :, :], t8, ALU.is_equal).then_inc(s["masks"], 1)
                dve.wait_ge(s["pre"], 4)
                for n, (inc, tot) in enumerate(((inc_g, b_tg), (inc_e, b_te))):
                    nc.vector.tensor_tensor_scan(inc[:, :, :].rearrange("p e t -> p (e t)"),
                                                 keep[:, :, :].rearrange("p e t -> p (e t)"), tot[:, :], 0.0,
                                                 ALU.mult, ALU.add).then_inc(s["scan"], 1)
                dve.wait_ge(s["scan"], 2)
                grid = "p (e t) -> p e t"
                nc.vector.tensor_tensor(ag[:, :, :], inc_g[:, :, :], b_tg[:, :].rearrange(grid, e=E), ALU.subtract)\
                    .then_inc(s["slots"], 1)
                nc.vector.tensor_tensor(ae[:, :, :], inc_e[:, :, :], b_te[:, :].rearrange(grid, e=E), ALU.subtract)\
                    .then_inc(s["slots"], 1)
                dve.wait_ge(s["slots"], 2)
                nc.vector.tensor_tensor(bg[:, :, :], ag[:, :, :], b_pg[:, :].rearrange(grid, e=E), ALU.add)\
                    .then_inc(s["slots"], 1)
                nc.vector.tensor_tensor(be[:, :, :], ae[:, :, :], b_pe[:, :].rearrange(grid, e=E), ALU.add)\
                    .then_inc(s["slots"], 1)
                dve.wait_ge(s["slots"], 4)
                nc.vector.scalar_tensor_tensor(sg[:, :, :], bg[:, :, :], -NOSLOT, gt[:, :, :], ALU.add, ALU.mult)\
                    .then_inc(s["slots"], 1)
                nc.vector.tensor_tensor(ce[:, :, :], be[:, :, :], inc_g[:, :, NT - 1:NT].to_broadcast([P, E, NT]),
                                        ALU.add).then_inc(s["slots"], 1)
                dve.wait_ge(s["slots"], 6)
                nc.vector.scalar_tensor_tensor(se[:, :, :], ce[:, :, :], -NOSLOT, eq[:, :, :], ALU.add, ALU.mult)\
                    .then_inc(s["slots"], 1)
                dve.wait_ge(s["slots"], 7)
                nc.vector.scalar_tensor_tensor(slot[:, :, :], sg[:, :, :], NOSLOT, se[:, :, :], ALU.add, ALU.add)\
                    .then_inc(s["slots"], 1)
                dve.wait_ge(s["slots"], 8)
                nc.vector.tensor_single_scalar(loi[:, :, :], slot[:, :, :], P - 1, ALU.bitwise_and)\
                    .then_inc(s["ints"], 1)
                nc.vector.tensor_single_scalar(hii[:, :, :], slot[:, :, :], 7, ALU.logical_shift_right)\
                    .then_inc(s["ints"], 1)
                dve.wait_ge(s["ints"], 2)
                nc.vector.tensor_copy(lo[:, :, :], loi[:, :, :]).then_inc(s["ints"], 1)
                nc.vector.tensor_copy(hi[:, :, :], hii[:, :, :]).then_inc(s["ints"], 1)
                dve.wait_ge(s["ints"], 4)

                dve.wait_ge(s["iota"], 1)

                def step(e, has, par):
                    if has(0):
                        if later(e):
                            dve.wait_ge(s["pair"], e)
                            dve.wait_ge(s["pair_p"], e)
                        nc.vector.tensor_tensor(hot_hi[:, :, :], cst[:, C_IOTA:C_IOTA + SH].unsqueeze(1)
                                                .to_broadcast([P, NT, SH]),
                                                hi[:, bass.ds(e, 1), :].rearrange("p e t -> p (e t)").unsqueeze(2)
                                                .to_broadcast([P, NT, SH]), ALU.is_equal).then_inc(s["hot_hi"], 1)
                        if later(e) and later(e - 1):
                            dve.wait_ge(s["lists"], e - 1)
                        nc.vector.tensor_tensor(hot_lo[:, par, :, :], iota[:, :, :],
                                                lo[:, bass.ds(e, 1), :].to_broadcast([P, P, NT]),
                                                ALU.is_equal).then_inc(s["hot_lo"], 1)
                        dve.wait_ge(s["hot_hi"], e + 1)
                        nc.vector.tensor_tensor(pair[:, par, :, 0:SH], hot_hi[:, :, :],
                                                cst[:, C_IOTA:C_IOTA + NT].unsqueeze(2).to_broadcast([P, NT, SH]),
                                                ALU.mult).then_inc(s["pair"], 1)
                    if has(-2):
                        dve.wait_ge(s["rows"], e - 1)
                        nc.vector.tensor_copy(g.rows[:, bass.ds(e - 2, 1), :], b_i[:, 0:2 * SH].unsqueeze(1))\
                            .then_inc(s["rows_out"], 1)
                pipeline_by_2(dve, step, E, 0, 2)
                dve.wait_ge(s["rows_out"], E)

            @block.tensor
            def _(pe):
                pe.wait_ge(s["prob_q"], 1)
                for b in range(4):
                    last = nc.tensor.transpose(b_t[:, b * P:(b + 1) * P],
                                               pbq[:, b, :, :].rearrange("p e t -> p (e t)"),
                                               cst[:, C_ID:C_ID + P])
                last.then_inc(s["tr"], 1)
                with pe.Fori(0, BITS) as i:
                    pe.wait_ge(s["count"], i + 1)
                    nc.tensor.matmul(b_n[:, 0:1], cst[:, C_SAME:C_SAME + P], cnt[:, :], start=True, stop=True)\
                        .then_inc(s["counted"], 1)
                pe.wait_ge(s["consts1"], 5)
                pe.wait_ge(s["masks"], 2)
                for w, mask, to in ((up, gt, b_pg), (ones, gt, b_tg), (up, eq, b_pe), (ones, eq, b_te)):
                    nc.tensor.matmul(to[:, :], w[:, :], mask[:, :, :].rearrange("p e t -> p (e t)"),
                                     start=True, stop=True).then_inc(s["pre"], 1)

                def step(e, has, par):
                    if has(0):
                        pe.wait_ge(s["pair"], e + 1)
                        pe.wait_ge(s["pair_p"], e + 1)
                        pe.wait_ge(s["hot_lo"], e + 1)
                        if later(e) and later(e - 1):
                            pe.wait_ge(s["lists_out"], e - 1)
                        for t in range(NT):
                            last = nc.tensor.matmul(b_l[par][0:2 * SH, 0:P], pair[:, par, t, :],
                                                    hot_lo[:, par, :, t], start=(t == 0), stop=(t == NT - 1))
                        last.then_inc(s["lists"], 1)
                    if has(-1):
                        pe.wait_ge(s["lists_out"], e)
                        if later(e - 1):
                            pe.wait_ge(s["rows_out"], e - 1)
                        nc.tensor.matmul(b_i[:, 0:2 * SH], lists[:, :], cst[0:2 * SH, C_ROW:C_ROW + 2 * SH],
                                         start=True, stop=True).then_inc(s["rows"], 1)
                pipeline_by_2(pe, step, E, 0, 2)
        m.clear()


def experts_phase(nc, a, out, g):
    with ExitStack() as ctx:
        m = Mem(nc, ctx)
        w1, w2, b2, lnw = g.e_w1, g.e_w2, g.e_b2, g.e_lnw
        b1e = m.sb("e_b1e", [P, MC])
        rows_g = m.sb("e_rows_g", [P, 2 * SH], U32)
        rows_s = m.sb("e_rows_s", [P, SH], U32)
        xg = [m.sb(f"e_xg{h}", [P, GT, D]) for h in range(2)]
        pg = [m.sb(f"e_pg{h}", [P, GT, E]) for h in range(2)]
        wt = [m.sb(f"e_wt{h}", [P, GT]) for h in range(2)]
        xhat = m.sb("e_xhat", [P, GT, D])
        st = m.sb("e_st", [P, GT, 6])
        mv = m.sb("e_mv", [P, GT, 2])
        veps = m.sb("e_veps", [P, GT])
        rstd = m.sb("e_rstd", [P, GT])
        hT = m.sb("e_hT", [P, DC, GTOK])
        uT = m.sb("e_uT", [P, MC, GTOK])
        tmp = m.sb("e_tmp", [P, D])
        ys = [m.sb(f"e_ys{h}", [P, GT, D]) for h in range(2)]
        b_u = [m.ps(f"e_bu{j}", GTOK) for j in range(4)]
        b_x = [m.ps(f"e_bx{j}", GTOK) for j in range(DC)]
        b_y = [m.ps(f"e_by{j}", GTOK) for j in range(2)]
        names = ("w1 w2 rows_g rows_s held gather0 gather1 gather_p0 gather_p1 b1e wt dve_held stats aggr eps rstd xhat xT hT u gelu "
                 "y y1 ys added").split()
        s = {n: m.sem("e_" + n) for n in names}
        ident = g.cst[:, C_ID:C_ID + P]
        HALF = 2

        with nc.Block() as block:
            @block.sync
            def _(sp):
                with sp.Fori(1, E) as e:
                    sp.wait_ge(s["u"], HALF * MC * e)
                    sp.dma_start(w1[:, :, :], a["fc1s"][e]).then_inc(s["w1"], 16)
                    sp.wait_ge(s["y"], HALF * GT * e)
                    sp.dma_start(w2[:, :, :], a["fc2s"][e]).then_inc(s["w2"], 16)

            @block.scalar
            def _(act):
                def step(e, has):
                    for h in range(HALF):
                        i = HALF * e + h
                        if has(0):
                            for n in range(MC):
                                act.wait_ge(s["u"], MC * i + n + 1)
                                if h == 0 and n == 0:
                                    act.wait_ge(s["b1e"], e + 1)
                                if n == 0 and (h or later(e)):
                                    act.wait_ge(s["y"], GT * i)
                                nc.scalar.activation(uT[:, n, :], b_u[n % 4][:, :], ACT.Gelu_apprx_tanh,
                                                     bias=b1e[:, n:n + 1]).then_inc(s["gelu"], 1)
                pipeline(act, step, E, 1, 1)

            @block.gpsimd
            def _(pool):
                def step(e, has):
                    for h in range(HALF):
                        i = HALF * e + h
                        if has(1):
                            if h == 0:
                                pool.wait_ge(s["rows_g"], e + 2)
                            if later(e + 1):
                                pool.wait_ge(s["xhat"], GT * (i + 1))
                            pool.sem_inc(s["held"], 1)
                            for k in range(GT):
                                c = h * GT + k
                                nc.gpsimd.indirect_dma_start(
                                    xg[h][:, k, :], None, g.tok_dram.rearrange("t p d -> (t p) d"),
                                    bass.IndirectOffsetOnAxis(rows_g[:, c:c + 1], 0)).then_inc(s[f"gather{h}"], 16)
                            for k in range(GT):
                                c = h * GT + k
                                nc.gpsimd.indirect_dma_start(
                                    pg[h][:, k, :], None, g.prob_dram.rearrange("p t e -> (p t) e"),
                                    bass.IndirectOffsetOnAxis(rows_g[:, SH + c:SH + c + 1], 0))\
                                    .then_inc(s[f"gather_p{h}"], 16)
                            pool.wait_ge(s["eps"], i + 3)
                            nc.gpsimd.tensor_tensor(rstd[:, :], veps[:, :], g.mhalf[:, 0:GT], ALU.pow)\
                                .then_inc(s["rstd"], 1)
                        if has(0):
                            for k in range(GT):
                                c = h * GT + k
                                pool.wait_ge(s["ys"], GT * i + k + 1)
                                if h or k or later(e):
                                    pool.wait_ge(s["added"], 16 * (GT * i + k))
                                pool.sem_inc(s["held"], 1)
                                nc.gpsimd.indirect_dma_start(
                                    out.rearrange("t p d -> (t p) d"),
                                    bass.IndirectOffsetOnAxis(rows_s[:, c:c + 1], 0), ys[h][:, k, :], None,
                                    compute_op=ALU.add).then_inc(s["added"], 16)
                pipeline(pool, step, E, 1, 1)
                pool.wait_ge(s["added"], 16 * E * SH)

            @block.vector
            def _(dve):
                def step(e, has):
                    if has(0):
                        if later(e):
                            dve.wait_ge(s["gelu"], HALF * MC * e)
                        nc.vector.tensor_scalar(b1e[:, :], g.e_b1[:, bass.ds(e, 1), :].rearrange("p e r -> p (e r)"),
                                                0.0, None, ALU.add).then_inc(s["b1e"], 1)
                    if has(1):
                        if later(e + 1):
                            for h in range(HALF):
                                dve.wait_ge(s[f"gather{h}"], 16 * GT * (e + 1))
                                dve.wait_ge(s[f"gather_p{h}"], 16 * GT * (e + 1))
                        nc.vector.tensor_scalar(rows_g[:, :], g.rows[:, bass.ds(e + 1, 1), :]
                                                .rearrange("p e r -> p (e r)"), 0.0, None, ALU.add)\
                            .then_inc(s["rows_g"], 1)
                    for h in range(HALF):
                        i = HALF * e + h
                        if h == 0 and has(0) or h == 1 and has(1):
                            dve.wait_ge(s["xT"], i + 2)
                            for c in range(DC):
                                nc.vector.tensor_scalar(hT[:, c, :], b_x[c][:, :], lnw[:, c, 0:1], lnw[:, c, 1:2],
                                                        ALU.mult, ALU.add).then_inc(s["hT"], 1)
                        if h == 0 and has(0):
                            if later(e):
                                dve.wait_ge(s["added"], 16 * SH * e)
                            nc.vector.tensor_scalar(rows_s[:, :], g.rows[:, bass.ds(e, 1), 0:SH]
                                                    .rearrange("p e r -> p (e r)"), 0.0, None, ALU.add)\
                                .then_inc(s["rows_s"], 1)
                        if has(0):
                            for k in range(GT):
                                n = GT * i + k
                                dve.wait_ge(s["y"], n + 1)
                                if k or h or later(e):
                                    dve.wait_ge(s["ys"], n)
                                if k == 0 and later(e):
                                    dve.wait_ge(s["added"], 16 * (GT * (i - 1)))
                                nc.vector.tensor_tensor(tmp[:, :], b_y[k % 2][:, 0:D],
                                                        b2[:, bass.ds(e, 1), :].rearrange("p e r -> p (e r)"),
                                                        ALU.add).then_inc(s["y1"], 1)
                                dve.wait_ge(s["y1"], n + 1)
                                if k == 0:
                                    dve.wait_ge(s["wt"], i + 1)
                                nc.vector.tensor_scalar(ys[h][:, k, :], tmp[:, :],
                                                        wt[h][:, k:k + 1], None,
                                                        ALU.mult).then_inc(s["ys"], 1)
                        if has(1):
                            dve.wait_ge(s[f"gather{h}"], 16 * GT * (e + 2))
                            for k in range(GT):
                                nc.vector.bn_stats(st[:, k, :], xg[h][:, k, :]).then_inc(s["stats"], 1)
                            dve.wait_ge(s[f"gather_p{h}"], 16 * GT * (e + 2))
                            if has(0):
                                dve.wait_ge(s["ys"], GT * (i + 1))
                            nc.vector.tensor_copy(wt[h][:, :].unsqueeze(2), pg[h][:, :, bass.ds(e + 1, 1)])\
                                .then_inc(s["wt"], 1)
                            dve.wait_ge(s["stats"], GT * (i + 3))
                            dve.sem_inc(s["dve_held"], 1)
                            for k in range(GT):
                                nc.vector.bn_aggr(mv[:, k, :], st[:, k, :]).then_inc(s["aggr"], 1)
                            dve.wait_ge(s["aggr"], GT * (i + 3))
                            nc.vector.tensor_scalar(veps[:, :], mv[:, :, 1], EPS1, None, ALU.add)\
                                .then_inc(s["eps"], 1)
                            dve.wait_ge(s["rstd"], i + 3)
                            if h or later(e + 1):
                                dve.wait_ge(s["xT"], i + 2)
                            for k in range(GT):
                                nc.vector.tensor_scalar(xhat[:, k, :], xg[h][:, k, :], mv[:, k, 0:1],
                                                        rstd[:, k:k + 1], ALU.subtract, ALU.mult)\
                                    .then_inc(s["xhat"], 1)
                dve.wait_ge(g.loaded_e, 80)
                pipeline(dve, step, E, 1, 1)

            @block.tensor
            def _(pe):
                def step(e, has):
                    for h in range(HALF):
                        i = HALF * e + h
                        if has(0):
                            pe.wait_ge(s["hT"], DC * (i + 1))
                            if h == 0 and later(e):
                                pe.wait_ge(s["w1"], 16 * e)
                            for n in range(MC):
                                if n >= 4 or h or later(e):
                                    pe.wait_ge(s["gelu"], MC * i + n - 3)
                                for kc in range(DC):
                                    last = nc.tensor.matmul(b_u[n % 4][:, :], w1[:, kc, n * P:(n + 1) * P],
                                                            hT[:, kc, :], start=(kc == 0), stop=(kc == DC - 1))
                                last.then_inc(s["u"], 1)
                        if h == 0 and has(0) or h == 1 and has(1):
                            pe.wait_ge(s["xhat"], GT * (i + 2))
                            if h == 0 or later(e + 1):
                                pe.wait_ge(s["hT"], DC * (i + 1))
                            for c in range(DC):
                                for k in range(GT):
                                    last = nc.tensor.transpose(b_x[c][:, k * P:(k + 1) * P],
                                                               xhat[:, k, c * P:(c + 1) * P], ident)
                            last.then_inc(s["xT"], 1)
                        if has(0):
                            if h == 0 and later(e):
                                pe.wait_ge(s["w2"], 16 * e)
                            pe.wait_ge(s["gelu"], MC * (i + 1))
                            for k in range(GT):
                                n = GT * i + k
                                if k >= 2 or h or later(e):
                                    pe.wait_ge(s["y1"], n - 1)
                                for kc in range(MC):
                                    last = nc.tensor.matmul(b_y[k % 2][:, 0:D], uT[:, kc, k * P:(k + 1) * P],
                                                            w2[:, kc, :], start=(kc == 0), stop=(kc == MC - 1))
                                last.then_inc(s["y"], 1)
                pe.wait_ge(g.loaded_e, 80)
                pipeline(pe, step, E, 1, 1)
        m.clear()


class Kept:
    pass


def program(nc, a, out, phases=9):
    with ExitStack() as ctx:
        m = Mem(nc, ctx)
        g = Kept()
        g.cst = m.sb("consts_sb", [P, C_ALL])[:, :]
        g.mhalf = m.sb("minus_half", [P, 32])
        g.X = m.sb("X", [P, NT, D])
        g.PT = m.sb("PT", [P, H, P])
        g.sh_1 = m.sb("shift_1", [P, DC, B])
        g.ln1g = m.sb("ln1g", [P, DC])[:, :]
        g.lg = m.sb("expert_scores", [P, E, NT])
        g.loaded, g.loaded1, g.centred = m.sem("loaded"), m.sem("loaded1"), m.sem("centred")
        g.loaded_e, g.loaded_w1 = m.sem("loaded_experts"), m.sem("loaded_w1")
        g.rows = m.sb("rows", [P, E, 2 * SH], U32)
        g.prob_dram = nc.dram_tensor("probs", [P, NT, E], F32, kind="Internal").ap()
        g.thr_dram = nc.dram_tensor("thresholds", [1, P], F32, kind="Internal").ap()
        g.tok_dram = nc.dram_tensor("tokens", [NT, P, D], F32, kind="Internal").ap()
        g.gate_dram = nc.dram_tensor("gates_of_rows", [B, 2 * D], F32, kind="Internal").ap()
        with ExitStack() as ctx0:
            m0 = Mem(nc, ctx0)
            g.w1_0 = m0.sb("m0_w1", [P, DC, MLP])[:, :, :]
            g.sh_m, g.sc_m = (m0.sb(n, [P, DC, B]) for n in ("shift_mlp", "scale_mlp"))
            with ExitStack() as ctx1:
                m1 = Mem(nc, ctx1)
                g.sh_a, g.sc_a = (m1.sb(n, [P, DC, B]) for n in ("shift_msa", "scale_msa"))
                g.wqkv0 = m1.sb("wqkv0", [P, DC, 3 * D])[:, :, :]
                g.wproj0 = m1.sb("wproj0", [P, DC, D])[:, :, :]
                g.qkb0 = m1.sb("qkb0", [P, 2 * DC])[:, :]
                g.vb0 = m1.sb("vb0", [P, D])[:, :]
                g.pb0 = m1.sb("pb0", [P, D])[:, :]
                g.mrow = m1.sb("mrow", [P, NT])[:, :]
                g.hidden = m1.sb("hidden", [P, NT, S])[:, :, :]
                g.vm = m1.sb("vm", [P, 2, H // 2, 2 * HD0])
                setup_phase(nc, a, g)
                if phases >= 1:
                    attention0_phase(nc, a, g)
            g.wqkv1 = m0.sb("wqkv1", [P, DC, 3 * V1])[:, :, :]
            g.wout1 = m0.sb("wout1", [P, H // 2, D])[:, :, :]
            g.wgate = m0.sb("wgate", [P, DC, E])[:, :, :]
            g.qn, g.kn = (m0.sb(n, [P, 2])[:, :] for n in ("qn", "kn"))
            if phases >= 2:
                mlp0_phase(nc, a, g)
            if phases >= 3:
                attention1_phase(nc, a, out, g)
        g.e_w1 = m.sb("e_w1", [P, DC, MLP])[:, :, :]
        g.e_w2 = m.sb("e_w2", [P, MC, D])[:, :, :]
        g.e_b1 = m.sb("e_b1", [P, E, MC])[:, :, :]
        g.e_b2 = m.sb("e_b2", [P, E, D])[:, :, :]
        g.e_lnw = m.sb("e_lnw", [P, DC, 2])[:, :, :]
        if phases >= 4:
            route_phase(nc, a, g)
        if phases >= 5:
            experts_phase(nc, a, out, g)


def feature_major(v):
    return np.ascontiguousarray(v.reshape(-1, P).T)


def weight(w):
    return np.ascontiguousarray(w.T.reshape(-1, P, w.shape[0]).transpose(1, 0, 2))


def layouts(x, cond_1024, mask_BxS_bk1, **w):
    n = {k: np.asarray(v) for k, v in w.items()}
    L0, L1 = "L0_cond_", "L1_cond_"
    mask = np.asarray(mask_BxS_bk1)
    ada_b = n[L0 + "ada_b"].reshape(6, DC, P)
    return {
        "x": np.asarray(x).reshape(NT, P, D),
        "condT": weight(np.asarray(cond_1024)),
        "mask": mask,
        "maskT": np.ascontiguousarray(mask.reshape(NT, P).T),
        "consts": constants(),
        "ada_w": weight(n[L0 + "ada_w"]),
        "ada_b": np.ascontiguousarray(ada_b[[0, 1, 3, 4]].reshape(4 * DC, P).T),
        "ada_row": n[L0 + "ada_b"].reshape(1, -1),
        "ada1_w": weight(n[L1 + "W_ada"]),
        "ada1_b": feature_major(n[L1 + "b_ada"]),
        "ln1_b": feature_major(n[L1 + "ln1_b"]),
        "ln1_g": feature_major(n[L1 + "ln1_g"]),
        "qkv0_w": weight(n[L0 + "qkv_w"]),
        "qkv0_row": n[L0 + "qkv_b"].reshape(1, -1),
        "qk0_b": feature_major(n[L0 + "qkv_b"][:2 * D]),
        "proj0_w": weight(n[L0 + "proj_w"]),
        "fc1_0_w": weight(n[L0 + "fc1_w"]),
        "fc1_0_b": feature_major(n[L0 + "fc1_b"]),
        "fc2_0_w": weight(n[L0 + "fc2_w"]),
        "fc2_0_row": n[L0 + "fc2_b"].reshape(1, -1),
        "qkv1_w": weight(n[L1 + "Wqkv"]),
        "out1_w": weight(n[L1 + "Wout"]),
        "gate_w": weight(n[L1 + "Wgate"]),
        "qn": np.stack([np.tile(n[L1 + "qn_g"], 2), np.tile(n[L1 + "qn_b"], 2)], 1),
        "kn": np.stack([np.tile(n[L1 + "kn_g"], 2), np.tile(n[L1 + "kn_b"], 2)], 1),
        "fc1s": np.stack([weight(w1) for w1 in n[L1 + "fc1s"]]),
        "fc2s": np.stack([weight(w2) for w2 in n[L1 + "fc2s"]]),
        "b1s": np.ascontiguousarray(n[L1 + "b1s"].reshape(E, MC, P).transpose(2, 0, 1)),
        "b2s": n[L1 + "b2s"].reshape(1, E, D),
        "mlp_ln": np.stack([feature_major(n[L1 + "mlp_g"]), feature_major(n[L1 + "mlp_b"])], 2),
        "proj0_row": n[L0 + "proj_b"].reshape(1, -1),
    }


def kernel(**inputs):
    import concourse.bacc as bacc
    from concourse.bass_utils import run_bass_kernel_spmd

    nc = bacc.Bacc("TRN2", target_bir_lowering=False, num_devices=1)
    arrays = {"in_" + n: v for n, v in layouts(**inputs).items()}
    a = {n[3:]: nc.dram_tensor(n, v.shape, mybir.dt.from_np(v.dtype), kind="ExternalInput").ap()
         for n, v in arrays.items()}
    out = nc.dram_tensor("out", [NT, P, D], F32, kind="ExternalOutput").ap()
    program(nc, a, out)
    r = run_bass_kernel_spmd(nc, [arrays], core_ids=[0])
    return r.results[0]["out"].reshape(B, S, D)
```

```python
import numpy as np
import concourse.bass as bass
from concourse import mybir
from contextlib import ExitStack

F32 = mybir.dt.float32
BF16 = mybir.dt.bfloat16
I32 = mybir.dt.int32
U32 = mybir.dt.uint32
U8 = mybir.dt.uint8
F32R = mybir.dt.float32r
ALU = mybir.AluOpType
ACT = mybir.ActivationFunctionType
AX = mybir.AxisListType.X

P = 128
B, S, D = 128, 64, 256
TOK = B * S
NT = TOK // P
DC = D // P
H = 16
HD0 = D // H
HD1 = 64
QK1 = 2 * H * HD1
V1 = H * HD1
MLP = 4 * D
MC = MLP // P
GT = 4
GTOK = GT * P
NG = NT // GT
WQK = QK1 // NG
E = 8
CAP = TOK // E
SH = CAP // P
EPS0, EPS1 = 1e-6, 1e-5
SCALE0, SCALE1 = HD0 ** -0.5, HD1 ** -0.5
HIDE = -1e30
HIGH = -4096
NOSLOT = 4096.0

C_ID, C_UP, C_SAME, C_IOTA = 0, P, 2 * P, 3 * P
C_HEAD = 4 * P
C_PICK = C_HEAD + 8
C_P = C_PICK + 8
C_ROW = C_P + 1
C_GROW = C_ROW + 8
BITS = 30
PAIRS = BITS // 2
C_TRY = C_GROW + 8
C_TAKE = C_TRY + 4 * (PAIRS + 1)
C_ALL = C_TAKE + 3 * PAIRS


def constants():
    c = np.zeros((P, C_ALL), np.float32)
    p = np.arange(P)
    c[:, C_ID:C_ID + P] = np.eye(P)
    c[:, C_UP:C_UP + P] = p[:, None] < p[None, :]
    c[:, C_SAME:C_SAME + P] = p[:, None] // 16 == p[None, :] // 16
    c[:, C_IOTA:C_IOTA + P] = p[None, :]
    c[:, C_HEAD:C_HEAD + 8] = p[:, None] // 16 == np.arange(8)[None, :]
    c[:, C_PICK:C_PICK + 8] = p[:, None] == 16 * np.arange(8)[None, :]
    c[:, C_P] = p
    for j in range(8):
        c[j, C_ROW + j], c[8 + j, C_ROW + j] = P, 1
        c[j, C_GROW + j], c[8 + j, C_GROW + j] = 1, NT
    for j in range(PAIRS):
        b = 4.0 ** (PAIRS - 1 - j)
        c[:, C_TRY + 4 * j:C_TRY + 4 * j + 3] = b, 2 * b, 3 * b
        c[:, C_TAKE + 3 * j:C_TAKE + 3 * j + 3] = b, 3 * b, b
    return c


def pipeline(eng, step, n, before, after):
    def edge(i):
        step(i, lambda k: 0 <= i + k < n)
    for i in range(-before, after):
        edge(i)
    with eng.Fori(after, n - before) as i:
        step(i, lambda k: True)
    for i in range(n - before, n + after):
        edge(i)


def pipeline_by(by, eng, step, n, before, after):
    def edge(i):
        step(i, lambda k: 0 <= i + k < n, i % by)
    first = after + -after % by
    last = n - before - (n - before - first) % by
    for i in range(-before, first):
        edge(i)
    with eng.Fori(0, (last - first) // by) as turn:
        for phase in range(by):
            step(by * turn + first + phase, lambda k: True, phase)
    for i in range(last, n + after):
        edge(i)


def later(t):
    return not isinstance(t, int) or t > 0


def block_of(PT, b_pt, half, b, e):
    to = PT[b * S:(b + 1) * S, half * 8:half * 8 + 8, b * S:(b + 1) * S]
    src = b_pt[e * S:(e + 1) * S, half * 4 * P:(half + 1) * 4 * P].rearrange("p (j q) -> p j q", q=P)
    return to.rearrange("p (j e) q -> p e j q", e=2)[:, e], src[:, :, b * S:(b + 1) * S]


def split_product(tensor, to, w_hi, w_lo, x_hi, x_lo, start, stop):
    tensor.matmul(to, w_lo, x_hi, start=start, stop=False)
    tensor.matmul(to, w_hi, x_lo, start=False, stop=False)
    return tensor.matmul(to, w_hi, x_hi, start=False, stop=stop)


class Mem:

    def __init__(self, nc, ctx):
        self.nc, self.ctx, self.sems = nc, ctx, []

    def sb(self, name, shape, dt=F32):
        return self.ctx.enter_context(self.nc.sbuf_tensor(name, shape, dt))

    def ps(self, name, cols):
        return self.ctx.enter_context(self.nc.psum_tensor(name, [P, cols], F32))

    def sem(self, name):
        self.sems.append(self.nc.alloc_semaphore(name))
        return self.sems[-1]

    def clear(self):
        self.nc.all_engine_barrier()
        self.nc.clear_and_free_semaphores(self.sems)
        self.nc.all_engine_barrier()


def setup_phase(nc, a, g):
    with ExitStack() as ctx:
        m = Mem(nc, ctx)
        wada = m.sb("wada", [P, DC, 6 * D])
        wada1 = m.sb("wada1", [P, DC, D])
        cT = m.sb("cT", [P, DC, B])
        sT = m.sb("sT", [P, DC, B])
        adab = m.sb("adab", [P, 4 * DC])
        bada1 = m.sb("bada1", [P, DC])
        ln1b = m.sb("ln1b", [P, DC])
        gbias = m.sb("gbias", [P, 2 * D])
        gates = m.sb("gates", [P, 2 * D])
        mask_keys = m.sb("mask_keys", [P, NT, S], U8)
        mask_rows = m.sb("mask_rows", [P, NT], U8)
        keysf = m.sb("keysf", [P, NT, S])
        hide = m.sb("hide", [P, NT])
        shb = m.sb("shb", [P, DC])
        pt = [m.ps(f"pmod{j}", 4 * P) for j in range(2)]
        pg = [m.ps(f"pgate{j}", 4 * P) for j in range(2)]
        loaded_c, loaded_w, loaded_b, loaded_m = (m.sem(n) for n in
                                                  ("loaded_c", "loaded_w", "loaded_b", "loaded_m"))
        silu_done, table_mm, table_out = m.sem("silu_done"), m.sem("table_mm"), m.sem("table_out")
        gate_mm, gate_out, gate_saved = m.sem("gate_mm"), m.sem("gate_out"), m.sem("gate_saved")
        keys_f, hidden_done = m.sem("keys_f"), m.sem("hidden_done")
        cleared, shift_bias = m.sem("cleared"), m.sem("shift_bias")
        parts = [(g.sh_a, 0, 0), (g.sc_a, 1, 0), (g.sh_m, 3, 1), (g.sc_m, 4, 1)]
        jobs = [(tab, k, c, n) for n, (tab, k, _) in enumerate(parts) for c in range(DC)]
        jobs += [(g.sh_1, None, c, 4) for c in range(DC)]
        with nc.Block() as block:
            @block.sync
            def _(sp):
                sp.dma_start(cT[:, :, :], a["condT"]).then_inc(loaded_c, 16)
                for s in range(2):
                    sp.dma_start(mask_keys[s * S:(s + 1) * S, :, :],
                                 a["mask"].rearrange("(t s) k -> s t k", s=2)[s:s + 1]
                                 .to_broadcast([S, NT, S])).then_inc(loaded_m, 16)
                sp.dma_start(mask_rows[:, :], a["maskT"]).then_inc(loaded_m, 16)
                sp.dma_start(wada[:, :, :], a["ada_w"]).then_inc(loaded_w, 16)
                sp.dma_start(wada1[:, :, :], a["ada1_w"]).then_inc(loaded_w, 16)
                sp.dma_start(adab[:, :], a["ada_b"]).then_inc(loaded_b, 16)
                sp.dma_start(bada1[:, :], a["ada1_b"]).then_inc(loaded_b, 16)
                sp.dma_start(ln1b[:, :], a["ln1_b"]).then_inc(loaded_b, 16)
                for j, k in enumerate((2, 5)):
                    sp.dma_start(gbias[:, j * D:(j + 1) * D],
                                 a["ada_row"][:, k * D:(k + 1) * D].to_broadcast([P, D])).then_inc(loaded_b, 16)
                for w, n in ((g.wqkv0, "qkv0_w"), (g.wproj0, "proj0_w"), (g.qkb0, "qk0_b"), (g.ln1g, "ln1_g")):
                    sp.dma_start(w, a[n]).then_inc(g.loaded, 16)
                sp.dma_start(g.vb0, a["v0_b"]).then_inc(g.loaded, 16)
                sp.dma_start(g.pb0, a["proj0_row"].to_broadcast([P, D])).then_inc(g.loaded, 16)
                sp.dma_start(g.cst, a["consts"]).then_inc(g.loaded, 16)
                sp.wait_ge(g.loaded, 16 * 7)
                sp.wait_ge(gate_out, 2)
                sp.dma_start(g.gate_dram, gates[:, :]).then_inc(gate_saved, 16)
                sp.wait_ge(gate_saved, 16)

            @block.gpsimd
            def _(pool):
                nc.gpsimd.memset(g.PT[:, :, :], 0.0).then_inc(cleared, 1)
                nc.gpsimd.memset(g.vm[:, :, :, :, :], 0.0).then_inc(cleared, 1)
                nc.gpsimd.memset(g.mhalf[:, :], -0.5).then_inc(cleared, 1)

            @block.scalar
            def _(act):
                act.wait_ge(loaded_c, 16)
                nc.scalar.activation(sT[:, :, :], cT[:, :, :], ACT.Silu).then_inc(silu_done, 1)

            @block.tensor
            def _(pe):
                pe.wait_ge(silu_done, 1)
                pe.wait_ge(loaded_w, 32)
                for n, (tab, k, c, _) in enumerate(jobs):
                    if n >= 2:
                        pe.wait_ge(table_out, n - 1)
                    for kc in range(DC):
                        w = wada1[:, kc, c * P:(c + 1) * P] if k is None else \
                            wada[:, kc, k * D + c * P:k * D + (c + 1) * P]
                        last = nc.tensor.matmul(pt[n % 2][:, 0:P], w, sT[:, kc, :],
                                                start=(kc == 0), stop=(kc == DC - 1))
                    last.then_inc(table_mm, 1)
                for j, k in enumerate((2, 5)):
                    for kc in range(DC):
                        last = nc.tensor.matmul(pg[j][:, 0:D], sT[:, kc, :],
                                                wada[:, kc, k * D:(k + 1) * D],
                                                start=(kc == 0), stop=(kc == DC - 1))
                    last.then_inc(gate_mm, 1)

            @block.vector
            def _(dve):
                dve.wait_ge(loaded_m, 48)
                nc.vector.tensor_scalar(keysf[:, :, :], mask_keys[:, :, :], -1.0, None, ALU.add).then_inc(keys_f, 1)
                nc.vector.tensor_scalar(g.mrow, mask_rows[:, :], 1.0, None, ALU.mult).then_inc(keys_f, 1)
                nc.vector.tensor_scalar(hide[:, :], mask_rows[:, :], -HIDE, None, ALU.mult).then_inc(keys_f, 1)
                dve.wait_ge(keys_f, 3)
                nc.vector.tensor_tensor(g.hidden, keysf[:, :, :],
                                        hide[:, :].unsqueeze(2).to_broadcast([P, NT, S]), ALU.mult)\
                    .then_inc(hidden_done, 1)
                dve.wait_ge(loaded_b, 16 * 5)
                nc.vector.tensor_tensor(shb[:, :], bada1[:, :], ln1b[:, :], ALU.add).then_inc(shift_bias, 1)
                dve.wait_ge(shift_bias, 1)
                for n, (tab, k, c, q) in enumerate(jobs):
                    dve.wait_ge(table_mm, n + 1)
                    if k is None:
                        ins = nc.vector.tensor_scalar(tab[:, c, :], pt[n % 2][:, 0:P], shb[:, c:c + 1], None, ALU.add)
                    else:
                        ins = nc.vector.tensor_scalar(tab[:, c, :], pt[n % 2][:, 0:P],
                                                      adab[:, 2 * q + c:2 * q + c + 1],
                                                      float(q % 2), ALU.add, ALU.add)
                    ins.then_inc(table_out, 1)
                for j in range(2):
                    dve.wait_ge(gate_mm, j + 1)
                    nc.vector.tensor_tensor(gates[:, j * D:(j + 1) * D], pg[j][:, 0:D],
                                            gbias[:, j * D:(j + 1) * D], ALU.add).then_inc(gate_out, 1)
        m.clear()


def attention0_phase(nc, a, g):
    with ExitStack() as ctx:
        m = Mem(nc, ctx)
        xhat = m.sb("a0_xhat", [P, D])
        st = m.sb("a0_st", [P, 6])
        mv = m.sb("a0_mv", [P, 2])
        veps = m.sb("a0_veps", [P, 1])
        rstd = m.sb("a0_rstd", [P, 1])
        hT = m.sb("a0_hT", [P, DC, P])
        qT = m.sb("a0_qT", [P, 2, DC, P])
        kT = m.sb("a0_kT", [P, DC, P])
        kbd = m.sb("a0_kbd", [P, DC, 2, 8, S])
        pr = m.sb("a0_p", [P, 2, H, S])
        mx = m.sb("a0_mx", [P, H])
        sm = m.sb("a0_sm", [P, H])
        rs = m.sb("a0_rs", [P, H])
        oT = m.sb("a0_oT", [P, DC, P])
        gt = m.sb("a0_gate", [P, D])
        tmp = m.sb("a0_tmp", [P, D])
        w1, w1hi = m.sb("a0_w1", [P, DC, MLP]), m.sb("a0_w1hi", [P, DC, MLP], I32)
        w2, w2hi = m.sb("a0_w2", [P, MC, D]), m.sb("a0_w2hi", [P, MC, D], I32)
        tmp1 = m.sb("a0_tmp1", [P, D])
        tmp2 = m.sb("a0_tmp2", [P, D])
        b_qk, b_vt = m.ps("a0_bqk", 4 * P), m.ps("a0_bvt", 4 * P)
        VB = 4
        b_s, b_pt = m.ps("a0_bs", H * S), m.ps("a0_bpt", H * S)
        b_o, b_pj = m.ps("a0_bo", 4 * P), m.ps("a0_bpj", 4 * P)
        names = ("x_in stats aggr eps rstd xhat xT hT qk v q_out k_out kbd vm s scored maxed "
                 "shifted exped summed recip probs pT pT_out o oT proj proj_out p1 p2 res gate held "
                 "w_in whi w_hi w_lo").split()
        s = {n: m.sem("a0_" + n) for n in names}
        ident = g.cst[:, C_ID:C_ID + P]
        PT = g.PT

        with nc.Block() as block:
            @block.sync
            def _(sp):
                AHEAD = 8

                def load_x(t):
                    if later(t):
                        sp.wait_ge(s["x_in"], 16 * t)
                    sp.dma_start(g.X[:, t, :], a["x"][t]).then_inc(s["x_in"], 16)

                def load_gates(t):
                    if later(t):
                        sp.wait_ge(s["p2"], t)
                    for b in range(2):
                        sp.dma_start(gt[b * S:(b + 1) * S, :],
                                     g.gate_dram[bass.ds(2 * t + b, 1), 0:D].to_broadcast([S, D]))\
                            .then_inc(s["gate"], 16)
                for t in range(AHEAD):
                    load_x(t)
                load_gates(0)
                sp.dma_start(w1[:, :, :], a["fc1_0_w"]).then_inc(s["w_in"], 16)
                sp.dma_start(w2[:, :, :], a["fc2_0_w"]).then_inc(s["w_in"], 16)
                with sp.Fori(1, NT - AHEAD + 1) as t:
                    load_x(t + AHEAD - 1)
                    load_gates(t)
                with sp.Fori(NT - AHEAD + 1, NT) as t:
                    load_gates(t)

            @block.scalar
            def _(act):
                def step(i, has, turn):
                    def pT_out(half):
                        if half == 0:
                            act.wait_ge(s["pT"], i - 2)
                            if later(i - 3):
                                act.wait_ge(s["o"], i - 3)
                        for b in range(2):
                            for e in range(2):
                                last = nc.scalar.copy(*block_of(PT, b_pt, half, b, e))
                        last.then_inc(s["pT_out"], 1)

                    if has(-4):
                        act.wait_ge(s["proj"], i - 3)
                        if later(i - 4):
                            act.wait_ge(s["p1"], i - 4)
                        nc.scalar.copy(tmp[:, :], b_pj[:, 0:D]).then_inc(s["proj_out"], 1)
                    if has(-3):
                        pT_out(0)
                    if has(0):
                        act.wait_ge(s["qk"], i + 1)
                        if later(i):
                            act.wait_ge(s["kbd"], i)
                        for c in range(DC):
                            last = nc.scalar.activation(kT[:, c, :], b_qk[:, (DC + c) * P:(DC + c + 1) * P],
                                                        ACT.Identity, bias=g.qkb0[:, DC + c:DC + c + 1])
                        last.then_inc(s["k_out"], 1)
                        if later(i) and later(i - 1):
                            act.wait_ge(s["s"], i - 1)
                        for c in range(DC):
                            last = nc.scalar.activation(qT[:, turn % 2, c, :], b_qk[:, c * P:(c + 1) * P], ACT.Identity,
                                                        bias=g.qkb0[:, c:c + 1])
                        last.then_inc(s["q_out"], 1)
                        act.wait_ge(s["v"], i + 1)
                        if later(i) and has(-4):
                            act.wait_ge(s["o"], i - 3)
                        for e in range(2):
                            last = nc.scalar.copy(
                                g.vm[:, turn, e, :, e * HD0:(e + 1) * HD0],
                                b_vt[:, 0:D].rearrange("p (j e d) -> p e j d", e=2, d=HD0)[:, e])
                        last.then_inc(s["vm"], 1)
                    if has(-3):
                        pT_out(1)
                    if has(1):
                        act.wait_ge(s["xT"], i + 2)
                        for c in range(DC):
                            for b in range(2):
                                col = bass.ds(2 * (i + 1) + b, 1)
                                last = nc.scalar.activation(hT[:, c, b * S:(b + 1) * S],
                                                            b_vt[:, D + c * P + b * S:D + c * P + (b + 1) * S],
                                                            ACT.Identity, scale=g.sc_a[:, c, col],
                                                            bias=g.sh_a[:, c, col])
                        last.then_inc(s["hT"], 1)
                    if has(-3):
                        act.wait_ge(s["o"], i - 2)
                        if later(i - 3):
                            act.wait_ge(s["proj"], i - 3)
                        for c in range(DC):
                            last = nc.scalar.activation(oT[:, c, :], b_o[:, c * P:(c + 1) * P], ACT.Identity,
                                                        bias=g.vb0[:, c:c + 1])
                        last.then_inc(s["oT"], 1)
                    if has(-1):
                        act.wait_ge(s["shifted"], i)
                        pa = pr[:, (turn - 1) % 2, :, :]
                        nc.scalar.activation(pa, pa, ACT.Exp, scale=SCALE0).then_inc(s["exped"], 1)
                pipeline_by(VB, act, step, NT, 1, 5)
                act.wait_ge(s["whi"], 2)
                nc.scalar.copy(g.w1_hi, w1hi[:, :, :].bitcast(F32)).then_inc(s["w_hi"], 1)
                nc.scalar.copy(g.w2_hi, w2hi[:, :, :].bitcast(F32)).then_inc(s["w_hi"], 1)
                act.wait_ge(s["w_hi"], 2)

            @block.gpsimd
            def _(pool):
                def step(i, has, turn):
                    if has(2):
                        pool.wait_ge(s["eps"], i + 3)
                        nc.gpsimd.tensor_tensor(rstd[:, :], veps[:, :], g.mhalf[:, 0:1], ALU.pow)\
                            .then_inc(s["rstd"], 1)
                    if has(-4):
                        pool.wait_ge(s["proj_out"], i - 3)
                        if later(i - 4):
                            pool.wait_ge(s["res"], i - 4)
                        nc.gpsimd.tensor_tensor(tmp1[:, :], tmp[:, :], g.pb0, ALU.add).then_inc(s["p1"], 1)
                        pool.wait_ge(s["p1"], i - 3)
                        pool.wait_ge(s["gate"], 32 * (i - 3))
                        nc.gpsimd.tensor_tensor(tmp2[:, :], tmp1[:, :], gt[:, :], ALU.mult).then_inc(s["p2"], 1)
                        pool.wait_ge(s["p2"], i - 3)
                        nc.gpsimd.tensor_tensor(g.X[:, i - 4, :], g.X[:, i - 4, :], tmp2[:, :], ALU.add)\
                            .then_inc(s["res"], 1)
                    if has(0):
                        pool.wait_ge(s["k_out"], i + 1)
                        if later(i):
                            pool.wait_ge(s["s"], i)
                        for c in range(DC):
                            last = nc.gpsimd.tensor_tensor(
                                kbd[:, c, :, :, :],
                                kT[:, c, :].rearrange("p (b k) -> p b k", b=2).unsqueeze(2).to_broadcast([P, 2, 8, S]),
                                g.cst[:, C_HEAD:C_HEAD + 8].unsqueeze(1).unsqueeze(3).to_broadcast([P, 2, 8, S]),
                                ALU.mult)
                        last.then_inc(s["kbd"], 1)
                pipeline_by(VB, pool, step, NT, 2, 5)

            @block.vector
            def _(dve):
                def step(i, has, turn):
                    pa, pb = pr[:, (turn - 1) % 2, :, :], pr[:, turn % 2, :, :]
                    if has(-2):
                        dve.wait_ge(s["exped"], i - 1)
                        nc.vector.reduce_sum(sm[:, :], pb, AX).then_inc(s["summed"], 1)
                    if has(-2):
                        dve.wait_ge(s["summed"], i - 1)
                        nc.vector.reciprocal(rs[:, :], sm[:, :]).then_inc(s["recip"], 1)
                    if has(-2):
                        dve.wait_ge(s["recip"], i - 1)
                        nc.vector.tensor_tensor(pb, pb, rs[:, :].unsqueeze(2).to_broadcast([P, H, S]), ALU.mult)\
                            .then_inc(s["probs"], 1)
                    if has(-1):
                        dve.wait_ge(s["s"], i)
                        if later(i - 1) and has(-3):
                            dve.wait_ge(s["pT"], i - 2)
                        nc.vector.scalar_tensor_tensor(
                            pa, b_s[:, :].rearrange("p (h k) -> p h k", h=H), g.mrow[:, bass.ds(i - 1, 1)],
                            g.hidden[:, i - 1, :].unsqueeze(1).to_broadcast([P, H, S]),
                            ALU.mult, ALU.add).then_inc(s["scored"], 1)
                    if has(-1):
                        dve.wait_ge(s["scored"], i)
                        nc.vector.reduce_max(mx[:, :], pa, AX).then_inc(s["maxed"], 1)
                        dve.wait_ge(s["maxed"], i)
                        nc.vector.tensor_tensor(pa, pa, mx[:, :].unsqueeze(2).to_broadcast([P, H, S]),
                                                ALU.subtract).then_inc(s["shifted"], 1)
                    if has(2):
                        dve.wait_ge(s["rstd"], i + 3)
                        if later(i + 2):
                            dve.wait_ge(s["xT"], i + 2)
                        nc.vector.tensor_scalar(xhat[:, :], g.X[:, i + 2, :], mv[:, 0:1], rstd[:, 0:1],
                                                ALU.subtract, ALU.mult).then_inc(s["xhat"], 1)
                    if has(3):
                        dve.wait_ge(s["x_in"], 16 * (i + 4))
                        nc.vector.bn_stats(st[:, :], g.X[:, i + 3, :]).then_inc(s["stats"], 1)
                        if later(i + 3):
                            dve.wait_ge(s["xhat"], i + 3)
                        dve.wait_ge(s["stats"], i + 4)
                        dve.sem_inc(s["held"], 1)
                        nc.vector.bn_aggr(mv[:, :], st[:, :]).then_inc(s["aggr"], 1)
                        dve.wait_ge(s["aggr"], i + 4)
                        nc.vector.tensor_scalar(veps[:, :], mv[:, 1:2], EPS0, None, ALU.add).then_inc(s["eps"], 1)
                pipeline_by(VB, dve, step, NT, 3, 5)
                dve.wait_ge(s["w_in"], 32)
                for w, hi in ((w1, w1hi), (w2, w2hi)):
                    nc.vector.tensor_single_scalar(hi[:, :, :], w[:, :, :].bitcast(I32), HIGH, ALU.bitwise_and)\
                        .then_inc(s["whi"], 1)
                dve.wait_ge(s["whi"], 2)
                for lo, w, hi in ((g.w1_lo, w1, w1hi), (g.w2_lo, w2, w2hi)):
                    nc.vector.tensor_tensor(lo, w[:, :, :], hi[:, :, :].bitcast(F32), ALU.subtract)\
                        .then_inc(s["w_lo"], 1)
                dve.wait_ge(s["w_lo"], 2)

            @block.tensor
            def _(pe):
                def step(i, has, turn):
                    if has(0):
                        pe.wait_ge(s["hT"], i + 1)
                        if later(i):
                            pe.wait_ge(s["q_out"], i)
                        for n in (2, 3, 0, 1):
                            for kc in range(DC):
                                last = nc.tensor.matmul(b_qk[:, n * P:(n + 1) * P],
                                                        g.wqkv0[:, kc, n * P:(n + 1) * P], hT[:, kc, :],
                                                        start=(kc == 0), stop=(kc == DC - 1))
                        last.then_inc(s["qk"], 1)
                        if later(i):
                            pe.wait_ge(s["vm"], i)
                        for kc in range(DC):
                            last = nc.tensor.matmul(b_vt[:, 0:D], hT[:, kc, :], g.wqkv0[:, kc, 2 * D:3 * D],
                                                    start=(kc == 0), stop=(kc == DC - 1))
                        last.then_inc(s["v"], 1)
                    if has(-1):
                        pe.wait_ge(s["kbd"], i)
                        pe.wait_ge(s["q_out"], i)
                        if later(i - 1):
                            pe.wait_ge(s["scored"], i - 1)
                        for c in range(DC):
                            for b in range(2):
                                last = nc.tensor.matmul(b_s[b * S:(b + 1) * S, c * 512:(c + 1) * 512],
                                                        qT[:, (turn - 1) % 2, c, b * S:(b + 1) * S],
                                                        kbd[:, c, b, :, :].rearrange("p h k -> p (h k)"),
                                                        start=True, stop=True)
                        last.then_inc(s["s"], 1)
                    if has(1):
                        pe.wait_ge(s["xhat"], i + 2)
                        if has(0):
                            pe.wait_ge(s["vm"], i + 1)
                        for c in range(DC):
                            last = nc.tensor.transpose(b_vt[:, D + c * P:D + (c + 1) * P],
                                                       xhat[:, c * P:(c + 1) * P], ident)
                        last.then_inc(s["xT"], 1)
                    if has(-3):
                        if later(i - 3):
                            pe.wait_ge(s["oT"], i - 3)
                        for j in range(H // 2):
                            r, c = j % 4, j // 4
                            if r == 0:
                                pe.wait_ge(s["pT_out"], 2 * (i - 3) + c + 1)
                            for e in range(2):
                                last = nc.tensor.matmul(b_o[32 * r:32 * r + 32, c * P:(c + 1) * P],
                                                        g.vm[:, (turn - 3) % VB, e, j, :], PT[:, 2 * j + e, :],
                                                        start=(e == 0), stop=(e == 1))
                        last.then_inc(s["o"], 1)
                    if has(-2):
                        pe.wait_ge(s["probs"], i - 1)
                        if later(i - 2):
                            pe.wait_ge(s["pT_out"], 2 * (i - 2))
                        for j in range(H // 2):
                            last = nc.tensor.transpose(
                                b_pt[:, j * P:(j + 1) * P],
                                pr[:, turn % 2, 2 * j:2 * j + 2, :].rearrange("p h k -> p (h k)"), ident)
                        last.then_inc(s["pT"], 1)
                    if has(-3):
                        pe.wait_ge(s["oT"], i - 2)
                        if later(i - 3):
                            pe.wait_ge(s["proj_out"], i - 3)
                        for kc in range(DC):
                            last = nc.tensor.matmul(b_pj[:, 0:D], oT[:, kc, :], g.wproj0[:, kc, :],
                                                    start=(kc == 0), stop=(kc == DC - 1))
                        last.then_inc(s["proj"], 1)
                pipeline_by(VB, pe, step, NT, 1, 5)
        m.clear()


def mlp0_phase(nc, a, g):
    with ExitStack() as ctx:
        m = Mem(nc, ctx)
        b1 = m.sb("m0_b1", [P, MC])
        b2 = m.sb("m0_b2", [P, D])
        xhat = m.sb("m0_xhat", [P, GT, D])
        st = m.sb("m0_st", [P, GT, 6])
        mv = m.sb("m0_mv", [P, GT, 2])
        veps = m.sb("m0_veps", [P, GT])
        rstd = m.sb("m0_rstd", [P, GT])
        hm = m.sb("m0_hm", [P, GTOK])
        hhi = hm[:, :].bitcast(I32)
        hT = m.sb("m0_hT", [P, GTOK])
        h_hi, h_lo = (m.sb("m0_h_" + n, [P, DC, GTOK], F32R) for n in ("hi", "lo"))
        UB = 3
        uf = m.sb("m0_u", [P, UB, GTOK])
        uhi = m.sb("m0_uhi", [P, UB, GTOK], I32)
        u_hi, u_lo = (m.sb("m0_u_" + n, [P, MC, GTOK], F32R) for n in ("hi", "lo"))
        gt = m.sb("m0_gate", [P, GT, D])
        tmp = m.sb("m0_tmp", [P, D])
        tmp2 = m.sb("m0_tmp2", [P, D])
        wst = m.sb("wst", [P, DC, WQK])
        wsum = m.sb("wsum", [P, DC, WQK // HD1])
        wmean = m.sb("wmean", [P, DC, WQK // HD1])
        whi = m.sb("whi", [P, DC, WQK], I32)
        b_u = [m.ps(f"m0_bu{j}", GTOK) for j in range(4)]
        b_x = [m.ps(f"m0_bx{j}", GTOK) for j in range(DC)]
        b_y = [m.ps(f"m0_by{j}", GTOK) for j in range(2)]
        names = ("b1 b2 gate stats aggr eps rstd xhat xT h_mul hT hhi h_hi h_lo u gelu uhi u_hi u_lo u_lo_dve "
                 "y p1 p2 res held wst wsum wmean wcen whi wsplit").split()
        s = {n: m.sem("m0_" + n) for n in names}
        ident = g.cst[:, C_ID:C_ID + P]
        BY_DVE = (3, 5, 7)
        BY_POOL = [n for n in range(MC) if n not in BY_DVE]

        def low_done(i, n):
            if n in BY_DVE:
                return s["u_lo_dve"], len(BY_DVE) * i + BY_DVE.index(n) + 1
            return s["u_lo"], len(BY_POOL) * i + BY_POOL.index(n) + 1

        def low(eng, n):
            return eng.tensor_tensor(u_lo[:, n, :], uf[:, n % UB, :], uhi[:, n % UB, :].bitcast(F32), ALU.subtract)

        with nc.Block() as block:
            @block.sync
            def _(sp):
                sp.dma_start(b1[:, :], a["fc1_0_b"]).then_inc(s["b1"], 16)
                sp.dma_start(b2[:, :], a["fc2_0_row"].to_broadcast([P, D])).then_inc(s["b2"], 16)

                def load_gates(i):
                    if later(i):
                        sp.wait_ge(s["p2"], GT * i)
                    for b in range(2):
                        rows = g.gate_dram[bass.ds(2 * GT * i, 2 * GT), D:2 * D]\
                            .rearrange("(t b) d -> b t d", b=2)
                        sp.dma_start(gt[b * S:(b + 1) * S, :, :], rows[b:b + 1].to_broadcast([S, GT, D]))\
                            .then_inc(s["gate"], 16)
                load_gates(0)

                def load_w(i):
                    if later(i):
                        sp.wait_ge(s["wsplit"], 2 * i)
                    sp.dma_start(wst[:, :, :], a["qkv1_w"][:, :, bass.ds(WQK * i, WQK)]).then_inc(s["wst"], 16)
                load_w(0)
                for w, n in ((g.wgate, "gate_w"), (g.qn, "qn"), (g.kn, "kn")):
                    sp.dma_start(w, a[n]).then_inc(g.loaded1, 16)
                with sp.Fori(1, NG) as i:
                    load_gates(i)
                    load_w(i)

            @block.scalar
            def _(act):
                def high(i, n):
                    act.wait_ge(s["uhi"], MC * i + n + 1)
                    nc.scalar.copy(u_hi[:, n, :], uhi[:, n % UB, :].bitcast(F32)).then_inc(s["u_hi"], 1)

                def step(i, has):
                    if has(0):
                        for n in range(MC):
                            act.wait_ge(s["u"], MC * i + n + 1)
                            if n >= UB:
                                act.wait_ge(*low_done(i, n - UB))
                            elif later(i):
                                act.wait_ge(s["u_lo"], len(BY_POOL) * i)
                                act.wait_ge(s["u_lo_dve"], len(BY_DVE) * i)
                            nc.scalar.activation(uf[:, n % UB, :], b_u[n % 4][:, :], ACT.Gelu_apprx_tanh,
                                                 bias=b1[:, n:n + 1]).then_inc(s["gelu"], 1)
                            if n == 1 and later(i):
                                act.wait_ge(s["y"], GT * i)
                            if n:
                                high(i, n - 1)
                        high(i, MC - 1)
                act.wait_ge(s["b1"], 16)
                pipeline(act, step, NG, 2, 1)

            @block.gpsimd
            def _(pool):
                def root(i, has):
                    if has(2):
                        pool.wait_ge(s["eps"], i + 3)
                        nc.gpsimd.tensor_tensor(rstd[:, :], veps[:, :], g.mhalf[:, 0:GT], ALU.pow)\
                            .then_inc(s["rstd"], 1)

                def step(i, has):
                    if has(0):
                        for n in BY_POOL:
                            pool.wait_ge(s["uhi"], MC * i + n + 1)
                            if n == 0 and later(i):
                                pool.wait_ge(s["y"], GT * i)
                            low(nc.gpsimd, n).then_inc(s["u_lo"], 1)
                            if n == GT:
                                root(i, has)
                    if not has(0):
                        root(i, has)
                pipeline(pool, step, NG, 2, 1)

            @block.vector
            def _(dve):
                def stats(i, k):
                    nc.vector.bn_stats(st[:, k, :], g.X[:, GT * i + k, :]).then_inc(s["stats"], 1)

                def variance(i):
                    dve.wait_ge(s["stats"], GT * (i + 1))
                    dve.sem_inc(s["held"], 1)
                    for k in range(GT):
                        nc.vector.bn_aggr(mv[:, k, :], st[:, k, :]).then_inc(s["aggr"], 1)
                    dve.wait_ge(s["aggr"], GT * (i + 1))
                    nc.vector.tensor_scalar(veps[:, :], mv[:, :, 1], EPS0, None, ALU.add).then_inc(s["eps"], 1)

                def normal(i):
                    dve.wait_ge(s["rstd"], i + 1)
                    if later(i):
                        dve.wait_ge(s["xT"], i)
                    for k in range(GT):
                        nc.vector.tensor_scalar(xhat[:, k, :], g.X[:, GT * i + k, :], mv[:, k, 0:1], rstd[:, k:k + 1],
                                                ALU.subtract, ALU.mult).then_inc(s["xhat"], 1)

                def split_w(i):
                    dve.wait_ge(s["wst"], 16 * (i + 1))
                    heads = wst[:, :, :].rearrange("p c (h d) -> p c h d", d=HD1)
                    nc.vector.reduce_sum(wsum[:, :, :], heads, AX).then_inc(s["wsum"], 1)
                    dve.wait_ge(s["wsum"], i + 1)
                    nc.vector.tensor_scalar(wmean[:, :, :], wsum[:, :, :], 1.0 / HD1, None, ALU.mult)\
                        .then_inc(s["wmean"], 1)
                    dve.wait_ge(s["wmean"], i + 1)
                    nc.vector.tensor_tensor(heads, heads, wmean[:, :, :].unsqueeze(3)
                                            .to_broadcast([P, DC, WQK // HD1, HD1]), ALU.subtract)\
                        .then_inc(s["wcen"], 1)
                    dve.wait_ge(s["wcen"], i + 1)
                    nc.vector.tensor_single_scalar(whi[:, :, :], wst[:, :, :].bitcast(I32), HIGH, ALU.bitwise_and)\
                        .then_inc(s["whi"], 1)
                    dve.wait_ge(s["whi"], i + 1)
                    at, part = bass.ds(WQK * i, WQK), whi[:, :, :].bitcast(F32)
                    nc.vector.tensor_copy(g.wq_hi[:, :, at], part).then_inc(s["wsplit"], 1)
                    nc.vector.tensor_tensor(g.wq_lo[:, :, at], wst[:, :, :], part, ALU.subtract)\
                        .then_inc(s["wsplit"], 1)

                def h_chunk(i, c):
                    if c == 0:
                        dve.wait_ge(s["xT"], i + 1)
                    n = DC * i + c
                    if c or later(i):
                        dve.wait_ge(s["h_hi"], n)
                        dve.wait_ge(s["h_lo"], n)
                    nc.vector.tensor_tensor(
                        hm[:, :].rearrange("p (b t) -> p b t", t=S),
                        b_x[c][:, :].rearrange("p (b t) -> p b t", t=S),
                        g.sc_m[:, c, bass.ds(2 * GT * i, 2 * GT)].unsqueeze(2)
                        .to_broadcast([P, 2 * GT, S]), ALU.mult).then_inc(s["h_mul"], 1)
                    dve.wait_ge(s["h_mul"], n + 1)
                    nc.vector.tensor_tensor(
                        hT[:, :].rearrange("p (b t) -> p b t", t=S),
                        hm[:, :].rearrange("p (b t) -> p b t", t=S),
                        g.sh_m[:, c, bass.ds(2 * GT * i, 2 * GT)].unsqueeze(2)
                        .to_broadcast([P, 2 * GT, S]), ALU.add).then_inc(s["hT"], 1)
                    dve.wait_ge(s["hT"], n + 1)
                    nc.vector.tensor_single_scalar(hhi, hT[:, :].bitcast(I32), HIGH, ALU.bitwise_and)\
                        .then_inc(s["hhi"], 1)
                    dve.wait_ge(s["hhi"], n + 1)
                    nc.vector.tensor_copy(h_hi[:, c, :], hm[:, :]).then_inc(s["h_hi"], 1)
                    nc.vector.tensor_tensor(h_lo[:, c, :], hT[:, :], hm[:, :], ALU.subtract)\
                        .then_inc(s["h_lo"], 1)

                def add(i, k):
                    if k == 0:
                        if not later(i):
                            dve.wait_ge(s["b2"], 16)
                        dve.wait_ge(s["gate"], 32 * (i + 1))
                    n = GT * i + k
                    dve.wait_ge(s["y"], n + 1)
                    nc.vector.tensor_tensor(tmp[:, :], b_y[k % 2][:, 0:D], b2[:, :], ALU.add)\
                        .then_inc(s["p1"], 1)
                    dve.wait_ge(s["p1"], n + 1)
                    nc.vector.tensor_tensor(tmp2[:, :], tmp[:, :], gt[:, k, :], ALU.mult)\
                        .then_inc(s["p2"], 1)
                    dve.wait_ge(s["p2"], n + 1)
                    nc.vector.tensor_tensor(g.X[:, n, :], g.X[:, n, :], tmp2[:, :], ALU.add)\
                        .then_inc(s["res"], 1)

                def high(i, n):
                    dve.wait_ge(s["gelu"], MC * i + n + 1)
                    if n >= UB:
                        dve.wait_ge(s["u_hi"], MC * i + n - UB + 1)
                    elif later(i):
                        dve.wait_ge(s["u_hi"], MC * i)
                    nc.vector.tensor_single_scalar(uhi[:, n % UB, :], uf[:, n % UB, :].bitcast(I32), HIGH,
                                                   ALU.bitwise_and).then_inc(s["uhi"], 1)
                    if n in BY_DVE:
                        dve.wait_ge(s["uhi"], MC * i + n + 1)
                        low(nc.vector, n).then_inc(s["u_lo_dve"], 1)

                def step(i, has):
                    for n in range(MC):
                        if has(0):
                            high(i, n)
                        if has(2) and n < GT:
                            stats(i + 2, n)
                        if has(2) and n == GT - 1:
                            if has(1):
                                dve.wait_ge(s["xhat"], GT * (i + 2))
                            variance(i + 2)
                        if has(0) and n == GT:
                            split_w(i)
                    for k in range(GT):
                        if has(1) and k in (0, 2):
                            h_chunk(i + 1, k // 2)
                        if has(2) and k == 3:
                            normal(i + 2)
                        if has(0):
                            add(i, k)
                pipeline(dve, step, NG, 2, 1)
                dve.wait_ge(s["res"], NT)
                dve.wait_ge(s["wsplit"], 2 * NG)

            @block.tensor
            def _(pe):
                def transpose_x(i):
                    pe.wait_ge(s["xhat"], GT * (i + 1))
                    if later(i):
                        pe.wait_ge(s["h_mul"], DC * i)
                    for c in range(DC):
                        for k in range(GT):
                            last = nc.tensor.transpose(b_x[c][:, k * P:(k + 1) * P],
                                                       xhat[:, k, c * P:(c + 1) * P], ident)
                    last.then_inc(s["xT"], 1)

                def step(i, has):
                    if has(0):
                        pe.wait_ge(s["h_hi"], DC * (i + 1))
                        pe.wait_ge(s["h_lo"], DC * (i + 1))
                        for n in range(MC):
                            if n >= 4:
                                pe.wait_ge(s["gelu"], MC * i + n - 3)
                            elif later(i):
                                pe.wait_ge(s["gelu"], MC * i + n - 3)
                            for kc in range(DC):
                                cols = slice(n * P, (n + 1) * P)
                                last = split_product(nc.tensor, b_u[n % 4][:, :], g.w1_hi[:, kc, cols],
                                                     g.w1_lo[:, kc, cols], h_hi[:, kc, :], h_lo[:, kc, :],
                                                     kc == 0, kc == DC - 1)
                            last.then_inc(s["u"], 1)
                    if has(1):
                        transpose_x(i + 1)
                    if has(0):
                        for k in range(GT):
                            n = GT * i + k
                            if k >= 2:
                                pe.wait_ge(s["p1"], n - 1)
                            elif later(i):
                                pe.wait_ge(s["p1"], n - 1)
                            for kc in range(MC):
                                if k == 0:
                                    pe.wait_ge(s["u_hi"], MC * i + kc + 1)
                                    pe.wait_ge(*low_done(i, kc))
                                toks = slice(k * P, (k + 1) * P)
                                last = split_product(nc.tensor, b_y[k % 2][:, 0:D], u_hi[:, kc, toks],
                                                     u_lo[:, kc, toks], g.w2_hi[:, kc, :], g.w2_lo[:, kc, :],
                                                     kc == 0, kc == MC - 1)
                            last.then_inc(s["y"], 1)
                pipeline(pe, step, NG, 2, 1)
        m.clear()


def attention1_phase(nc, a, out, g):
    with ExitStack() as ctx:
        m = Mem(nc, ctx)
        xhat = m.sb("a1_xhat", [P, D])
        st = m.sb("a1_st", [P, 6])
        mv = m.sb("a1_mv", [P, 2])
        veps = m.sb("a1_veps", [P, 1])
        rstd = m.sb("a1_rstd", [P, 1])
        hT = m.sb("a1_hT", [P, DC, P])
        hhi = m.sb("a1_hhi", [P, DC, P], I32)
        h_hi, h_lo = m.sb("a1_h_hi", [P, DC, P], F32R), m.sb("a1_h_lo", [P, DC, P], F32R)
        sq = m.sb("a1_sq", [P, QK1])
        ss = m.sb("a1_ss", [P, 2 * H])
        vq = m.sb("a1_vq", [P, 2 * H])
        rq = m.sb("a1_rq", [P, 2 * H])
        qk = m.sb("a1_qk", [P, QK1])
        qT = m.sb("a1_qT", [P, H // 2, P])
        kbd = m.sb("a1_kbd", [P, H // 2, 2, 2, S])
        v = m.sb("a1_v", [P, V1])
        pr = m.sb("a1_p", [P, H, S])
        mx = m.sb("a1_mx", [P, H])
        sm = m.sb("a1_sm", [P, H])
        rs = m.sb("a1_rs", [P, H])
        oT, ohi = sq[:, 0:V1], sq[:, V1:2 * V1]
        o_hi, o_lo = (m.sb("a1_o_" + n, [P, V1], F32R) for n in ("hi", "lo"))
        xs = m.sb("a1_xs", [P, D])
        xsT = m.sb("a1_xsT", [P, DC, P])
        b_qk = m.ps("a1_bqk", QK1)
        b_a = m.ps("a1_ba", H * S)
        b_b = m.ps("a1_bb", H * S)
        BK = 512
        names = ("stats aggr eps rstd xhat xT hT hhi h_hi h_lo qk sq red vq rq qkn qkT q_out kbd_lo kbd_hi v v_out s maxed "
                 "shifted exped summed recip probs pT pT_out o oT ohi o_hi o_lo proj res xsT xsT_out lg lg_out "
                 "stored cleared wout wv_in wvhi wv wouthi wout_parts").split()
        s = {n: m.sem("a1_" + n) for n in names}
        ident = g.cst[:, C_ID:C_ID + P]
        PT = m.sb("a1_PT", [P, H, P])
        wout = m.sb("a1_wout", [P, H // 2, D])
        wv = PT[:, :, :].rearrange("p h q -> p (h q)").rearrange("p (c n) -> p c n", c=DC)
        wvhi = kbd[:, :, :, :, :].rearrange("p j b e k -> p (j b e k)").rearrange("p (c n) -> p c n", c=DC)
        wouthi = wvhi
        wout_hi, wout_lo = (w.rearrange("p m d -> p (m d)").rearrange("p (j d) -> p j d", d=D)
                            for w in (g.w2_hi, g.w2_lo))
        QG = 4

        with nc.Block() as block:
            @block.sync
            def _(sp):
                def store(t):
                    sp.wait_ge(s["res"], t + 1)
                    sp.dma_start(g.tok_dram[t], xs[:, :]).then_inc(s["stored"], 16)
                    sp.dma_start(out[t], xs[:, :]).then_inc(s["stored"], 16)
                sp.dma_start(wv, a["qkv1_w"][:, :, QK1:]).then_inc(s["wv_in"], 16)
                sp.dma_start(wout[:, :, :], a["out1_w"]).then_inc(s["wout"], 16)
                with sp.Fori(0, NT) as t:
                    store(t)
                sp.wait_ge(s["stored"], 32 * NT)

            @block.scalar
            def _(act):
                def step(i, has):
                    def high(half):
                        act.wait_ge(s["ohi"], 2 * (i - 1) + half + 1)
                        if half == 0 and later(i - 1):
                            act.wait_ge(s["proj"], i - 1)
                        nc.scalar.copy(o_hi[:, half * BK:(half + 1) * BK], ohi[:, half * BK:(half + 1) * BK])\
                            .then_inc(s["o_hi"], 1)
                    if has(0):
                        for n in range(QG):
                            act.wait_ge(s["qk"], QG * i + n + 1)
                            if later(i):
                                act.wait_ge(s["red"], QG * i + n - QG + 1)
                            if n == 0 and later(i) and later(i - 1):
                                act.wait_ge(s["o_lo"], 2 * (i - 1))
                                act.wait_ge(s["o_hi"], 2 * (i - 1))
                            nc.scalar.activation(sq[:, n * BK:(n + 1) * BK], b_qk[:, n * BK:(n + 1) * BK],
                                                 ACT.Square).then_inc(s["sq"], 1)
                            if n == 0 and has(-1):
                                act.wait_ge(s["shifted"], i)
                                nc.scalar.activation(pr[:, :, :], pr[:, :, :], ACT.Exp, scale=SCALE1)\
                                    .then_inc(s["exped"], 1)
                            if n == 2 and has(-2):
                                act.wait_ge(s["lg"], i - 1)
                                nc.scalar.copy(g.lg[:, :, bass.ds(i - 2, 1)], b_b[:, BK:BK + E].unsqueeze(2))\
                                    .then_inc(s["lg_out"], 1)
                    elif has(-1):
                        act.wait_ge(s["shifted"], i)
                        nc.scalar.activation(pr[:, :, :], pr[:, :, :], ACT.Exp, scale=SCALE1)\
                            .then_inc(s["exped"], 1)
                    if not has(0) and has(-2):
                        act.wait_ge(s["lg"], i - 1)
                        nc.scalar.copy(g.lg[:, :, bass.ds(i - 2, 1)], b_b[:, BK:BK + E].unsqueeze(2))\
                            .then_inc(s["lg_out"], 1)
                    if has(-1):
                        act.wait_ge(s["pT"], i)
                        for half in range(2):
                            for b in range(2):
                                for e in range(2):
                                    last = nc.scalar.copy(*block_of(PT, b_b, half, b, e))
                            last.then_inc(s["pT_out"], 1)
                        for half in range(2):
                            act.wait_ge(s["o"], 2 * (i - 1) + half + 1)
                            if has(0) and half == 0:
                                act.wait_ge(s["red"], QG * (i + 1))
                            nc.scalar.copy(oT[:, half * BK:(half + 1) * BK], b_b[:, half * BK:(half + 1) * BK])\
                                .then_inc(s["oT"], 1)
                        high(0)
                    if has(0):
                        act.wait_ge(s["v"], i + 1)
                        nc.scalar.copy(v[:, :], b_a[:, :]).then_inc(s["v_out"], 1)
                    if has(-1):
                        high(1)
                    if has(0):
                        act.wait_ge(s["qkT"], i + 1)
                        nc.scalar.activation(qT[:, :, :].rearrange("p j t -> p (j t)"), b_qk[:, 0:V1], ACT.Identity,
                                             bias=g.qn[:, 1:2], scale=g.qn[:, 0:1]).then_inc(s["q_out"], 1)
                        if not later(i):
                            act.wait_ge(s["cleared"], 2)
                        nc.scalar.activation(kbd[0:S, :, :, 0, :].rearrange("p j b k -> p (j b) k"),
                                             b_qk[0:S, V1:QK1].rearrange("p (n k) -> p n k", k=S), ACT.Identity,
                                             bias=g.kn[0:S, 1:2], scale=g.kn[0:S, 0:1]).then_inc(s["kbd_lo"], 1)
                act.wait_ge(g.loaded1, 16 * 3)
                pipeline(act, step, NT, 0, 3)

            @block.gpsimd
            def _(pool):
                def step(i, has):
                    if has(1):
                        pool.wait_ge(s["eps"], i + 2)
                        nc.gpsimd.tensor_tensor(rstd[:, :], veps[:, :], g.mhalf[:, 0:1], ALU.pow)\
                            .then_inc(s["rstd"], 1)
                    if has(0) and not later(i):
                        pool.wait_ge(s["wv"], 2)
                        pool.wait_ge(s["wout_parts"], 2)
                        nc.gpsimd.memset(kbd[:, :, :, :, :], 0.0).then_inc(s["cleared"], 1)
                        nc.gpsimd.memset(PT[:, :, :], 0.0).then_inc(s["cleared"], 1)
                    if has(0):
                        for n in range(QG):
                            pool.wait_ge(s["vq"], QG * i + n + 1)
                            nc.gpsimd.tensor_tensor(rq[:, 8 * n:8 * n + 8], vq[:, 8 * n:8 * n + 8],
                                                    g.mhalf[:, 0:8], ALU.pow).then_inc(s["rq"], 1)
                pipeline(pool, step, NT, 1, 3)

            @block.vector
            def _(dve):
                def step(i, has):
                    def sums(n):
                        dve.wait_ge(s["sq"], QG * i + n + 1)
                        nc.vector.reduce_sum(ss[:, n * 8:(n + 1) * 8],
                                             sq[:, n * BK:(n + 1) * BK].rearrange("p (h d) -> p h d", d=HD1), AX)\
                            .then_inc(s["red"], 1)

                    def moments(n):
                        dve.wait_ge(s["red"], QG * i + n + 1)
                        nc.vector.tensor_scalar(vq[:, 8 * n:8 * n + 8], ss[:, 8 * n:8 * n + 8], 1.0 / HD1, EPS1,
                                                ALU.mult, ALU.add).then_inc(s["vq"], 1)

                    if has(1):
                        nc.vector.bn_stats(st[:, :], g.X[:, i + 1, :]).then_inc(s["stats"], 1)
                        dve.wait_ge(s["stats"], i + 2)
                    if has(0):
                        dve.wait_ge(s["xT"], i + 1)
                        for c in range(DC):
                            last = nc.vector.scalar_tensor_tensor(
                                hT[:, c, :].rearrange("p (b t) -> p b t", b=2),
                                b_b[:, BK + c * P:BK + (c + 1) * P].rearrange("p (b t) -> p b t", b=2),
                                g.ln1g[:, c:c + 1],
                                g.sh_1[:, c, bass.ds(2 * i, 2)].unsqueeze(2).to_broadcast([P, 2, S]),
                                ALU.mult, ALU.add)
                        last.then_inc(s["hT"], 1)
                        dve.wait_ge(s["hT"], i + 1)
                        nc.vector.tensor_single_scalar(hhi[:, :, :], hT[:, :, :].bitcast(I32), HIGH, ALU.bitwise_and)\
                            .then_inc(s["hhi"], 1)
                        dve.wait_ge(s["hhi"], i + 1)
                        nc.vector.tensor_copy(h_hi[:, :, :], hhi[:, :, :].bitcast(F32)).then_inc(s["h_hi"], 1)
                        nc.vector.tensor_tensor(h_lo[:, :, :], hT[:, :, :], hhi[:, :, :].bitcast(F32), ALU.subtract)\
                            .then_inc(s["h_lo"], 1)
                    if has(0) and not later(i):
                        dve.wait_ge(s["wv_in"], 16)
                        nc.vector.tensor_single_scalar(wvhi.bitcast(I32), wv.bitcast(I32), HIGH, ALU.bitwise_and)\
                            .then_inc(s["wvhi"], 1)
                        dve.wait_ge(s["wvhi"], 1)
                        nc.vector.tensor_copy(g.wv_hi, wvhi).then_inc(s["wv"], 1)
                        nc.vector.tensor_tensor(g.wv_lo, wv, wvhi, ALU.subtract).then_inc(s["wv"], 1)
                        dve.wait_ge(s["wv"], 2)
                        dve.wait_ge(s["wout"], 16)
                        raw = wout[:, :, :].rearrange("p j d -> p (j d)").rearrange("p (c n) -> p c n", c=DC)
                        nc.vector.tensor_single_scalar(wouthi.bitcast(I32), raw.bitcast(I32), HIGH, ALU.bitwise_and)\
                            .then_inc(s["wouthi"], 1)
                        dve.wait_ge(s["wouthi"], 1)
                        for part, op in ((wout_hi, None), (wout_lo, ALU.subtract)):
                            to = part.rearrange("p j d -> p (j d)").rearrange("p (c n) -> p c n", c=DC)
                            (nc.vector.tensor_copy(to, wouthi) if op is None else
                             nc.vector.tensor_tensor(to, raw, wouthi, op)).then_inc(s["wout_parts"], 1)
                    if has(1):
                        nc.vector.bn_aggr(mv[:, :], st[:, :]).then_inc(s["aggr"], 1)
                    if has(-2):
                        dve.wait_ge(s["proj"], i - 1)
                        if later(i - 2):
                            dve.wait_ge(s["stored"], 32 * (i - 2))
                            dve.wait_ge(s["xsT"], i - 2)
                        nc.vector.tensor_tensor(xs[:, :], g.X[:, i - 2, :], b_b[:, 0:D], ALU.add)\
                            .then_inc(s["res"], 1)
                    if has(-1):
                        dve.wait_ge(s["s"], i)
                        nc.vector.reduce_max(mx[:, :], b_a[:, :].rearrange("p (h k) -> p h k", h=H), AX)\
                            .then_inc(s["maxed"], 1)
                        dve.wait_ge(s["maxed"], i)
                        nc.vector.tensor_tensor(pr[:, :, :], b_a[:, :].rearrange("p (h k) -> p h k", h=H),
                                                mx[:, :].unsqueeze(2).to_broadcast([P, H, S]), ALU.subtract)\
                            .then_inc(s["shifted"], 1)
                    if has(0):
                        sums(0)
                        moments(0)
                    if has(1):
                        dve.wait_ge(s["aggr"], i + 2)
                        nc.vector.tensor_scalar(veps[:, :], mv[:, 1:2], EPS1, None, ALU.add).then_inc(s["eps"], 1)
                    if has(-2):
                        dve.wait_ge(s["xsT"], i - 1)
                        nc.vector.tensor_copy(xsT[:, :, :].rearrange("p c t -> p (c t)"), b_b[:, 0:D])\
                            .then_inc(s["xsT_out"], 1)

                    if has(-1):
                        dve.wait_ge(s["exped"], i)
                        nc.vector.reduce_sum(sm[:, :], pr[:, :, :], AX).then_inc(s["summed"], 1)
                        dve.wait_ge(s["summed"], i)
                        nc.vector.reciprocal(rs[:, :], sm[:, :]).then_inc(s["recip"], 1)
                        dve.wait_ge(s["recip"], i)
                        nc.vector.tensor_tensor(pr[:, :, :], pr[:, :, :],
                                                rs[:, :].unsqueeze(2).to_broadcast([P, H, S]), ALU.mult)\
                            .then_inc(s["probs"], 1)
                    if has(0):
                        for n in range(1, QG):
                            sums(n)
                            moments(n)
                    if has(1):
                        dve.wait_ge(s["rstd"], i + 2)
                        if later(i + 1):
                            dve.wait_ge(s["xT"], i + 1)
                        nc.vector.tensor_scalar(xhat[:, :], g.X[:, i + 1, :], mv[:, 0:1], rstd[:, 0:1],
                                                ALU.subtract, ALU.mult).then_inc(s["xhat"], 1)
                    def over_norm(n):
                        if n == 0 and later(i):
                            dve.wait_ge(s["qkT"], i)
                        dve.wait_ge(s["rq"], QG * i + n + 1)
                        nc.vector.tensor_tensor(
                            qk[:, n * BK:(n + 1) * BK].rearrange("p (h d) -> p h d", d=HD1),
                            b_qk[:, n * BK:(n + 1) * BK].rearrange("p (h d) -> p h d", d=HD1),
                            rq[:, 8 * n:8 * n + 8].unsqueeze(2).to_broadcast([P, 8, HD1]), ALU.mult)\
                            .then_inc(s["qkn"], 1)

                    def split_o(half):
                        cols = slice(half * BK, (half + 1) * BK)
                        dve.wait_ge(s["oT"], 2 * (i - 1) + half + 1)
                        nc.vector.tensor_single_scalar(ohi[:, cols].bitcast(I32), oT[:, cols].bitcast(I32), HIGH,
                                                       ALU.bitwise_and).then_inc(s["ohi"], 1)
                        if half == 0 and later(i - 1):
                            dve.wait_ge(s["proj"], i - 1)
                        dve.wait_ge(s["ohi"], 2 * (i - 1) + half + 1)
                        nc.vector.tensor_tensor(o_lo[:, cols], oT[:, cols], ohi[:, cols], ALU.subtract)\
                            .then_inc(s["o_lo"], 1)
                    if has(0):
                        for n in range(QG - 1):
                            over_norm(n)
                    if has(-1):
                        split_o(0)
                    if has(0):
                        over_norm(QG - 1)
                    if has(-1):
                        split_o(1)
                    if has(0):
                        dve.wait_ge(s["qkT"], i + 1)
                        if not later(i):
                            dve.wait_ge(s["cleared"], 1)
                        nc.vector.tensor_scalar(kbd[S:P, :, :, 1, :].rearrange("p j b k -> p (j b) k"),
                                                b_qk[S:P, V1:QK1].rearrange("p (n k) -> p n k", k=S),
                                                g.kn[S:P, 0:1], g.kn[S:P, 1:2], ALU.mult, ALU.add)\
                            .then_inc(s["kbd_hi"], 1)
                dve.wait_ge(g.loaded1, 16 * 3)
                pipeline(dve, step, NT, 1, 3)

            @block.tensor
            def _(pe):
                def step(i, has):
                    if has(-1):
                        pe.wait_ge(s["q_out"], i)
                        pe.wait_ge(s["kbd_lo"], i)
                        pe.wait_ge(s["kbd_hi"], i)
                        pe.wait_ge(s["v_out"], i)
                        for j in range(H // 2):
                            for b in range(2):
                                last = nc.tensor.matmul(b_a[b * S:(b + 1) * S, j * P:(j + 1) * P],
                                                        qT[:, j, b * S:(b + 1) * S],
                                                        kbd[:, j, b, :, :].rearrange("p e k -> p (e k)"),
                                                        start=True, stop=True)
                        last.then_inc(s["s"], 1)

                    def products(n):
                        for kc in range(DC):
                            cols = slice(n * BK, (n + 1) * BK)
                            last = split_product(nc.tensor, b_qk[:, cols], h_hi[:, kc, :], h_lo[:, kc, :],
                                                 g.wq_hi[:, kc, cols], g.wq_lo[:, kc, cols],
                                                 kc == 0, kc == DC - 1)
                        last.then_inc(s["qk"], 1)
                    def values(n):
                        for kc in range(DC):
                            cols = slice(n * BK, (n + 1) * BK)
                            if not later(i):
                                pe.wait_ge(s["wv"], 2)
                            last = split_product(nc.tensor, b_a[:, n * BK:(n + 1) * BK],
                                                 h_hi[:, kc, :], h_lo[:, kc, :],
                                                 g.wv_hi[:, kc, cols], g.wv_lo[:, kc, cols],
                                                 kc == 0, kc == DC - 1)
                        if n == 1:
                            last.then_inc(s["v"], 1)
                    if has(0):
                        pe.wait_ge(s["h_hi"], i + 1)
                        pe.wait_ge(s["h_lo"], i + 1)
                        products(0)
                        products(1)
                    if has(-2):
                        pe.wait_ge(s["res"], i - 1)
                        for c in range(DC):
                            last = nc.tensor.transpose(b_b[:, c * P:(c + 1) * P], xs[:, c * P:(c + 1) * P], ident)
                        last.then_inc(s["xsT"], 1)
                    if has(0):
                        products(2)
                    if has(-2):
                        pe.wait_ge(s["xsT_out"], i - 1)
                        for kc in range(DC):
                            last = nc.tensor.matmul(b_b[:, BK:BK + E], xsT[:, kc, :], g.wgate[:, kc, :],
                                                    start=(kc == 0), stop=(kc == DC - 1))
                        last.then_inc(s["lg"], 1)
                    if has(0):
                        products(3)
                    if has(0):
                        if has(-1):
                            pe.wait_ge(s["shifted"], i)
                        values(0)
                    if has(-1):
                        pe.wait_ge(s["probs"], i)
                        if later(i - 1):
                            pe.wait_ge(s["lg_out"], i - 1)
                        for j in range(H // 2):
                            last = nc.tensor.transpose(b_b[:, j * P:(j + 1) * P],
                                                       pr[:, 2 * j:2 * j + 2, :].rearrange("p h k -> p (h k)"), ident)
                        last.then_inc(s["pT"], 1)
                    if has(0):
                        values(1)
                    if has(-1):
                        for h in range(H):
                            if h % (H // 2) == 0:
                                pe.wait_ge(s["pT_out"], 2 * (i - 1) + h // (H // 2) + 1)
                            r, j = h % 2, h // 2
                            last = nc.tensor.matmul(b_b[r * S:(r + 1) * S, j * P:(j + 1) * P],
                                                    v[:, h * HD1:(h + 1) * HD1], PT[:, h, :],
                                                    start=True, stop=True)
                            if (h + 1) % (H // 2) == 0:
                                last.then_inc(s["o"], 1)
                    if has(0):
                        for j in range(H):
                            if j % QG == 0:
                                pe.wait_ge(s["qkn"], QG * i + j // QG + 1)
                            last = nc.tensor.transpose(b_qk[:, j * P:(j + 1) * P], qk[:, j * P:(j + 1) * P], ident)
                        last.then_inc(s["qkT"], 1)
                    if has(-1):
                        if not later(i - 1):
                            pe.wait_ge(s["wout_parts"], 2)
                        for kc in range(H // 2):
                            if kc % (H // 4) == 0:
                                pe.wait_ge(s["o_hi"], 2 * (i - 1) + kc // (H // 4) + 1)
                                pe.wait_ge(s["o_lo"], 2 * (i - 1) + kc // (H // 4) + 1)
                            rows = slice(kc * P, (kc + 1) * P)
                            last = split_product(nc.tensor, b_b[:, 0:D], o_hi[:, rows], o_lo[:, rows],
                                                 wout_hi[:, kc, :], wout_lo[:, kc, :], kc == 0, kc == H // 2 - 1)
                        last.then_inc(s["proj"], 1)
                    if has(1):
                        pe.wait_ge(s["xhat"], i + 2)
                        for c in range(DC):
                            last = nc.tensor.transpose(b_b[:, BK + c * P:BK + (c + 1) * P],
                                                       xhat[:, c * P:(c + 1) * P], ident)
                        last.then_inc(s["xT"], 1)
                pe.wait_ge(g.loaded1, 16 * 3)
                pipeline(pe, step, NT, 1, 3)
        m.clear()


def route_phase(nc, a, g):
    NE = E * NT
    with ExitStack() as ctx:
        m = Mem(nc, ctx)
        mx = m.sb("r_mx", [P, NT])
        sm = m.sb("r_sm", [P, NT])
        rs = m.sb("r_rs", [P, NT])
        pb = m.sb("r_prob", [P, E, NT])
        pbt = m.sb("r_prob_t", [P, NT, E])
        pbq = m.sb("r_prob_q", [P, 4, E, 16])
        byp = m.sb("r_by_expert", [P, 4 * P])
        junk = m.sb("r_junk", [P, 3, 4 * P])
        cnt = m.sb("r_cnt", [P, 3])
        tryi = m.sb("r_tryi", [P, 4 * (PAIRS + 1)], I32)
        cand = m.sb("r_cand", [P, 4], I32)
        take = m.sb("r_take", [P, 3], I32)
        bits = m.sb("r_bits", [P, 1], I32)
        thr = m.sb("r_thr", [P, P])
        gt, eq = m.sb("r_gt", [P, E, NT], BF16), m.sb("r_eq", [P, E, NT], BF16)
        up, ones = m.sb("r_up", [P, P], BF16), m.sb("r_ones", [P, P], BF16)
        keep = m.sb("r_keep", [P, E, NT])
        inc_g, inc_e = m.sb("r_inc_g", [P, E, NT]), m.sb("r_inc_e", [P, E, NT])
        ag, ae = m.sb("r_ag", [P, E, NT]), m.sb("r_ae", [P, E, NT])
        bg, be = m.sb("r_bg", [P, E, NT]), m.sb("r_be", [P, E, NT])
        ce = m.sb("r_ce", [P, E, NT])
        sg, se = m.sb("r_sg", [P, E, NT]), m.sb("r_se", [P, E, NT])
        slot = m.sb("r_slot", [P, E, NT], I32)
        loi, hii = m.sb("r_loi", [P, E, NT], I32), m.sb("r_hii", [P, E, NT], I32)
        lo, hi = m.sb("r_lo", [P, E, NT], BF16), m.sb("r_hi", [P, E, NT], BF16)
        iota = m.sb("r_iota", [P, P, NT], BF16)
        hot_lo = m.sb("r_hot_lo", [P, 2, P, NT], BF16)
        hot_hi = m.sb("r_hot_hi", [P, NT, SH], BF16)
        pair = m.sb("r_pair", [P, 2, NT, 2 * SH], BF16)
        lists = m.sb("r_lists", [2 * SH, P])
        b_t, b_n, b_l, b_i = (m.ps(f"r_b{n}", 512) for n in "tnli")
        b_pg, b_tg, b_pe, b_te = (m.ps(f"r_b{n}", 512) for n in ("pg", "tg", "pe", "te"))
        names = ("max sub exp sum recip prob prob_t prob_q saved tr by_p count counted take bits cand thr_out thr_in "
                 "masks pre scan slots ints hot_lo iota hot_hi pair pair_p lists lists_out rows rows_out held consts1").split()
        s = {n: m.sem("r_" + n) for n in names}
        cst = g.cst
        b_l = (b_l, b_t)

        def over_tiles(x, n=NT):
            return x.unsqueeze(1).to_broadcast([P, E, n])

        with nc.Block() as block:
            @block.sync
            def _(sp):
                for to, n in ((g.e_w1, "fc1s"), (g.e_w2, "fc2s")):
                    sp.dma_start(to, a[n][0]).then_inc(g.loaded_e, 16)
                sp.dma_start(g.e_b1, a["b1s"]).then_inc(g.loaded_e, 16)
                sp.dma_start(g.e_lnw, a["mlp_ln"]).then_inc(g.loaded_e, 16)
                sp.dma_start(g.e_b2, a["b2s"].to_broadcast([P, E, D])).then_inc(g.loaded_e, 16)
                sp.wait_ge(s["prob_t"], 1)
                sp.dma_start(g.prob_dram, pbt[:, :, :]).then_inc(s["saved"], 16)
                sp.wait_ge(s["cand"], PAIRS + 1)
                sp.dma_start(g.thr_dram.rearrange("a p -> p a"), cand[:, 3:4].bitcast(F32)).then_inc(s["thr_out"], 16)
                sp.wait_ge(s["thr_out"], 16)
                sp.dma_start(thr[:, :], g.thr_dram.to_broadcast([P, P])).then_inc(s["thr_in"], 16)
                sp.wait_ge(s["saved"], 16)

            @block.scalar
            def _(act):
                act.wait_ge(s["sub"], 1)
                nc.scalar.activation(pb[:, :, :], pb[:, :, :], ACT.Exp).then_inc(s["exp"], 1)
                act.wait_ge(s["tr"], 1)
                nc.scalar.copy(byp[:, :], b_t[:, :]).then_inc(s["by_p"], 1)

                def step(e, has, par):
                    if has(0):
                        act.wait_ge(s["hot_hi"], e + 1)
                        if later(e) and later(e - 1):
                            act.wait_ge(s["lists"], e - 1)
                        nc.scalar.activation(pair[:, par, :, SH:2 * SH], hot_hi[:, :, :], ACT.Identity,
                                             scale=cst[:, C_P:C_P + 1]).then_inc(s["pair_p"], 1)
                    if has(-1):
                        act.wait_ge(s["lists"], e)
                        if later(e - 1):
                            act.wait_ge(s["rows"], e - 1)
                        nc.scalar.copy(lists[:, :], b_l[1 - par][0:2 * SH, 0:P]).then_inc(s["lists_out"], 1)
                pipeline_by(2, act, step, E, 0, 2)

            @block.gpsimd
            def _(pool):
                nc.gpsimd.tensor_copy(up[:, :], cst[:, C_UP:C_UP + P]).then_inc(s["consts1"], 1)
                nc.gpsimd.memset(ones[:, :], 1.0).then_inc(s["consts1"], 1)
                nc.gpsimd.memset(keep[:, :, 1:NT], 1.0).then_inc(s["consts1"], 1)
                nc.gpsimd.memset(keep[:, :, 0:1], 0.0).then_inc(s["consts1"], 1)
                nc.gpsimd.tensor_copy(tryi[:, :], cst[:, C_TRY:C_TAKE]).then_inc(s["consts1"], 1)
                def gather_first():
                    pool.wait_ge(s["saved"], 16)
                    pool.wait_ge(s["rows_out"], 1)
                    pool.sem_inc(s["held"], 1)
                    for h in range(2):
                        for to, src, first in ((g.xg, g.tok_dram.rearrange("t p d -> (t p) d"), 0),
                                               (g.pg, g.prob_dram.rearrange("p t e -> (p t) e"), SH)):
                            for k in range(GT):
                                c = first + h * GT + k
                                nc.gpsimd.indirect_dma_start(
                                    to[h][:, k, :], None, src,
                                    bass.IndirectOffsetOnAxis(g.rows[:, 0, c:c + 1], 0)).then_inc(g.gathered[h], 16)
                nc.gpsimd.tensor_copy(iota[:, :, :], cst[:, C_IOTA:C_IOTA + P].unsqueeze(2).to_broadcast([P, P, NT]))\
                    .then_inc(s["iota"], 1)
                gather_first()

            @block.vector
            def _(dve):
                nc.vector.reduce_max(mx[:, :], g.lg[:, :, :].rearrange("p e t -> p t e"), AX).then_inc(s["max"], 1)
                dve.wait_ge(s["max"], 1)
                nc.vector.tensor_tensor(pb[:, :, :], g.lg[:, :, :], over_tiles(mx[:, :]), ALU.subtract)\
                    .then_inc(s["sub"], 1)
                dve.wait_ge(s["exp"], 1)
                nc.vector.reduce_sum(sm[:, :], pb[:, :, :].rearrange("p e t -> p t e"), AX).then_inc(s["sum"], 1)
                dve.wait_ge(s["sum"], 1)
                nc.vector.reciprocal(rs[:, :], sm[:, :]).then_inc(s["recip"], 1)
                dve.wait_ge(s["recip"], 1)
                nc.vector.tensor_tensor(pb[:, :, :], pb[:, :, :], over_tiles(rs[:, :]), ALU.mult)\
                    .then_inc(s["prob"], 1)
                dve.wait_ge(s["prob"], 1)
                nc.vector.tensor_copy(pbq[:, :, :, :], pb[:, :, :].rearrange("p e (b t) -> p b e t", b=4))\
                    .then_inc(s["prob_q"], 1)
                nc.vector.tensor_copy(pbt[:, :, :], pb[:, :, :].rearrange("p e t -> p t e")).then_inc(s["prob_t"], 1)
                dve.wait_ge(s["consts1"], 5)
                nc.vector.tensor_copy(cand[:, :], tryi[:, 0:4]).then_inc(s["cand"], 1)
                dve.wait_ge(s["by_p"], 1)
                with dve.Fori(0, PAIRS // 3) as third:
                    for r in range(3):
                        i = 3 * third + r
                        dve.wait_ge(s["cand"], i + 1)
                        for c in range(3):
                            nc.vector.tensor_scalar(junk[:, c, :], byp[:, :], cand[:, c:c + 1].bitcast(F32), None,
                                                    ALU.is_ge, ALU.add, accum_out=cnt[:, c:c + 1])\
                                .then_inc(s["count"], 1)
                        dve.wait_ge(s["counted"], i + 1)
                        nc.vector.scalar_tensor_tensor(take[:, :], b_n[:, 0:3], float(CAP),
                                                       cst[:, bass.ds(C_TAKE + 3 * i, 3)],
                                                       ALU.is_ge, ALU.mult).then_inc(s["take"], 1)
                        dve.wait_ge(s["take"], i + 1)
                        nc.vector.scalar_tensor_tensor(bits[:, :], take[:, 0:1], take[:, 1:2], take[:, 2:3],
                                                       ALU.bitwise_xor, ALU.bitwise_xor).then_inc(s["bits"], 1)
                        dve.wait_ge(s["bits"], i + 1)
                        nc.vector.scalar_tensor_tensor(cand[:, :], tryi[:, bass.ds(4 * i + 4, 4)], bits[:, :],
                                                       cand[:, 3:4].to_broadcast([P, 4]),
                                                       ALU.bitwise_xor, ALU.bitwise_xor).then_inc(s["cand"], 1)
                dve.wait_ge(s["thr_in"], 16)
                t8 = thr[:, :].rearrange("p (e t) -> p e t", t=16)[:, :, 0:1].to_broadcast([P, E, NT])
                nc.vector.tensor_tensor(gt[:, :, :], pb[:, :, :], t8, ALU.is_gt).then_inc(s["masks"], 1)
                nc.vector.tensor_tensor(eq[:, :, :], pb[:, :, :], t8, ALU.is_equal).then_inc(s["masks"], 1)
                dve.wait_ge(s["pre"], 4)
                for n, (inc, tot) in enumerate(((inc_g, b_tg), (inc_e, b_te))):
                    nc.vector.tensor_tensor_scan(inc[:, :, :].rearrange("p e t -> p (e t)"),
                                                 keep[:, :, :].rearrange("p e t -> p (e t)"), tot[:, :], 0.0,
                                                 ALU.mult, ALU.add).then_inc(s["scan"], 1)
                dve.wait_ge(s["scan"], 2)
                grid = "p (e t) -> p e t"
                nc.vector.tensor_tensor(ag[:, :, :], inc_g[:, :, :], b_tg[:, :].rearrange(grid, e=E), ALU.subtract)\
                    .then_inc(s["slots"], 1)
                nc.vector.tensor_tensor(ae[:, :, :], inc_e[:, :, :], b_te[:, :].rearrange(grid, e=E), ALU.subtract)\
                    .then_inc(s["slots"], 1)
                dve.wait_ge(s["slots"], 2)
                nc.vector.tensor_tensor(bg[:, :, :], ag[:, :, :], b_pg[:, :].rearrange(grid, e=E), ALU.add)\
                    .then_inc(s["slots"], 1)
                nc.vector.tensor_tensor(be[:, :, :], ae[:, :, :], b_pe[:, :].rearrange(grid, e=E), ALU.add)\
                    .then_inc(s["slots"], 1)
                dve.wait_ge(s["slots"], 4)
                nc.vector.scalar_tensor_tensor(sg[:, :, :], bg[:, :, :], -NOSLOT, gt[:, :, :], ALU.add, ALU.mult)\
                    .then_inc(s["slots"], 1)
                nc.vector.tensor_tensor(ce[:, :, :], be[:, :, :], inc_g[:, :, NT - 1:NT].to_broadcast([P, E, NT]),
                                        ALU.add).then_inc(s["slots"], 1)
                dve.wait_ge(s["slots"], 6)
                nc.vector.scalar_tensor_tensor(se[:, :, :], ce[:, :, :], -NOSLOT, eq[:, :, :], ALU.add, ALU.mult)\
                    .then_inc(s["slots"], 1)
                dve.wait_ge(s["slots"], 7)
                nc.vector.scalar_tensor_tensor(slot[:, :, :], sg[:, :, :], NOSLOT, se[:, :, :], ALU.add, ALU.add)\
                    .then_inc(s["slots"], 1)
                dve.wait_ge(s["slots"], 8)
                nc.vector.tensor_single_scalar(loi[:, :, :], slot[:, :, :], P - 1, ALU.bitwise_and)\
                    .then_inc(s["ints"], 1)
                nc.vector.tensor_single_scalar(hii[:, :, :], slot[:, :, :], 7, ALU.logical_shift_right)\
                    .then_inc(s["ints"], 1)
                dve.wait_ge(s["ints"], 2)
                nc.vector.tensor_copy(lo[:, :, :], loi[:, :, :]).then_inc(s["ints"], 1)
                nc.vector.tensor_copy(hi[:, :, :], hii[:, :, :]).then_inc(s["ints"], 1)
                dve.wait_ge(s["ints"], 4)

                dve.wait_ge(s["iota"], 1)

                def step(e, has, par):
                    if has(0):
                        if later(e):
                            dve.wait_ge(s["pair"], e)
                            dve.wait_ge(s["pair_p"], e)
                        nc.vector.tensor_tensor(hot_hi[:, :, :], cst[:, C_IOTA:C_IOTA + SH].unsqueeze(1)
                                                .to_broadcast([P, NT, SH]),
                                                hi[:, bass.ds(e, 1), :].rearrange("p e t -> p (e t)").unsqueeze(2)
                                                .to_broadcast([P, NT, SH]), ALU.is_equal).then_inc(s["hot_hi"], 1)
                        if later(e) and later(e - 1):
                            dve.wait_ge(s["lists"], e - 1)
                        nc.vector.tensor_tensor(hot_lo[:, par, :, :], iota[:, :, :],
                                                lo[:, bass.ds(e, 1), :].to_broadcast([P, P, NT]),
                                                ALU.is_equal).then_inc(s["hot_lo"], 1)
                        dve.wait_ge(s["hot_hi"], e + 1)
                        nc.vector.tensor_tensor(pair[:, par, :, 0:SH], hot_hi[:, :, :],
                                                cst[:, C_IOTA:C_IOTA + NT].unsqueeze(2).to_broadcast([P, NT, SH]),
                                                ALU.mult).then_inc(s["pair"], 1)
                    if has(-2):
                        dve.wait_ge(s["rows"], e - 1)
                        nc.vector.tensor_copy(g.rows[:, bass.ds(e - 2, 1), :], b_i[:, 0:2 * SH].unsqueeze(1))\
                            .then_inc(s["rows_out"], 1)
                pipeline_by(2, dve, step, E, 0, 2)
                dve.wait_ge(s["rows_out"], E)

            @block.tensor
            def _(pe):
                pe.wait_ge(s["prob_q"], 1)
                for b in range(4):
                    last = nc.tensor.transpose(b_t[:, b * P:(b + 1) * P],
                                               pbq[:, b, :, :].rearrange("p e t -> p (e t)"),
                                               cst[:, C_ID:C_ID + P])
                last.then_inc(s["tr"], 1)
                with pe.Fori(0, PAIRS) as i:
                    pe.wait_ge(s["count"], 3 * (i + 1))
                    nc.tensor.matmul(b_n[:, 0:3], cst[:, C_SAME:C_SAME + P], cnt[:, :], start=True, stop=True)\
                        .then_inc(s["counted"], 1)
                pe.wait_ge(s["consts1"], 5)
                pe.wait_ge(s["masks"], 2)
                for w, mask, to in ((up, gt, b_pg), (ones, gt, b_tg), (up, eq, b_pe), (ones, eq, b_te)):
                    nc.tensor.matmul(to[:, :], w[:, :], mask[:, :, :].rearrange("p e t -> p (e t)"),
                                     start=True, stop=True).then_inc(s["pre"], 1)

                def step(e, has, par):
                    if has(0):
                        pe.wait_ge(s["pair"], e + 1)
                        pe.wait_ge(s["pair_p"], e + 1)
                        pe.wait_ge(s["hot_lo"], e + 1)
                        if later(e) and later(e - 1):
                            pe.wait_ge(s["lists_out"], e - 1)
                        for t in range(NT):
                            last = nc.tensor.matmul(b_l[par][0:2 * SH, 0:P], pair[:, par, t, :],
                                                    hot_lo[:, par, :, t], start=(t == 0), stop=(t == NT - 1))
                        last.then_inc(s["lists"], 1)
                    if has(-1):
                        pe.wait_ge(s["lists_out"], e)
                        if later(e - 1):
                            pe.wait_ge(s["rows_out"], e - 1)
                        nc.tensor.matmul(b_i[:, 0:2 * SH], lists[:, :], cst[0:2 * SH, C_ROW:C_ROW + 2 * SH],
                                         start=True, stop=True).then_inc(s["rows"], 1)
                pipeline_by(2, pe, step, E, 0, 2)
        m.clear()


def experts_phase(nc, a, out, g):
    with ExitStack() as ctx:
        m = Mem(nc, ctx)
        w1, w2, b2, lnw = g.e_w1, g.e_w2, g.e_b2, g.e_lnw
        w1_hi, w1_lo = (m.sb("e_w1_" + n, [P, DC, MLP], F32R) for n in ("hi", "lo"))
        w2_hi, w2_lo = (m.sb("e_w2_" + n, [P, MC, D], F32R) for n in ("hi", "lo"))
        free = g.X[:, :, :].rearrange("p t d -> p (t d)")
        UB = 3
        sizes = (DC * MLP, MC * D, DC * GTOK, DC * GTOK, UB * GTOK, UB * GTOK, GT * D, GT * D, GT * D)
        starts = [sum(sizes[:n]) for n in range(len(sizes))]
        w1hi, w2hi, hhi, hT, uf, uhi, xhat, ys0, ys1 = (free[:, at:at + n] for at, n in zip(starts, sizes))
        w1hi = w1hi.rearrange("p (c m) -> p c m", c=DC)
        w2hi = w2hi.rearrange("p (c d) -> p c d", c=MC)
        hhi, hT = (t.rearrange("p (c t) -> p c t", c=DC) for t in (hhi, hT))
        uf, uhi = (t.rearrange("p (n t) -> p n t", n=UB) for t in (uf, uhi))
        xhat, ys0, ys1 = (t.rearrange("p (k d) -> p k d", k=GT) for t in (xhat, ys0, ys1))
        ys = (ys0, ys1)
        u_hi, u_lo = (m.sb("e_u_" + n, [P, MC, GTOK], F32R) for n in ("hi", "lo"))
        h_hi, h_lo = (m.sb("e_h_" + n, [P, DC, GTOK], F32R) for n in ("hi", "lo"))
        b1e = m.sb("e_b1e", [P, MC])
        rows_g = m.sb("e_rows_g", [P, 2 * SH], U32)
        rows_s = m.sb("e_rows_s", [P, SH], U32)
        xg, pg = g.xg, g.pg
        wt = [m.sb(f"e_wt{h}", [P, GT]) for h in range(2)]
        st = m.sb("e_st", [P, GT, 6])
        mv = m.sb("e_mv", [P, GT, 2])
        veps = m.sb("e_veps", [P, GT])
        rstd = m.sb("e_rstd", [P, GT])
        tmp = m.sb("e_tmp", [P, D])
        b_u = [m.ps(f"e_bu{j}", GTOK) for j in range(4)]
        b_x = [m.ps(f"e_bx{j}", GTOK) for j in range(DC)]
        b_y = [m.ps(f"e_by{j}", GTOK) for j in range(2)]
        names = ("w1 w2 rows_g rows_s held gather0 gather1 gather_p0 gather_p1 b1e wt dve_held stats aggr eps rstd xhat xT hT hhi h_hi h_lo "
                 "w1hi w1_hi w1_lo w2hi w2_hi w2_lo u gelu uhi u_hi u_lo "
                 "y y1 ys added").split()
        s = {n: m.sem("e_" + n) for n in names}
        ident = g.cst[:, C_ID:C_ID + P]
        HALF = 2

        with nc.Block() as block:
            @block.sync
            def _(sp):
                with sp.Fori(1, E) as e:
                    sp.wait_ge(s["w1hi"], e)
                    sp.wait_ge(s["w1_lo"], e)
                    sp.dma_start(w1[:, :, :], a["fc1s"][e]).then_inc(s["w1"], 16)
                    sp.wait_ge(s["w2_lo"], 2 * e)
                    sp.dma_start(w2[:, :, :], a["fc2s"][e]).then_inc(s["w2"], 16)

            @block.scalar
            def _(act):
                def high(i, n):
                    act.wait_ge(s["uhi"], MC * i + n + 1)
                    nc.scalar.copy(u_hi[:, n, :], uhi[:, n % UB, :]).then_inc(s["u_hi"], 1)

                def step(e, has):
                    for h in range(HALF):
                        i = HALF * e + h
                        if has(0):
                            for n in range(MC):
                                act.wait_ge(s["u"], MC * i + n + 1)
                                if h == 0 and n == 0:
                                    act.wait_ge(s["b1e"], e + 1)
                                if n >= UB:
                                    act.wait_ge(s["u_lo"], MC * i + n - UB + 1)
                                elif h or later(e):
                                    act.wait_ge(s["u_lo"], MC * i)
                                nc.scalar.activation(uf[:, n % UB, :], b_u[n % 4][:, :], ACT.Gelu_apprx_tanh,
                                                     bias=b1e[:, n:n + 1]).then_inc(s["gelu"], 1)
                                if n == 1 and (h or later(e)):
                                    act.wait_ge(s["y"], GT * i)
                                if n:
                                    high(i, n - 1)
                                if h == 0 and n in (4, 6):
                                    half = slice((n // 2 - 2) * MC // 2, (n // 2 - 1) * MC // 2)
                                    act.wait_ge(s["w2hi"], e + 1)
                                    nc.scalar.copy(w2_hi[:, half, :], w2hi[:, half, :]).then_inc(s["w2_hi"], 1)
                            high(i, MC - 1)
                        if has(0) if h == 0 else has(1):
                            act.wait_ge(s["hhi"], i + 2)
                            nc.scalar.copy(h_hi[:, :, :], hhi).then_inc(s["h_hi"], 1)
                        if h == 1 and has(1):
                            act.wait_ge(s["w1hi"], e + 2)
                            if has(0):
                                act.wait_ge(s["u"], HALF * MC * (e + 1))
                            nc.scalar.copy(w1_hi[:, :, :], w1hi).then_inc(s["w1_hi"], 1)
                pipeline(act, step, E, 1, 1)

            @block.gpsimd
            def _(pool):
                def step(e, has):
                    for h in range(HALF):
                        i = HALF * e + h
                        if has(1) and later(e + 1):
                            if h == 0:
                                pool.wait_ge(s["rows_g"], e + 1)
                            pool.wait_ge(s["xhat"], GT * (i + 1))
                            pool.sem_inc(s["held"], 1)
                            for k in range(GT):
                                c = h * GT + k
                                nc.gpsimd.indirect_dma_start(
                                    xg[h][:, k, :], None, g.tok_dram.rearrange("t p d -> (t p) d"),
                                    bass.IndirectOffsetOnAxis(rows_g[:, c:c + 1], 0)).then_inc(s[f"gather{h}"], 16)
                            for k in range(GT):
                                c = h * GT + k
                                nc.gpsimd.indirect_dma_start(
                                    pg[h][:, k, :], None, g.prob_dram.rearrange("p t e -> (p t) e"),
                                    bass.IndirectOffsetOnAxis(rows_g[:, SH + c:SH + c + 1], 0))\
                                    .then_inc(s[f"gather_p{h}"], 16)
                        if has(1):
                            pool.wait_ge(s["eps"], i + 3)
                            nc.gpsimd.tensor_tensor(rstd[:, :], veps[:, :], g.mhalf[:, 0:GT], ALU.pow)\
                                .then_inc(s["rstd"], 1)
                        if has(0):
                            for k in range(GT):
                                c = h * GT + k
                                pool.wait_ge(s["ys"], GT * i + k + 1)
                                if h or k or later(e):
                                    pool.wait_ge(s["added"], 16 * (GT * i + k))
                                pool.sem_inc(s["held"], 1)
                                nc.gpsimd.indirect_dma_start(
                                    out.rearrange("t p d -> (t p) d"),
                                    bass.IndirectOffsetOnAxis(rows_s[:, c:c + 1], 0), ys[h][:, k, :], None,
                                    compute_op=ALU.add).then_inc(s["added"], 16)
                pipeline(pool, step, E, 1, 1)
                pool.wait_ge(s["added"], 16 * E * SH)

            @block.vector
            def _(dve):
                def high_w1(e):
                    if later(e):
                        dve.wait_ge(s["w1"], 16 * e)
                        dve.wait_ge(s["w1_lo"], e)
                        dve.wait_ge(s["w1_hi"], e)
                    nc.vector.tensor_single_scalar(w1hi.bitcast(I32), w1.bitcast(I32), HIGH, ALU.bitwise_and)\
                        .then_inc(s["w1hi"], 1)

                def low_w1(e):
                    if later(e):
                        dve.wait_ge(s["u"], HALF * MC * e)
                    dve.wait_ge(s["w1hi"], e + 1)
                    nc.vector.tensor_tensor(w1_lo[:, :, :], w1, w1hi, ALU.subtract)\
                        .then_inc(s["w1_lo"], 1)

                def high_w2(e):
                    if later(e):
                        dve.wait_ge(s["w2"], 16 * e)
                        dve.wait_ge(s["w2_lo"], 2 * e)
                        dve.wait_ge(s["w2_hi"], 2 * e)
                    nc.vector.tensor_single_scalar(w2hi.bitcast(I32), w2.bitcast(I32), HIGH, ALU.bitwise_and)\
                        .then_inc(s["w2hi"], 1)

                def low_w2(e, n):
                    if n == 0 and later(e):
                        dve.wait_ge(s["y"], HALF * GT * e)
                    half = slice(n * MC // 2, (n + 1) * MC // 2)
                    dve.wait_ge(s["w2hi"], e + 1)
                    nc.vector.tensor_tensor(w2_lo[:, half, :], w2[:, half, :], w2hi[:, half, :], ALU.subtract)\
                        .then_inc(s["w2_lo"], 1)

                def split_u(i, n, used):
                    dve.wait_ge(s["gelu"], MC * i + n + 1)
                    if used:
                        dve.wait_ge(s["u_hi"], MC * i + n - UB + 1 if n >= UB else MC * i)
                    nc.vector.tensor_single_scalar(uhi[:, n % UB, :].bitcast(I32), uf[:, n % UB, :].bitcast(I32), HIGH,
                                                   ALU.bitwise_and).then_inc(s["uhi"], 1)
                    dve.wait_ge(s["uhi"], MC * i + n + 1)
                    nc.vector.tensor_tensor(u_lo[:, n, :], uf[:, n % UB, :], uhi[:, n % UB, :], ALU.subtract)\
                        .then_inc(s["u_lo"], 1)

                def split_h(i):
                    dve.wait_ge(s["xT"], i + 1)
                    for c in range(DC):
                        nc.vector.tensor_scalar(hT[:, c, :], b_x[c][:, :], lnw[:, c, 0:1], lnw[:, c, 1:2],
                                                ALU.mult, ALU.add).then_inc(s["hT"], 1)
                    dve.wait_ge(s["hT"], DC * (i + 1))
                    nc.vector.tensor_single_scalar(hhi.bitcast(I32), hT.bitcast(I32), HIGH, ALU.bitwise_and)\
                        .then_inc(s["hhi"], 1)
                    dve.wait_ge(s["hhi"], i + 1)
                    nc.vector.tensor_tensor(h_lo[:, :, :], hT, hhi, ALU.subtract).then_inc(s["h_lo"], 1)

                def weigh(e, h, k):
                    i = HALF * e + h
                    n = GT * i + k
                    dve.wait_ge(s["y"], n + 1)
                    if k or h or later(e):
                        dve.wait_ge(s["ys"], n)
                    if k == 0 and later(e):
                        dve.wait_ge(s["added"], 16 * (GT * (i - 1)))
                    nc.vector.tensor_tensor(tmp[:, :], b_y[k % 2][:, 0:D],
                                            b2[:, bass.ds(e, 1), :].rearrange("p e r -> p (e r)"),
                                            ALU.add).then_inc(s["y1"], 1)
                    dve.wait_ge(s["y1"], n + 1)
                    if k == 0:
                        dve.wait_ge(s["wt"], i + 1)
                    nc.vector.tensor_scalar(ys[h][:, k, :], tmp[:, :], wt[h][:, k:k + 1], None, ALU.mult)\
                        .then_inc(s["ys"], 1)

                def moments(e, h, used):
                    i = HALF * e + h
                    if later(e):
                        dve.wait_ge(s[f"gather{h}"], 16 * GT * e)
                    else:
                        dve.wait_ge(g.gathered[h], 32 * GT)
                    for k in range(GT):
                        nc.vector.bn_stats(st[:, k, :], xg[h][:, k, :]).then_inc(s["stats"], 1)
                    if later(e):
                        dve.wait_ge(s[f"gather_p{h}"], 16 * GT * e)
                    if used:
                        dve.wait_ge(s["ys"], GT * (i - 1))
                    nc.vector.tensor_copy(wt[h][:, :].unsqueeze(2), pg[h][:, :, bass.ds(e, 1)]).then_inc(s["wt"], 1)
                    dve.wait_ge(s["stats"], GT * (i + 1))
                    if h or later(e):
                        dve.wait_ge(s["xhat"], GT * i)
                    dve.sem_inc(s["dve_held"], 1)
                    for k in range(GT):
                        nc.vector.bn_aggr(mv[:, k, :], st[:, k, :]).then_inc(s["aggr"], 1)
                    dve.wait_ge(s["aggr"], GT * (i + 1))
                    nc.vector.tensor_scalar(veps[:, :], mv[:, :, 1], EPS1, None, ALU.add).then_inc(s["eps"], 1)

                def normal(i, h, used):
                    dve.wait_ge(s["rstd"], i + 1)
                    if used:
                        dve.wait_ge(s["xT"], i)
                    for k in range(GT):
                        nc.vector.tensor_scalar(xhat[:, k, :], xg[h][:, k, :], mv[:, k, 0:1], rstd[:, k:k + 1],
                                                ALU.subtract, ALU.mult).then_inc(s["xhat"], 1)

                def step(e, has):
                    if has(1) and later(e + 1):
                        if later(e):
                            for h in range(HALF):
                                dve.wait_ge(s[f"gather{h}"], 16 * GT * e)
                                dve.wait_ge(s[f"gather_p{h}"], 16 * GT * e)
                        nc.vector.tensor_scalar(rows_g[:, :], g.rows[:, bass.ds(e + 1, 1), :]
                                                .rearrange("p e r -> p (e r)"), 0.0, None, ALU.add)\
                            .then_inc(s["rows_g"], 1)
                    for h in range(HALF):
                        i = HALF * e + h
                        follows = has(0) if h == 0 else has(1)
                        if has(0):
                            for n in range(MC):
                                split_u(i, n, n >= UB or h or later(e))
                                if h == 0 and n in (3, 5):
                                    low_w2(e, n // 2 - 1)
                                if n == 2 and follows:
                                    normal(i + 1, 1 - h, later(e) or h == 0 or has(0))
                        elif follows:
                            normal(i + 1, 1 - h, False)
                        if follows:
                            split_h(i + 1)
                        if h == 1 and has(1):
                            if has(0):
                                dve.wait_ge(s["gelu"], HALF * MC * (e + 1))
                            nc.vector.tensor_scalar(b1e[:, :], g.e_b1[:, bass.ds(e + 1, 1), :]
                                                    .rearrange("p e r -> p (e r)"), 0.0, None, ALU.add)\
                                .then_inc(s["b1e"], 1)
                        if h == 0 and has(0):
                            if later(e):
                                dve.wait_ge(s["added"], 16 * SH * e)
                            nc.vector.tensor_scalar(rows_s[:, :], g.rows[:, bass.ds(e, 1), 0:SH]
                                                    .rearrange("p e r -> p (e r)"), 0.0, None, ALU.add)\
                                .then_inc(s["rows_s"], 1)
                        for k in range(GT):
                            if k == 2 and h == 1 and has(1):
                                low_w1(e + 1)
                            if has(0):
                                weigh(e, h, k)
                        if has(1):
                            moments(e + 1, h, has(0))
                            if h == 0:
                                high_w1(e + 1)
                                high_w2(e + 1)
                dve.wait_ge(g.loaded_e, 80)
                pipeline(dve, step, E, 1, 1)

            @block.tensor
            def _(pe):
                def step(e, has):
                    for h in range(HALF):
                        i = HALF * e + h
                        if has(0):
                            pe.wait_ge(s["h_hi"], i + 1)
                            pe.wait_ge(s["h_lo"], i + 1)
                            if h == 0:
                                pe.wait_ge(s["w1_hi"], e + 1)
                                pe.wait_ge(s["w1_lo"], e + 1)
                            for n in range(MC):
                                if n >= 4 or h or later(e):
                                    pe.wait_ge(s["gelu"], MC * i + n - 3)
                                for kc in range(DC):
                                    cols = slice(n * P, (n + 1) * P)
                                    last = split_product(nc.tensor, b_u[n % 4][:, :], w1_hi[:, kc, cols],
                                                         w1_lo[:, kc, cols], h_hi[:, kc, :], h_lo[:, kc, :],
                                                         kc == 0, kc == DC - 1)
                                last.then_inc(s["u"], 1)
                        if h == 0 and has(0) or h == 1 and has(1):
                            pe.wait_ge(s["xhat"], GT * (i + 2))
                            if h == 0 or later(e + 1):
                                pe.wait_ge(s["hT"], DC * (i + 1))
                            for c in range(DC):
                                for k in range(GT):
                                    last = nc.tensor.transpose(b_x[c][:, k * P:(k + 1) * P],
                                                               xhat[:, k, c * P:(c + 1) * P], ident)
                            last.then_inc(s["xT"], 1)
                        if has(0):
                            for k in range(GT):
                                n = GT * i + k
                                if k >= 2 or h or later(e):
                                    pe.wait_ge(s["y1"], n - 1)
                                for kc in range(MC):
                                    if k == 0:
                                        if h == 0 and kc % (MC // 2) == 0:
                                            pe.wait_ge(s["w2_hi"], 2 * e + kc // (MC // 2) + 1)
                                            pe.wait_ge(s["w2_lo"], 2 * e + kc // (MC // 2) + 1)
                                        pe.wait_ge(s["u_hi"], MC * i + kc + 1)
                                        pe.wait_ge(s["u_lo"], MC * i + kc + 1)
                                    toks = slice(k * P, (k + 1) * P)
                                    last = split_product(nc.tensor, b_y[k % 2][:, 0:D], u_hi[:, kc, toks],
                                                         u_lo[:, kc, toks], w2_hi[:, kc, :], w2_lo[:, kc, :],
                                                         kc == 0, kc == MC - 1)
                                last.then_inc(s["y"], 1)
                pe.wait_ge(g.loaded_e, 80)
                pipeline(pe, step, E, 1, 1)
        m.clear()


class Kept:
    pass


def program(nc, a, out, phases=9):
    with ExitStack() as ctx:
        m = Mem(nc, ctx)
        g = Kept()
        g.cst = m.sb("consts_sb", [P, C_ALL])[:, :]
        g.mhalf = m.sb("minus_half", [P, 32])
        g.X = m.sb("X", [P, NT, D])
        g.sh_1 = m.sb("shift_1", [P, DC, B])
        g.ln1g = m.sb("ln1g", [P, DC])[:, :]
        g.lg = m.sb("expert_scores", [P, E, NT])
        g.loaded, g.loaded1 = m.sem("loaded"), m.sem("loaded1")
        g.loaded_e, g.gathered = m.sem("loaded_experts"), [m.sem(f"gathered{h}") for h in range(2)]
        g.rows = m.sb("rows", [P, E, 2 * SH], U32)
        g.prob_dram = nc.dram_tensor("probs", [P, NT, E], F32, kind="Internal").ap()
        g.thr_dram = nc.dram_tensor("thresholds", [1, P], F32, kind="Internal").ap()
        g.tok_dram = nc.dram_tensor("tokens", [NT, P, D], F32, kind="Internal").ap()
        g.gate_dram = nc.dram_tensor("gates_of_rows", [B, 2 * D], F32, kind="Internal").ap()
        with ExitStack() as ctx0:
            m0 = Mem(nc, ctx0)
            wparts = m0.sb("w_parts", [P, 4, DC * MLP], F32R)
            g.w1_hi, g.w1_lo = (wparts[:, n, :].rearrange("p (c m) -> p c m", c=DC) for n in (0, 1))
            g.w2_hi, g.w2_lo = (wparts[:, n, :].rearrange("p (c m) -> p c m", c=MC) for n in (2, 3))
            g.wv_hi, g.wv_lo = g.w1_hi, g.w1_lo
            g.sh_m, g.sc_m = (m0.sb(n, [P, DC, B]) for n in ("shift_mlp", "scale_mlp"))
            with ExitStack() as ctx1:
                m1 = Mem(nc, ctx1)
                g.sh_a, g.sc_a = (m1.sb(n, [P, DC, B]) for n in ("shift_msa", "scale_msa"))
                g.wqkv0 = m1.sb("wqkv0", [P, DC, 3 * D])[:, :, :]
                g.wproj0 = m1.sb("wproj0", [P, DC, D])[:, :, :]
                g.qkb0 = m1.sb("qkb0", [P, 2 * DC])[:, :]
                g.vb0 = m1.sb("vb0", [P, DC])[:, :]
                g.pb0 = m1.sb("pb0", [P, D])[:, :]
                g.mrow = m1.sb("mrow", [P, NT])[:, :]
                g.hidden = m1.sb("hidden", [P, NT, S])[:, :, :]
                g.PT = m1.sb("PT0", [P, H, P])
                g.vm = m1.sb("vm", [P, 4, 2, H // 2, 2 * HD0])
                setup_phase(nc, a, g)
                if phases >= 1:
                    attention0_phase(nc, a, g)
            g.wq_hi, g.wq_lo = (m0.sb(n, [P, DC, QK1], F32R)[:, :, :] for n in ("wqk1_hi", "wqk1_lo"))
            g.wgate = m0.sb("wgate", [P, DC, E])[:, :, :]
            g.qn, g.kn = (m0.sb(n, [P, 2])[:, :] for n in ("qn", "kn"))
            if phases >= 2:
                mlp0_phase(nc, a, g)
            if phases >= 3:
                attention1_phase(nc, a, out, g)
        g.e_w1 = m.sb("e_w1", [P, DC, MLP])[:, :, :]
        g.e_w2 = m.sb("e_w2", [P, MC, D])[:, :, :]
        g.e_b1 = m.sb("e_b1", [P, E, MC])[:, :, :]
        g.e_b2 = m.sb("e_b2", [P, E, D])[:, :, :]
        g.e_lnw = m.sb("e_lnw", [P, DC, 2])[:, :, :]
        g.xg = [m.sb(f"e_xg{h}", [P, GT, D]) for h in range(2)]
        g.pg = [m.sb(f"e_pg{h}", [P, GT, E]) for h in range(2)]
        if phases >= 4:
            route_phase(nc, a, g)
        if phases >= 5:
            experts_phase(nc, a, out, g)


def feature_major(v):
    return np.ascontiguousarray(v.reshape(-1, P).T)


def weight(w):
    return np.ascontiguousarray(w.T.reshape(-1, P, w.shape[0]).transpose(1, 0, 2))


def layouts(x, cond_1024, mask_BxS_bk1, **w):
    n = {k: np.asarray(v) for k, v in w.items()}
    L0, L1 = "L0_cond_", "L1_cond_"
    mask = np.asarray(mask_BxS_bk1)
    ada_b = n[L0 + "ada_b"].reshape(6, DC, P)
    return {
        "x": np.asarray(x).reshape(NT, P, D),
        "condT": weight(np.asarray(cond_1024)),
        "mask": mask,
        "maskT": np.ascontiguousarray(mask.reshape(NT, P).T),
        "consts": constants(),
        "ada_w": weight(n[L0 + "ada_w"]),
        "ada_b": np.ascontiguousarray(ada_b[[0, 1, 3, 4]].reshape(4 * DC, P).T),
        "ada_row": n[L0 + "ada_b"].reshape(1, -1),
        "ada1_w": weight(n[L1 + "W_ada"]),
        "ada1_b": feature_major(n[L1 + "b_ada"]),
        "ln1_b": feature_major(n[L1 + "ln1_b"]),
        "ln1_g": feature_major(n[L1 + "ln1_g"]),
        "qkv0_w": weight(n[L0 + "qkv_w"]),
        "v0_b": feature_major(n[L0 + "qkv_b"][2 * D:]),
        "qk0_b": feature_major(n[L0 + "qkv_b"][:2 * D]),
        "proj0_w": weight(n[L0 + "proj_w"]),
        "fc1_0_w": weight(n[L0 + "fc1_w"]),
        "fc1_0_b": feature_major(n[L0 + "fc1_b"]),
        "fc2_0_w": weight(n[L0 + "fc2_w"]),
        "fc2_0_row": n[L0 + "fc2_b"].reshape(1, -1),
        "qkv1_w": weight(n[L1 + "Wqkv"]),
        "out1_w": weight(n[L1 + "Wout"]),
        "gate_w": weight(n[L1 + "Wgate"]),
        "qn": np.stack([np.tile(n[L1 + "qn_g"], 2), np.tile(n[L1 + "qn_b"], 2)], 1),
        "kn": np.stack([np.tile(n[L1 + "kn_g"], 2), np.tile(n[L1 + "kn_b"], 2)], 1),
        "fc1s": np.stack([weight(w1) for w1 in n[L1 + "fc1s"]]),
        "fc2s": np.stack([weight(w2) for w2 in n[L1 + "fc2s"]]),
        "b1s": np.ascontiguousarray(n[L1 + "b1s"].reshape(E, MC, P).transpose(2, 0, 1)),
        "b2s": n[L1 + "b2s"].reshape(1, E, D),
        "mlp_ln": np.stack([feature_major(n[L1 + "mlp_g"]), feature_major(n[L1 + "mlp_b"])], 2),
        "proj0_row": n[L0 + "proj_b"].reshape(1, -1),
    }


def kernel(**inputs):
    import concourse.bacc as bacc
    from concourse.bass_utils import run_bass_kernel_spmd

    nc = bacc.Bacc("TRN2", target_bir_lowering=False, num_devices=1)
    arrays = {"in_" + n: v for n, v in layouts(**inputs).items()}
    a = {n[3:]: nc.dram_tensor(n, v.shape, mybir.dt.from_np(v.dtype), kind="ExternalInput").ap()
         for n, v in arrays.items()}
    out = nc.dram_tensor("out", [NT, P, D], F32, kind="ExternalOutput").ap()
    program(nc, a, out)
    r = run_bass_kernel_spmd(nc, [arrays], core_ids=[0])
    return r.results[0]["out"].reshape(B, S, D)
```
